# Optimizing a Trainium2 kernel written in Bass

```python
import numpy as np
import jax
import jax.numpy as jnp

def _softmax(x, axis=-1):
    return jax.nn.softmax(x, axis=axis)

def _gelu(x):
    return jax.nn.gelu(x, approximate=True)

def _silu(x):
    return jax.nn.silu(x)

def _sigmoid(x):
    return jax.nn.sigmoid(x)

def _layernorm(x, axis=-1, eps=1e-05):
    m = jnp.mean(x, axis=axis, keepdims=True)
    v = jnp.var(x, axis=axis, keepdims=True)
    return (x - m) / jnp.sqrt(v + eps)

def _scatter_add(tgt, idx, src, axis=0):
    return tgt.at[idx].add(src)

def _segment_sum(src, seg, n):
    return jax.ops.segment_sum(src, seg, n)
kernel_name = 'mk_gnn_preln_d2_gnn_r16_1deaf7'

def setup_inputs(seed: int=0):
    np.random.seed(seed)
    _w = jnp.asarray

    def _rec_inputs():
        import jax
        import jax.numpy as jnp
        _gk = jax.random.key(seed)
        x = -0.0002117 + 1 * jax.random.normal(jax.random.fold_in(_gk, 1), (6250, 256), jnp.float32)
        src = jax.random.randint(jax.random.fold_in(_gk, 2), (100000,), 0, 6250, jnp.int32)
        dst = jax.random.randint(jax.random.fold_in(_gk, 3), (100000,), 0, 6250, jnp.int32)
        _o = jnp.argsort(dst, stable=True)
        src = src[_o]
        dst = dst[_o]
        return (x, src, dst)
    x, src, dst = _rec_inputs()

    def _L0_gnn_setup():
        import jax, jax.numpy as jnp
        import numpy as np
        N = 6250
        E = 50000
        EMB = 256
        HID = 256
        EPS = 1e-05

        def _pool_max(h, edge_src, edge_dst):
            pooled = jax.ops.segment_max(h[edge_src], edge_dst, num_segments=N)
            cnt = jax.ops.segment_sum(jnp.ones((edge_dst.shape[0],), h.dtype), edge_dst, num_segments=N)
            return jnp.where((cnt > 0)[:, None], pooled, jnp.zeros((), h.dtype))

        def _layernorm(x, g, b):
            mu = jnp.mean(x, axis=-1, keepdims=True)
            var = jnp.mean(jnp.square(x - mu), axis=-1, keepdims=True)
            return (x - mu) * jax.lax.rsqrt(var + EPS) * g + b
        key = jax.random.key(seed)
        ks = jax.random.split(key, 12)
        s = 0.05
        return {'embeddings': jax.random.normal(ks[0], (N, EMB), jnp.float32), 'edge_src': jax.random.randint(ks[1], (E,), 0, N, jnp.int32), 'edge_dst': jax.random.randint(ks[2], (E,), 0, N, jnp.int32), 'Wp1': jax.random.normal(ks[3], (HID, EMB), jnp.float32) * s, 'bp1': jnp.zeros((HID,), jnp.float32), 'Wm1': jax.random.normal(ks[4], (HID, EMB + HID), jnp.float32) * s, 'bm1': jnp.zeros((HID,), jnp.float32), 'Wm2': jax.random.normal(ks[5], (HID, 2 * HID), jnp.float32) * s, 'bm2': jnp.zeros((HID,), jnp.float32), 'Wm3': jax.random.normal(ks[6], (HID, 2 * HID), jnp.float32) * s, 'bm3': jnp.zeros((HID,), jnp.float32), 'ln2_g': jnp.ones((HID,), jnp.float32), 'ln2_b': jnp.zeros((HID,), jnp.float32), 'ln3_g': jnp.ones((HID,), jnp.float32), 'ln3_b': jnp.zeros((HID,), jnp.float32)}
    _L0_gnn_all = _L0_gnn_setup()
    _L0_gnn_in = {k: v for k, v in _L0_gnn_all.items() if k in ('Wp1', 'bp1', 'Wm1', 'bm1', 'Wm2', 'bm2', 'Wm3', 'bm3', 'ln2_g', 'ln2_b', 'ln3_g', 'ln3_b')}
    del _L0_gnn_all

    def _L1_gnn_setup():
        import jax, jax.numpy as jnp
        import numpy as np
        N = 1250
        E = 20000
        HID = 256
        HEADS = 8
        HD = HID // HEADS
        key = jax.random.key(seed)
        ks = jax.random.split(key, 12)
        scale = 1.0 / np.sqrt(HID).astype(np.float32)

        def lin_w(k):
            return jax.random.normal(k, (HID, HID), jnp.float32) * scale

        def lin_b(k):
            return jax.random.normal(k, (HID,), jnp.float32) * 0.01
        return {'h': jax.random.normal(ks[0], (N, HID), jnp.float32), 'Wq': lin_w(ks[1]), 'bq': lin_b(ks[2]), 'Wk': lin_w(ks[3]), 'bk': lin_b(ks[4]), 'Wv': lin_w(ks[5]), 'bv': lin_b(ks[6]), 'Wo': lin_w(ks[7]), 'bo': lin_b(ks[8]), 'rows': jax.random.randint(ks[9], (E,), 0, N), 'cols': jax.random.randint(ks[10], (E,), 0, N)}
    _L1_gnn_all = _L1_gnn_setup()
    _L1_gnn_in = {k: v for k, v in _L1_gnn_all.items() if k in ('Wq', 'bq', 'Wk', 'bk', 'Wv', 'bv', 'Wo', 'bo')}
    del _L1_gnn_all
    return {'x': x, 'src': src, 'dst': dst, 'L0_gnn_Wp1': _L0_gnn_in['Wp1'], 'L0_gnn_bp1': _L0_gnn_in['bp1'], 'L0_gnn_Wm1': _L0_gnn_in['Wm1'], 'L0_gnn_bm1': _L0_gnn_in['bm1'], 'L0_gnn_Wm2': _L0_gnn_in['Wm2'], 'L0_gnn_bm2': _L0_gnn_in['bm2'], 'L0_gnn_Wm3': _L0_gnn_in['Wm3'], 'L0_gnn_bm3': _L0_gnn_in['bm3'], 'L0_gnn_ln2_g': _L0_gnn_in['ln2_g'], 'L0_gnn_ln2_b': _L0_gnn_in['ln2_b'], 'L0_gnn_ln3_g': _L0_gnn_in['ln3_g'], 'L0_gnn_ln3_b': _L0_gnn_in['ln3_b'], 'L1_gnn_Wq': _L1_gnn_in['Wq'], 'L1_gnn_bq': _L1_gnn_in['bq'], 'L1_gnn_Wk': _L1_gnn_in['Wk'], 'L1_gnn_bk': _L1_gnn_in['bk'], 'L1_gnn_Wv': _L1_gnn_in['Wv'], 'L1_gnn_bv': _L1_gnn_in['bv'], 'L1_gnn_Wo': _L1_gnn_in['Wo'], 'L1_gnn_bo': _L1_gnn_in['bo']}

def reference(x, src, dst, L0_gnn_Wp1, L0_gnn_bp1, L0_gnn_Wm1, L0_gnn_bm1, L0_gnn_Wm2, L0_gnn_bm2, L0_gnn_Wm3, L0_gnn_bm3, L0_gnn_ln2_g, L0_gnn_ln2_b, L0_gnn_ln3_g, L0_gnn_ln3_b, L1_gnn_Wq, L1_gnn_bq, L1_gnn_Wk, L1_gnn_bk, L1_gnn_Wv, L1_gnn_bv, L1_gnn_Wo, L1_gnn_bo):
    import jax
    import jax.numpy as jnp

    def _L0_gnn_ref(embeddings, edge_src, edge_dst, Wp1, bp1, Wm1, bm1, Wm2, bm2, Wm3, bm3, ln2_g, ln2_b, ln3_g, ln3_b):
        import jax, jax.numpy as jnp
        import numpy as np
        N = 6250
        E = 50000
        EMB = 256
        HID = 256
        EPS = 1e-05

        def _pool_max(h, edge_src, edge_dst):
            pooled = jax.ops.segment_max(h[edge_src], edge_dst, num_segments=N)
            cnt = jax.ops.segment_sum(jnp.ones((edge_dst.shape[0],), h.dtype), edge_dst, num_segments=N)
            return jnp.where((cnt > 0)[:, None], pooled, jnp.zeros((), h.dtype))

        def _layernorm(x, g, b):
            mu = jnp.mean(x, axis=-1, keepdims=True)
            var = jnp.mean(jnp.square(x - mu), axis=-1, keepdims=True)
            return (x - mu) * jax.lax.rsqrt(var + EPS) * g + b
        h1 = jax.nn.relu(embeddings @ Wp1.T + bp1)
        p1 = _pool_max(h1, edge_src, edge_dst)
        x = jax.nn.relu(jnp.concatenate([embeddings, p1], axis=1) @ Wm1.T + bm1)
        p2 = _pool_max(x, edge_src, edge_dst)
        y2 = jax.nn.relu(jnp.concatenate([x, p2], axis=1) @ Wm2.T + bm2)
        x = _layernorm(y2 + x, ln2_g, ln2_b)
        p3 = _pool_max(x, edge_src, edge_dst)
        y3 = jax.nn.relu(jnp.concatenate([x, p3], axis=1) @ Wm3.T + bm3)
        x = _layernorm(y3 + x, ln3_g, ln3_b)
        return x

    def _L1_gnn_ref(h, Wq, bq, Wk, bk, Wv, bv, Wo, bo, rows, cols):
        import jax, jax.numpy as jnp
        import numpy as np
        N = 1250
        E = 20000
        HID = 256
        HEADS = 8
        HD = HID // HEADS
        n = h.shape[0]
        scaling = HD ** (-0.5)
        q = (h @ Wq + bq).reshape(n, HD, HEADS) * scaling
        k = (h @ Wk + bk).reshape(n, HD, HEADS)
        v = (h @ Wv + bv).reshape(n, HD, HEADS)
        s = jnp.einsum('edh,edh->eh', q[rows], k[cols])
        m = jax.ops.segment_max(s, rows, num_segments=n)
        e = jnp.exp(s - m[rows])
        z = jax.ops.segment_sum(e, rows, num_segments=n)
        attn = e / z[rows]
        out = jax.ops.segment_sum(attn[:, None, :] * v[cols], rows, num_segments=n)
        return out.reshape(n, -1) @ Wo + bo
    h = jnp.maximum(_layernorm(x, axis=-1), 0.0)
    x = x + _L0_gnn_ref(h, src, dst, L0_gnn_Wp1, L0_gnn_bp1, L0_gnn_Wm1, L0_gnn_bm1, L0_gnn_Wm2, L0_gnn_bm2, L0_gnn_Wm3, L0_gnn_bm3, L0_gnn_ln2_g, L0_gnn_ln2_b, L0_gnn_ln3_g, L0_gnn_ln3_b)
    h = jnp.maximum(_layernorm(x, axis=-1), 0.0)
    x = x + _L1_gnn_ref(h, L1_gnn_Wq, L1_gnn_bq, L1_gnn_Wk, L1_gnn_bk, L1_gnn_Wv, L1_gnn_bv, L1_gnn_Wo, L1_gnn_bo, src, dst)
    return x

_drawn_inputs = setup_inputs


def setup_inputs(seed=0):
    import zlib

    import numpy as np

    out = dict(_drawn_inputs(seed))
    spreads = {'L0_gnn_bp1': (0.0, 0.1),
     'L0_gnn_bm1': (0.0, 0.1),
     'L0_gnn_bm2': (0.0, 0.1),
     'L0_gnn_bm3': (0.0, 0.1),
     'L0_gnn_ln2_g': (1.0, 0.2),
     'L0_gnn_ln2_b': (0.0, 0.1),
     'L0_gnn_ln3_g': (1.0, 0.2),
     'L0_gnn_ln3_b': (0.0, 0.1)}
    factors = {'L1_gnn_bq': 64.0, 'L1_gnn_bk': 64.0, 'L1_gnn_bv': 8.0, 'L1_gnn_bo': 8.0}
    for name, (base, spread) in spreads.items():
        noise = np.random.default_rng([zlib.crc32(name.encode()), seed]).standard_normal(out[name].shape)
        drawn = base * np.exp(spread * noise) if base else spread * noise
        out[name] = jnp.asarray(drawn.astype(out[name].dtype))
    for name, factor in factors.items():
        out[name] = (out[name] * factor).astype(out[name].dtype)
    return out
```

```python
from contextlib import ExitStack, contextmanager

import concourse.bass as bass
from concourse import mybir

F32, BF16, I32, I16 = mybir.dt.float32, mybir.dt.bfloat16, mybir.dt.int32, mybir.dt.int16
ALU, ACT, AX = mybir.AluOpType, mybir.ActivationFunctionType, mybir.AxisListType

P = 128
D = 256
KC = D // P
HEADS = 8
HD = D // HEADS
EPS = 1e-5
NEG = -1e30
FAR = 1_000_000.0
ACC = D + HEADS
KV = D + ACC
ROW = KV + HEADS
STATE = ACC + HEADS
UN = 7
J = 9
UB = 3


class Count:

    def __init__(self, sem, start=0):
        self.sem, self.base = sem, start

    def of(self, i, u, per=UN):
        return self.base + (i * per + (u + 1))

    def close(self, n):
        self.base += n


class Chain:

    def __init__(self, eng, sem):
        self.eng, self.sem, self.base, self.term = eng, sem, 0, 0

    def inc(self, ins):
        ins.then_inc(self.sem, 1)
        self.base += 1
        return self.base + self.term

    def link(self, ins):
        self.eng.wait_ge(self.sem, self.inc(ins))

    @contextmanager
    def body(self, i, per, times):
        start, self.term = self.base, i * per
        yield
        assert self.base - start == per, (self.base - start, per)
        self.base, self.term = start + per * times, 0


def staged(eng, steps, un, stages, chain=None, links=0):
    turns = steps // un
    assert turns * un == steps
    late = -(-max(delay for delay, _ in stages) // un)

    def turn(i, edge):
        for u in range(un):
            for delay, stage in stages:
                d, uu = divmod(u - delay, un)
                if edge and not 0 <= i * un + u - delay < steps:
                    continue
                stage(i + d, uu)

    first = 1 + late
    for i in range(first):
        turn(i, True)
    with eng.Fori(first, turns) as i:
        if chain is None:
            turn(i, False)
        else:
            with chain.body(i - first, links * un, turns - first):
                turn(i, False)
    for i in range(turns, turns + late):
        turn(i, True)


def gnn_kernel(nc, x, src, dst, wp1, bp1, wm1, bm1, wm2, bm2, wm3, bm3, g2, b2, g3, b3,
               wq, bq, wk, bk, wv, bv, wo, bo, out):
    N, E = x.shape[0], src.shape[0]
    NT = -(-N // P)
    NT = -(-NT // UN) * UN
    TAIL = N - (NT - 1) * P
    NB = -(-(-(-E // P)) // J)
    NB = -(-NB // UB) * UB
    CH = NB * J
    LASTE = E - (P - 1) * CH
    EMPTY = P * CH
    PAD = NT * P - 1
    assert 0 < TAIL < P and 0 < LASTE < CH and PAD >= N

    tab = nc.dram_tensor("tab", [NT * P, D], F32, kind="Internal").ap()
    hist = nc.dram_tensor("hist", [EMPTY + 1, D], F32, kind="Internal").ap()
    kvtab = nc.dram_tensor("kvtab", [NT * P, KV], F32, kind="Internal").ap()
    qtab = nc.dram_tensor("qtab", [NT * P, D], F32, kind="Internal").ap()
    ahist = nc.dram_tensor("ahist", [EMPTY + 1, STATE], F32, kind="Internal").ap()
    tab_t = tab.rearrange("(t p) f -> t p f", p=P)
    kvtab_t = kvtab.rearrange("(t p) f -> t p f", p=P)
    qtab_t = qtab.rearrange("(t p) f -> t p f", p=P)
    hist_p = hist[0:EMPTY, :].rearrange("(p j) f -> p j f", p=P)
    ahist_p = ahist[0:EMPTY, :].rearrange("(p j) f -> p j f", p=P)

    def rows(v, n=P):
        return bass.AP(tensor=v.tensor, offset=v.offset, ap=[[0, n], [1, v.shape[0]]])

    with ExitStack() as top:
        def scope():
            return ExitStack()

        names = {}

        def sb(stack, name, shape, dt=F32):
            names[name] = names.get(name, 0) + 1
            return stack.enter_context(nc.sbuf_tensor(f"{name}_{names[name]}", shape, dt))

        def sem(name):
            return top.enter_context(nc.semaphore(name))

        X = sb(top, "X", [P, NT, D])
        src_ix = sb(top, "src_ix", [P, CH + 2 * J], I32)
        dst_ix = sb(top, "dst_ix", [P, CH + 2 * J], I32)
        reset = sb(top, "reset", [P, CH])
        ident = sb(top, "ident", [P, P])
        node_ix = sb(top, "node_ix", [P, NT], I32)
        node_ix2 = sb(top, "node_ix2", [P, NT], I32)
        fix_ix = sb(top, "fix_ix", [P, 1], I32)
        Rrow = sb(top, "Rrow", [P, P])
        eps = sb(top, "eps", [P, 1])
        ix = sb(top, "ix", [P, UB, 2, J], I32)
        nix = sb(top, "nix", [P, UN], I32)
        stat = sb(top, "stat", [P, UN, 6])
        mv = sb(top, "mv", [P, UN, 2])
        sd = sb(top, "sd", [P, UN])
        rstd = sb(top, "rstd", [P, UN])
        nmr = sb(top, "nmr", [P, UN])
        srt_src = sb(top, "srt_src", [P, NT])
        deg_src = sb(top, "deg_src", [P, NT])
        bank = [top.enter_context(nc.psum_tensor(f"bank{n}", [P, 512], F32)) for n in range(8)]

        s_const = sem("s_const")
        const_base = [10]
        s_load = sem("s_load")
        s_misc = Count(sem("s_misc"))
        s_misc2 = Count(sem("s_misc2"))
        c_stat, c_sd, c_norm, c_h, c_T, c_hT, c_mm, c_y, c_z, c_out, c_ix = (
            Count(sem(n), UN) for n in ("c_stat", "c_sd", "c_norm", "c_h", "c_T", "c_hT", "c_mm", "c_y", "c_z",
                                    "c_out", "c_ix"))
        c_T2, c_hT2, c_mm2, c_keep = (Count(sem(n), UN) for n in ("c_T2", "c_hT2", "c_mm2", "c_keep"))
        counts = (c_stat, c_sd, c_norm, c_h, c_T, c_hT, c_mm, c_y, c_z, c_out, c_ix, c_T2, c_hT2, c_mm2, c_keep)
        s_gat = [Count(sem(f"s_gat{u}")) for u in range(UN)]
        s_cur = [Count(sem(f"s_cur{u}")) for u in range(UN)]
        s_st = [Count(sem(f"s_st{u}")) for u in range(UN)]
        s_eg = [Count(sem(f"s_eg{b}")) for b in range(UB)]
        s_hs = [Count(sem(f"s_hs{b}")) for b in range(UB)]
        c_eix, c_batch, c_w, c_e = (Count(sem(n)) for n in ("c_eix", "c_batch", "c_w", "c_e"))
        s_held = {"vector": sem("s_held_v"), "pool": sem("s_held_p")}
        s_pe = Count(sem("s_pe"))
        s_dve = Count(sem("s_dve"))
        chain = Chain(nc.vector, sem("chain"))

        def block():
            return nc.Block()

        def ring(stack, name, width=D):
            return sb(stack, name, [P, UN, width])

        def hold(eng, who, sem, value):
            eng.wait_ge(sem, value)
            eng.sem_inc(s_held[who], 1)

        TURNED = (0, 1, 0, 1, 0, 1, 0)
        PRODUCT = (0, 1, 2, 0, 1, 2, 1)

        def prior(u, ring):
            return next(v for v in range(u - 1, u - UN - 1, -1) if ring[v % UN] == ring[u])

        def ps_T(u):
            return bank[TURNED[u]][:, 0:D]

        def ps_small(u):
            return bank[2 + 2 * PRODUCT[u]][:, 0:D]

        def ps_wide(u):
            return bank[3 + 2 * PRODUCT[u]][:, :]

        ones = sb(top, "ones", [P, P])
        keys = nc.dram_tensor("keys", [EMPTY + 2], I32, kind="Internal").ap()

        with scope() as st0:
            zrow = sb(st0, "zrow", [1, D + STATE])
            pad2 = sb(st0, "pad2", [1, 2], I32)
            with block() as blk:
                @blk.gpsimd
                def _(g):
                    g.memset(ident[:, :], 0.0).then_inc(s_const, 1)
                    g.memset(ones[:, :], 1.0).then_inc(s_const, 1)
                    g.memset(src_ix[:, :], PAD).then_inc(s_const, 1)
                    g.memset(dst_ix[:, :], PAD).then_inc(s_const, 1)
                    g.memset(pad2[:, :], PAD).then_inc(s_const, 1)
                    g.memset(X[:, NT - 1, :], 0.0).then_inc(s_const, 1)
                    g.memset(eps[:, :], EPS).then_inc(s_const, 1)
                    g.memset(zrow[:, :], 0.0).then_inc(s_const, 1)
                    g.wait_ge(s_const, 8)
                    g.memset(zrow[:, D + D:D + ACC], 1.0).then_inc(s_const, 1)
                    g.affine_select(out=ident[:, :], in_=ident[:, :], compare_op=ALU.not_equal, fill=1.0,
                                    base=0, pattern=[[-1, P]], channel_multiplier=1).then_inc(s_const, 1)

                @blk.sync
                def _(sp):
                    for c in counts:
                        sp.sem_inc(c.sem, UN)
                    sp.wait_ge(s_const, 10)
                    full = (P - 1) * CH
                    for dest, v in ((src_ix, src), (dst_ix, dst)):
                        sp.dma_start(dest[0:P - 1, 0:CH], v[0:full].rearrange("(p j) -> p j", j=CH)).then_inc(s_load, 16)
                        sp.dma_start(dest[P - 1:P, 0:LASTE], v[full:E].rearrange("(p j) -> p j", p=1)).then_inc(s_load, 16)
                    sp.dma_start(X[:, 0:NT - 1, :], x[0:(NT - 1) * P, :].rearrange("(t p) f -> p t f", p=P)).then_inc(s_load, 16)
                    sp.dma_start(X[0:TAIL, NT - 1, :], x[(NT - 1) * P:N, :]).then_inc(s_load, 16)
                    sp.dma_start(hist[EMPTY:EMPTY + 1, :], zrow[:, 0:D]).then_inc(s_load, 16)
                    sp.dma_start(ahist[EMPTY:EMPTY + 1, :], zrow[:, D:D + STATE]).then_inc(s_load, 16)
                    sp.dma_start(keys[0:1].rearrange("(a b) -> a b", a=1), pad2[:, 0:1]).then_inc(s_load, 16)
                    sp.dma_start(keys[EMPTY + 1:EMPTY + 2].rearrange("(a b) -> a b", a=1), pad2[:, 1:2]).then_inc(s_load, 16)
                    sp.wait_ge(s_load, 16 * 10)
            loads = 10

        def edge_marks(order):
            with scope() as st, block() as blk:
                near = sb(st, "near", [P, CH + 2], I32)
                nearf = sb(st, "nearf", [P, CH + 2])
                jp = sb(st, "jp", [P, CH])
                jpi = sb(st, "jpi", [P, CH], I32)
                neq = sb(st, "neq", [P, CH + 1])
                first_i = sb(st, "first_i", [P, 1], I32)
                firstf = sb(st, "firstf", [P, 1])
                end = sb(st, "end", [P, 1])
                flag = sb(st, "flag", [P, 1])
                flagw = sb(st, "flagw", [P, P])
                const0, m0 = const_base[0], s_misc2.base
                const_base[0] += 2

                @blk.gpsimd
                def _(g):
                    g.iota(jpi[:, :], [[1, CH]], base=0, channel_multiplier=0).then_inc(s_const, 1)
                    g.iota(first_i[:, :], [[0, 1]], base=0, channel_multiplier=CH).then_inc(s_const, 1)

                @blk.sync
                def _(sp):
                    sp.dma_start(keys[1:EMPTY + 1].rearrange("(p j) -> p j", j=CH), order[:, 0:CH]).then_inc(s_misc2.sem, 16)
                    sp.wait_ge(s_misc2.sem, m0 + 16)
                    sp.dma_start(near[:, :], bass.AP(tensor=keys.tensor, offset=keys.offset, ap=[[CH, P], [1, CH + 2]])).then_inc(s_misc2.sem, 16)

                @blk.vector
                def _(v):
                    v.wait_ge(s_const, const0 + 2)
                    chain.link(v.tensor_copy(jp[:, :], jpi[:, :]))
                    chain.link(v.tensor_copy(firstf[:, :], first_i[:, :]))
                    v.wait_ge(s_misc2.sem, m0 + 32)
                    chain.link(v.tensor_copy(nearf[:, :], near[:, :]))
                    chain.link(v.tensor_tensor(neq[:, :], nearf[:, 0:CH + 1], nearf[:, 1:CH + 2], ALU.not_equal))
                    chain.link(v.tensor_scalar(reset[:, :], neq[:, 0:CH], NEG, None, ALU.mult))
                    chain.link(v.memset(reset[:, 0:1], NEG))
                    chain.link(v.tensor_scalar(jp[:, :], jp[:, :], FAR, None, ALU.add))
                    chain.link(v.scalar_tensor_tensor(out=jp[:, :], in0=neq[:, 1:CH + 1], scalar=-FAR, in1=jp[:, :],
                                                      op0=ALU.mult, op1=ALU.add))
                    chain.link(v.tensor_reduce(end[:, :], jp[:, :], AX.X, ALU.min))
                    chain.link(v.scalar_tensor_tensor(out=end[:, :], in0=neq[:, 0:1], scalar=FAR,
                                                      in1=end[:, :], op0=ALU.mult, op1=ALU.add))
                    chain.link(v.tensor_tensor(end[:, :], end[:, :], firstf[:, :], ALU.add))
                    chain.link(v.tensor_copy(fix_ix[:, :], end[:, :]))
                    chain.link(v.tensor_tensor(flag[:, :], nearf[:, 1:2], nearf[:, CH:CH + 1], ALU.not_equal))
                    chain.link(v.tensor_tensor(flag[:, :], flag[:, :], neq[:, 0:1], ALU.max))
                    chain.link(v.tensor_scalar(flagw[:, :], ones[:, :], flag[:, 0:1], None, ALU.mult))
                    v.sem_inc(s_dve.sem, 1)
                    v.wait_ge(s_pe.sem, s_pe.base + 1)
                    chain.link(v.tensor_scalar(Rrow[:, :], bank[0][:, 0:P], NEG, None, ALU.mult))

                @blk.tensor
                def _(pe):
                    pe.wait_ge(s_dve.sem, s_dve.base + 1)
                    pe.matmul(bank[0][:, 0:P], flagw[:, :], ident[:, :], start=True, stop=True).then_inc(s_pe.sem, 1)
            s_dve.close(1)
            s_pe.close(1)
            s_misc2.close(32)

        def norm_stages(v, a, of_y):
            def stats(i, u):
                hold(v, "vector", chain.sem, chain.inc(v.bn_stats(stat[:, u, :], of_y(i, u))))
                chain.inc(v.bn_aggr(mv[:, u, :], stat[:, u, :]))
                v.wait_ge(chain.sem, chain.base + chain.term)
                v.sem_inc(c_stat.sem, 1)

            def recip(i, u):
                v.wait_ge(c_sd.sem, c_sd.of(i, u))
                chain.link(v.reciprocal(rstd[:, u:u + 1], sd[:, u:u + 1]))
                chain.link(v.scalar_tensor_tensor(out=nmr[:, u:u + 1], in0=mv[:, u, 0:1], scalar=-1.0,
                                                  in1=rstd[:, u:u + 1], op0=ALU.mult, op1=ALU.mult))
                v.sem_inc(c_norm.sem, 1)

            def sqrt(i, u):
                a.wait_ge(c_stat.sem, c_stat.of(i, u))
                a.activation(sd[:, u:u + 1], mv[:, u, 1:2], ACT.Sqrt, bias=eps[:, 0:1]).then_inc(c_sd.sem, 1)
            return stats, recip, sqrt

        def project(weights, emit, stores, store_sp, per_out):
            with scope() as st, block() as blk:
                h, hT = ring(st, "h"), ring(st, "hT")
                @blk.vector
                def _(v):
                    stats, recip, _ = norm_stages(v, None, lambda i, u: X[:, i * UN + u, :])

                    def finish(i, u):
                        v.wait_ge(c_mm.sem, c_mm.of(i, u))
                        if stores:
                            v.wait_ge(s_st[u].sem, s_st[u].base + i * 16 * stores)
                        emit(v, i, u)
                        v.sem_inc(c_out.sem, 1)
                    staged(v, NT, UN, [(0, stats), (1, recip), (4, finish)], chain, 4 + per_out)

                @blk.scalar
                def _(a):
                    _, _, sqrt = norm_stages(None, a, None)

                    def relu(i, u):
                        a.wait_ge(c_norm.sem, c_norm.of(i, u))
                        a.wait_ge(c_T.sem, c_T.of(i - 1, u))
                        a.activation(h[:, u, :], X[:, i * UN + u, :], ACT.Relu, bias=nmr[:, u:u + 1],
                                     scale=rstd[:, u:u + 1]).then_inc(c_h.sem, 1)

                    def evac(i, u):
                        a.wait_ge(c_T.sem, c_T.of(i, u))
                        a.wait_ge(c_mm.sem, c_mm.of(i - 1, u))
                        a.activation(hT[:, u, :], ps_T(u), ACT.Copy).then_inc(c_hT.sem, 1)
                    staged(a, NT, UN, [(0, sqrt), (2, relu), (3, evac)])

                @blk.tensor
                def _(pe):
                    def turn(i, u):
                        pe.wait_ge(c_h.sem, c_h.of(i, u))
                        pe.wait_ge(c_hT.sem, c_hT.of(i, prior(u, TURNED)))
                        for k in range(KC):
                            t = pe.transpose(ps_T(u)[:, k * P:(k + 1) * P], h[:, u, k * P:(k + 1) * P], ident[:, :])
                        t.then_inc(c_T.sem, 1)

                    def multiply(i, u):
                        pe.wait_ge(c_hT.sem, c_hT.of(i, u))
                        pe.wait_ge(c_out.sem, c_out.of(i, prior(u, PRODUCT)))
                        for w, place in weights:
                            for k in range(KC):
                                m = pe.matmul(place(u), hT[:, u, k * P:(k + 1) * P], w(k), start=(k == 0), stop=(k == KC - 1))
                        m.then_inc(c_mm.sem, 1)
                    staged(pe, NT, UN, [(0, turn), (1, multiply)])

                if stores:
                    @blk.sync
                    def _(sp):
                        def store(i, u):
                            sp.wait_ge(c_out.sem, c_out.of(i, u))
                            store_sp(sp, i, u)
                        staged(sp, NT, UN, [(0, store)])
                        for u in range(UN):
                            sp.wait_ge(s_st[u].sem, s_st[u].base + (NT // UN) * 16 * stores)
            for c in (c_stat, c_sd, c_norm, c_h, c_T, c_hT, c_mm, c_out):
                c.close(NT)
            for c in s_st:
                c.close((NT // UN) * 16 * stores)

        def max_pass(G, side):
            with block() as blk:
                @blk.gpsimd
                def _(g):
                    def gather(i, b):
                        hold(g, "pool", c_eix.sem, c_eix.of(i, b, UB))
                        hold(g, "pool", s_hs[b].sem, s_hs[b].base + i * 16)
                        for k in range(J):
                            g.indirect_dma_start(G[b][:, k, :], None, tab, bass.IndirectOffsetOnAxis(ix[:, b, 0, k:k + 1], 0),
                                                 bounds_check=NT * P - 1, oob_is_err=False).then_inc(s_eg[b].sem, 16)
                    staged(g, NB, UB, [(0, gather)])

                @blk.vector
                def _(v):
                    chain.link(v.memset(G[UB - 1][:, J - 1, :], 0.0))
                    for m in range(2):
                        chain.link(v.tensor_copy(ix[:, m, 0, :], src_ix[:, m * J:(m + 1) * J]))
                        v.sem_inc(c_eix.sem, 1)

                    def fold(i, b):
                        n = i * UB + b
                        v.wait_ge(s_eg[b].sem, s_eg[b].base + (i * (16 * J) + 16 * J))
                        for k in range(J):
                            before = G[b][:, k - 1, :] if k else G[(b - 1) % UB][:, J - 1, :]
                            chain.link(v.scalar_tensor_tensor(out=G[b][:, k, :], in0=before, scalar=reset[:, bass.ds(n * J + k, 1)],
                                                              in1=G[b][:, k, :], op0=ALU.add, op1=ALU.max))
                        v.sem_inc(c_batch.sem, 1)
                        chain.link(v.tensor_copy(ix[:, (b + 2) % UB, 0, :], src_ix[:, bass.ds(n * J + 2 * J, J)]))
                        v.sem_inc(c_eix.sem, 1)
                    before, after = side.vector(v)
                    staged(v, NB, UB, before + [(0, fold)] + after, chain, J + 1 + side.links)

                @blk.sync
                def _(sp):
                    def store(i, b):
                        sp.wait_ge(c_batch.sem, c_batch.of(i, b, UB))
                        sp.dma_start(hist_p[:, bass.ds((i * UB + b) * J, J), :], G[b][:, :, :]).then_inc(s_hs[b].sem, 16)
                    staged(sp, NB, UB, [(0, store)])
                    for b in range(UB):
                        sp.wait_ge(s_hs[b].sem, s_hs[b].base + (NB // UB) * 16)

                @blk.tensor
                def _(pe):
                    staged(pe, NB, UB, side.tensor(pe))

                if side.scalar is not None:
                    @blk.scalar
                    def _(a):
                        staged(a, NB, UB, side.scalar(a))
            c_eix.close(NB + 2)
            c_batch.close(NB)
            for b in range(UB):
                s_eg[b].close(NB // UB * 16 * J)
                s_hs[b].close(NB // UB * 16)
            side.close()

        def is_first(i, b, k=0):
            return isinstance(i, int) and i * UB + b == 0 and k == 0

        def columns(i, b, k):
            return i * (UB * J) + (b * J + k + 1)

        def one_hots(v, low, high, iota, dlo, dhi, n):
            chain.inc(v.tensor_tensor(low, iota[:, None, :].to_broadcast([P, J, P]),
                                      dlo[:, bass.ds(n * J, J)][:, :, None].to_broadcast([P, J, P]), ALU.is_equal))
            chain.link(v.tensor_tensor(high, iota[:, None, 0:NT].to_broadcast([P, J, NT]),
                                       dhi[:, bass.ds(n * J, J)][:, :, None].to_broadcast([P, J, NT]), ALU.is_equal))

        def split_keys(v, key_ix, ti, lo, hi):
            chain.link(v.tensor_scalar(ti[:, :], key_ix[:, 0:CH], P - 1, None, ALU.bitwise_and))
            chain.link(v.tensor_copy(lo[:, :], ti[:, :]))
            chain.link(v.tensor_scalar(ti[:, :], key_ix[:, 0:CH], P.bit_length() - 1, None, ALU.logical_shift_right))
            chain.link(v.tensor_copy(hi[:, :], ti[:, :]))

        class Degrees:
            links = 6

            def __init__(self, st):
                self.cnt = [sb(st, "cnt", [P, NT]) for _ in range(2)]
                self.low = [sb(st, "low", [P, J, P], BF16) for _ in range(2)]
                self.high = [sb(st, "high", [P, J, NT], BF16) for _ in range(2)]
                self.iota = sb(st, "iota", [P, P], BF16)
                self.lo = [sb(st, "lo", [P, CH], BF16) for _ in range(2)]
                self.hi = [sb(st, "hi", [P, CH], BF16) for _ in range(2)]
                self.c_oh, self.c_mm = Count(sem("deg_oh")), Count(sem("deg_mm"))
                ti = sb(st, "ti", [P, CH], I32)
                const0 = const_base[0]
                const_base[0] += 1
                with block() as blk:
                    @blk.gpsimd
                    def _(g):
                        g.iota(ti[:, 0:P], [[1, P]], base=0, channel_multiplier=0).then_inc(s_const, 1)

                    @blk.vector
                    def _(v):
                        v.wait_ge(s_const, const0 + 1)
                        chain.link(v.tensor_copy(self.iota[:, :], ti[:, 0:P]))
                        for k, key in enumerate((dst_ix, src_ix)):
                            chain.inc(v.memset(self.cnt[k][:, :], 0.0))
                            split_keys(v, key, ti, self.lo[k], self.hi[k])

            def vector(self, v):
                def make(i, b):
                    for k in range(2):
                        one_hots(v, self.low[k][:, :, :], self.high[k][:, :, :], self.iota, self.lo[k], self.hi[k], i * UB + b)
                    v.sem_inc(self.c_oh.sem, 1)

                def add(i, b):
                    v.wait_ge(self.c_mm.sem, self.c_mm.of(i, b, UB))
                    for k in range(2):
                        chain.link(v.tensor_tensor(self.cnt[k][:, :], bank[k][:, 0:NT], self.cnt[k][:, :], ALU.add))
                return [(0, make)], [(0, add)]

            def tensor(self, pe):
                def count(i, b):
                    pe.wait_ge(self.c_oh.sem, self.c_oh.of(i, b, UB))
                    for n in range(2):
                        for k in range(J):
                            m = pe.matmul(bank[n][:, 0:NT], self.low[n][:, k, :], self.high[n][:, k, :], start=(k == 0), stop=(k == J - 1))
                    m.then_inc(self.c_mm.sem, 1)
                return [(0, count)]

            scalar = None

            def close(self):
                pass

        class Ranks:
            links = 2 + 3 + 2

            def __init__(self, st, place):
                self.place = place
                self.low = [sb(st, "low", [P, J, P], BF16) for _ in range(UB)]
                self.high = [sb(st, "high", [P, J, NT], BF16) for _ in range(UB)]
                self.lowT = [sb(st, "lowT", [P, J, P]) for _ in range(UB)]
                self.same = [sb(st, "same", [P, J, P], BF16)]
                self.before = sb(st, "before", [P, UB, NT])
                self.first = sb(st, "first", [P, NT])
                self.iota = sb(st, "iota", [P, P], BF16)
                self.identb = sb(st, "identb", [P, P], BF16)
                self.upper = sb(st, "upper", [P, P])
                self.pick = sb(st, "pick", [P, J, NT])
                self.lo, self.hi = sb(st, "lo", [P, CH], BF16), sb(st, "hi", [P, CH], BF16)
                self.c = {n: Count(sem("rank_" + n)) for n in ("oh", "turn", "lowT", "pair", "same", "upd", "before", "sum", "place", "init")}
                const0 = const_base[0]
                const_base[0] += 2
                with scope() as t, block() as blk:
                    ti = sb(t, "ti", [P, CH], I32)

                    @blk.gpsimd
                    def _(g):
                        g.iota(ti[:, 0:P], [[1, P]], base=0, channel_multiplier=0).then_inc(s_const, 1)
                        g.affine_select(out=self.upper[:, :], in_=ones[:, :], compare_op=ALU.is_gt, fill=0.0, base=0,
                                        pattern=[[1, P]], channel_multiplier=-1).then_inc(s_const, 1)

                    @blk.vector
                    def _(v):
                        v.wait_ge(s_const, const0 + 2)
                        chain.link(v.tensor_copy(self.iota[:, :], ti[:, 0:P]))
                        chain.link(v.tensor_copy(self.identb[:, :], ident[:, :]))
                        chain.link(v.tensor_tensor(self.first[:, :], srt_src[:, :], deg_src[:, :], ALU.subtract))
                        split_keys(v, src_ix, ti, self.lo, self.hi)

            def vector(self, v):
                c = self.c

                def make(i, b):
                    one_hots(v, self.low[b][:, :, :], self.high[b][:, :, :], self.iota, self.lo, self.hi, i * UB + b)
                    v.sem_inc(c["oh"].sem, 1)

                def mask(i, b):
                    v.wait_ge(c["pair"].sem, c["pair"].of(i, b, UB))
                    same = self.same[0]
                    for k in range(0, J, 4):
                        n = min(4, J - k)
                        m = v.tensor_tensor(same[:, k:k + n, :], bank[2 + k // 4][:, 0:n * P].rearrange("p (k e) -> p k e", e=P),
                                            self.upper[:, None, :].to_broadcast([P, n, P]), ALU.mult)
                        chain.link(m) if k + 4 >= J else chain.inc(m)
                    v.sem_inc(c["same"].sem, 1)

                def choose(i, b):
                    v.wait_ge(c["sum"].sem, c["sum"].of(i, b, UB))
                    chain.link(v.tensor_tensor(self.pick[:, :, :], bank[5][:, 0:J * NT].rearrange("p (k t) -> p k t", t=NT),
                                               self.high[b][:, :, :], ALU.mult))
                    chain.link(v.tensor_reduce(self.place[:, bass.ds((i * UB + b) * J, J)], self.pick[:, :, :], AX.X, ALU.add))
                    v.sem_inc(c["place"].sem, 1)
                return [(3, choose), (0, make)], [(2, mask)]

            def scalar(self, a):
                c = self.c

                def copy_low(i, b):
                    a.wait_ge(c["turn"].sem, c["turn"].of(i, b, UB))
                    for k in range(0, J, 8):
                        n = min(8, J - k)
                        m = a.activation(self.lowT[b][:, k:k + n, :], self.bf(k // 8)[:, 0:n * P].rearrange("p (k e) -> p k e", e=P), ACT.Copy)
                    m.then_inc(c["lowT"].sem, 1)

                def copy_before(i, b):
                    if is_first(i, b):
                        a.wait_ge(c["init"].sem, 1)
                        a.activation(self.before[:, 0, :], bank[6][:, 0:NT], ACT.Copy).then_inc(c["before"].sem, 1)
                    for k in range(J):
                        a.wait_ge(c["upd"].sem, columns(i, b, k))
                        a.activation(self.before[:, (k + 1) % UB, :], bank[6][:, 0:NT], ACT.Copy).then_inc(c["before"].sem, 1)
                return [(0, copy_low), (2, copy_before)]

            def bf(self, n):
                return bank[n][:, :].bitcast(BF16)

            def tensor(self, pe):
                c = self.c

                def turn(i, b):
                    pe.wait_ge(c["oh"].sem, c["oh"].of(i, b, UB))
                    pe.wait_ge(c["lowT"].sem, c["lowT"].of(i, b - 1, UB))
                    for k in range(J):
                        t = pe.transpose(self.bf(k // 8)[:, (k % 8) * P:(k % 8 + 1) * P], self.low[b][:, k, :], self.identb[:, :])
                    t.then_inc(c["turn"].sem, 1)

                def pair(i, b):
                    pe.wait_ge(c["lowT"].sem, c["lowT"].of(i, b, UB))
                    pe.wait_ge(c["same"].sem, c["same"].of(i, b - 1, UB))
                    for k in range(J):
                        t = pe.matmul(bank[2 + k // 4][:, (k % 4) * P:(k % 4 + 1) * P], self.lowT[b][:, k, :], self.lowT[b][:, k, :],
                                      start=True, stop=True)
                    t.then_inc(c["pair"].sem, 1)

                def add_up(i, b):
                    if is_first(i, b):
                        pe.matmul(bank[6][:, 0:NT], ident[:, :], self.first[:, :], start=True, stop=True,
                                  skip_group_check=True).then_inc(c["init"].sem, 1)
                    pe.wait_ge(c["same"].sem, c["same"].of(i, b, UB))
                    pe.wait_ge(c["place"].sem, c["place"].of(i, b - 1, UB))
                    for k in range(J):
                        to = bank[5][:, k * NT:(k + 1) * NT]
                        pe.matmul(to, self.same[0][:, k, :], self.high[b][:, k, :], start=True, stop=False)
                        pe.wait_ge(c["before"].sem, columns(i, b, k))
                        pe.matmul(bank[6][:, 0:NT], self.low[b][:, k, :], self.high[b][:, k, :], start=False, stop=True,
                                  skip_group_check=True).then_inc(c["upd"].sem, 1)
                        m = pe.matmul(to, self.lowT[b][:, k, :], self.before[:, k % UB, :], start=False, stop=True)
                    m.then_inc(c["sum"].sem, 1)
                return [(0, turn), (1, pair), (2, add_up)]

            def close(self):
                pass

        class Permute:
            links = 3 * J
            RG = 3

            def __init__(self, st, place):
                self.row, self.col = sb(st, "row", [P, CH]), sb(st, "col", [P, CH])
                self.lo, self.hi = sb(st, "lo", [P, CH]), sb(st, "hi", [P, CH])
                self.iota = sb(st, "iota", [P, CH], I16)
                self.cols = sb(st, "cols", [P, self.RG, CH], BF16)
                self.rows = sb(st, "rows", [P, self.RG, 2, P], BF16)
                self.c_oh, self.c_mm = Count(sem("perm_oh")), Count(sem("perm_mm"))
                const0 = const_base[0]
                const_base[0] += 1
                with scope() as t, block() as blk:
                    ti = sb(t, "ti", [P, CH], I32)
                    tf = sb(t, "tf", [P, CH])

                    @blk.gpsimd
                    def _(g):
                        g.iota(ti[:, :], [[1, CH]], base=0, channel_multiplier=0).then_inc(s_const, 1)

                    @blk.vector
                    def _(v):
                        v.wait_ge(s_const, const0 + 1)
                        chain.link(v.tensor_copy(self.iota[:, :], ti[:, :]))
                        split_keys(v, dst_ix, ti, self.lo, self.hi)
                        divide(v, place[:, :], self.row[:, :], self.col[:, :], ti[:, :], tf[:, :])

            def vector(self, v):
                def make(i, b):
                    n = i * UB + b
                    for k in range(J):
                        r = k % self.RG
                        if not (isinstance(i, int) and i * UB + b == 0 and k < self.RG):
                            v.wait_ge(self.c_mm.sem, columns(i, b, k - self.RG))
                        at = bass.ds(n * J + k, 1)
                        chain.inc(v.tensor_scalar(self.cols[:, r, :], self.iota[:, :], self.col[:, at], None, ALU.is_equal))
                        for m, val in enumerate((self.lo, self.hi)):
                            chain.inc(v.tensor_scalar(self.rows[:, r, m, :], self.iota[:, 0:P], self.row[:, at], val[:, at], ALU.is_equal, ALU.mult))
                        v.wait_ge(chain.sem, chain.base + chain.term)
                        v.sem_inc(self.c_oh.sem, 1)
                return [], [(0, make)]

            def tensor(self, pe):
                def put(i, b):
                    for k in range(J):
                        r = k % self.RG
                        pe.wait_ge(self.c_oh.sem, columns(i, b, k))
                        for m in range(2):
                            for half, (c0, c1) in enumerate(((0, 512), (512, CH))):
                                t = pe.matmul(bank[2 * m + half][:, 0:c1 - c0], self.rows[:, r, m, :], self.cols[:, r, c0:c1],
                                              start=is_first(i, b, k), stop=True, skip_group_check=True)
                        t.then_inc(self.c_mm.sem, 1)
                return [(0, put)]

            scalar = None

            def close(self):
                with block() as blk:
                    @blk.vector
                    def _(v):
                        for half, (c0, c1) in enumerate(((0, 512), (512, CH))):
                            chain.link(v.tensor_copy(self.lo[:, c0:c1], bank[half][:, 0:c1 - c0]))
                            chain.link(v.scalar_tensor_tensor(out=self.lo[:, c0:c1], in0=bank[2 + half][:, 0:c1 - c0], scalar=float(P),
                                                              in1=self.lo[:, c0:c1], op0=ALU.mult, op1=ALU.add))
                        chain.link(v.tensor_copy(dst_ix[:, 0:CH], self.lo[:, :]))

        def divide(v, a, quot, rest, ti, tf):
            chain.link(v.tensor_scalar(tf, a, 1.0 / CH, None, ALU.mult))
            chain.link(v.tensor_copy(ti, tf))
            chain.link(v.tensor_copy(quot, ti))
            chain.link(v.scalar_tensor_tensor(out=rest, in0=quot, scalar=-float(CH), in1=a, op0=ALU.mult, op1=ALU.add))
            for op, bound, by in ((ALU.is_lt, 0.0, -1.0), (ALU.is_ge, float(CH), 1.0)):
                chain.link(v.tensor_scalar(tf, rest, bound, by, op, ALU.mult))
                chain.link(v.tensor_tensor(quot, quot, tf, ALU.add))
                chain.link(v.scalar_tensor_tensor(out=rest, in0=tf, scalar=-float(CH), in1=rest, op0=ALU.mult, op1=ALU.add))

        def sources_in_order():
            with scope() as st:
                row, col = sb(st, "row", [P, NT]), sb(st, "col", [P, NT])
                has, base = sb(st, "has", [P, NT]), sb(st, "base", [P, NT])
                tile = sb(st, "tile", [P, NT])
                lo, hi = sb(st, "lo", [P, NT]), sb(st, "hi", [P, NT])
                iota = sb(st, "iota", [P, CH], I16)
                cols = sb(st, "cols", [P, 2, CH], BF16)
                rows_ = sb(st, "rows", [P, 2, 2, P], BF16)
                done = sb(st, "done", [P, P, NT])
                fin = sb(st, "fin", [P, P])
                bound = sb(st, "bound", [P, P])
                start = sb(st, "start", [P, 1])
                zero = sb(st, "zero", [P, CH])
                marks = sb(st, "marks", [P, CH])
                ti = sb(st, "ti", [P, CH], I32)
                tj = sb(st, "tj", [P, NT], I32)
                tb = sb(st, "tb", [P, P], I32)
                tf = sb(st, "tf", [P, NT])
                pi = sb(st, "pi", [P, 1], I32)
                c_oh, c_mm2 = Count(sem("srt_oh")), Count(sem("srt_mm"))
                const0 = const_base[0]
                const_base[0] += 4
                with block() as blk:
                    @blk.gpsimd
                    def _(g):
                        g.iota(ti[:, :], [[1, CH]], base=0, channel_multiplier=0).then_inc(s_const, 1)
                        g.iota(tj[:, :], [[1, NT]], base=0, channel_multiplier=0).then_inc(s_const, 1)
                        g.iota(tb[:, :], [[CH, P]], base=0, channel_multiplier=0).then_inc(s_const, 1)
                        g.iota(pi[:, :], [[0, 1]], base=0, channel_multiplier=1).then_inc(s_const, 1)

                    @blk.vector
                    def _(v):
                        v.wait_ge(s_const, const0 + 4)
                        chain.inc(v.memset(zero[:, :], 0.0))
                        chain.inc(v.tensor_copy(iota[:, :], ti[:, :]))
                        chain.inc(v.tensor_copy(bound[:, :], tb[:, :]))
                        chain.inc(v.tensor_copy(tile[:, :], tj[:, :]))
                        chain.inc(v.tensor_copy(start[:, :], pi[:, :]))
                        chain.inc(v.tensor_scalar(has[:, :], deg_src[:, :], 0.0, None, ALU.is_gt))
                        chain.link(v.tensor_tensor(base[:, :], srt_src[:, :], deg_src[:, :], ALU.subtract))
                        chain.link(v.tensor_tensor(hi[:, :], tile[:, :], has[:, :], ALU.mult))
                        chain.link(v.tensor_scalar(lo[:, :], has[:, :], start[:, 0:1], None, ALU.mult))
                        divide(v, base[:, :], row[:, :], col[:, :], tj[:, :], tf[:, :])
                        for t in range(NT):
                            r = t % 2
                            if t >= 2:
                                v.wait_ge(c_mm2.sem, t - 1)
                            chain.inc(v.tensor_scalar(cols[:, r, :], iota[:, :], col[:, t:t + 1], None, ALU.is_equal))
                            for m, val in enumerate((lo, hi)):
                                chain.link(v.tensor_scalar(rows_[:, r, m, :], iota[:, 0:P], row[:, t:t + 1], val[:, t:t + 1], ALU.is_equal, ALU.mult))
                            v.sem_inc(c_oh.sem, 1)
                        chain.link(v.tensor_tensor(done[:, :, :], srt_src[:, None, :].to_broadcast([P, P, NT]),
                                                   bound[:, :, None].to_broadcast([P, P, NT]), ALU.is_le))
                        chain.link(v.tensor_reduce(fin[:, :], done[:, :, :], AX.X, ALU.add))
                        v.sem_inc(s_dve.sem, 1)
                        v.wait_ge(c_mm2.sem, NT + 1)
                        chain.link(v.tensor_copy(start[:, :], bank[4][:, 0:1]))
                        for half, (c0, c1) in enumerate(((0, 512), (512, CH))):
                            chain.link(v.tensor_copy(marks[:, c0:c1], bank[half][:, 0:c1 - c0]))
                            chain.link(v.scalar_tensor_tensor(out=marks[:, c0:c1], in0=bank[2 + half][:, 0:c1 - c0], scalar=float(P),
                                                              in1=marks[:, c0:c1], op0=ALU.mult, op1=ALU.add))
                        chain.link(v.tensor_tensor_scan(marks[:, :], zero[:, :], marks[:, :], start[:, 0:1], ALU.add, ALU.max))
                        chain.link(v.tensor_copy(src_ix[:, 0:CH], marks[:, :]))

                    @blk.tensor
                    def _(pe):
                        for t in range(NT):
                            r = t % 2
                            pe.wait_ge(c_oh.sem, t + 1)
                            for m in range(2):
                                for half, (c0, c1) in enumerate(((0, 512), (512, CH))):
                                    x_ = pe.matmul(bank[2 * m + half][:, 0:c1 - c0], rows_[:, r, m, :], cols[:, r, c0:c1],
                                                   start=(t == 0), stop=True, skip_group_check=True)
                            x_.then_inc(c_mm2.sem, 1)
                        pe.wait_ge(s_dve.sem, s_dve.base + 1)
                        pe.matmul(bank[4][:, 0:1], fin[:, :], ones[:, 0:1], start=True, stop=True).then_inc(c_mm2.sem, 1)
                s_dve.close(1)

        def find_rows(cnts):
            with ExitStack() as st, block() as blk:
                upto = sb(st, "upto", [P, P])
                tot, cum, has = sb(st, "tot", [P, 2, NT]), sb(st, "cum", [P, 2, NT]), sb(st, "has", [P, NT])
                const0 = const_base[0]
                const_base[0] += 1

                @blk.gpsimd
                def _(g):
                    g.affine_select(out=upto[:, :], in_=ones[:, :], compare_op=ALU.is_ge, fill=0.0, base=0,
                                    pattern=[[1, P]], channel_multiplier=-1).then_inc(s_const, 1)

                @blk.tensor
                def _(pe):
                    pe.wait_ge(s_const, const0 + 1)
                    for k in range(2):
                        pe.matmul(bank[2 * k][:, 0:NT], upto[:, :], cnts[k][:, :], start=True, stop=True)
                        m = pe.matmul(bank[2 * k + 1][:, 0:NT], ones[:, :], cnts[k][:, :], start=True, stop=True)
                    m.then_inc(s_pe.sem, 1)

                @blk.vector
                def _(v):
                    v.wait_ge(s_pe.sem, s_pe.base + 1)
                    for k, dest in enumerate((node_ix, node_ix2)):
                        c, t = cum[:, k, :], tot[:, k, :]
                        chain.link(v.tensor_copy(t, bank[2 * k + 1][:, 0:NT]))
                        chain.link(v.tensor_tensor_scan(c, ones[:, 0:NT], t, 0.0, ALU.mult, ALU.add))
                        chain.link(v.tensor_tensor(c, c, t, ALU.subtract))
                        chain.link(v.tensor_tensor(c, bank[2 * k][:, 0:NT], c, ALU.add))
                        if k:
                            chain.inc(v.tensor_copy(srt_src[:, :], c))
                            chain.inc(v.tensor_copy(deg_src[:, :], cnts[k][:, :]))
                        chain.link(v.tensor_scalar(has[:, :], cnts[k][:, :], 0.0, None, ALU.is_gt))
                        chain.link(v.tensor_scalar(c, c, -1.0 - EMPTY, None, ALU.add))
                        chain.link(v.tensor_tensor(c, c, has[:, :], ALU.mult))
                        chain.link(v.tensor_scalar(c, c, float(EMPTY), None, ALU.add))
                        chain.link(v.tensor_copy(dest[:, :], c))
            s_pe.close(1)

        def carry_max(G):
            last = G[UB - 1][:, J - 1, :]
            with ExitStack() as st, block() as blk:
                scanned = sb(st, "scanned", [P, KC, P])
                found = sb(st, "found", [P, D])
                m0 = s_misc.base

                @blk.tensor
                def _(pe):
                    for k in range(KC):
                        t = pe.transpose(bank[0][:, k * P:(k + 1) * P], last[:, k * P:(k + 1) * P], ident[:, :])
                    t.then_inc(s_pe.sem, 1)
                    pe.wait_ge(s_dve.sem, s_dve.base + 2)
                    for k in range(KC):
                        t = pe.transpose(bank[1][:, k * P:(k + 1) * P], scanned[:, k, :], ident[:, :])
                    t.then_inc(s_pe.sem, 1)

                @blk.vector
                def _(v):
                    chain.link(v.memset(found[:, :], 0.0))
                    v.sem_inc(s_dve.sem, 1)
                    chain.link(v.memset(scanned[:, :, 0:1], NEG))
                    v.wait_ge(s_pe.sem, s_pe.base + 1)
                    for k in range(KC):
                        chain.link(v.tensor_tensor_scan(scanned[:, k, 1:P], Rrow[:, 0:P - 1], bank[0][:, k * P:(k + 1) * P - 1],
                                                        NEG, ALU.add, ALU.max))
                    v.sem_inc(s_dve.sem, 1)
                    v.wait_ge(s_pe.sem, s_pe.base + 2)
                    v.wait_ge(s_misc.sem, m0 + 16)
                    chain.link(v.tensor_tensor(found[:, :], bank[1][:, 0:D], found[:, :], ALU.max))
                    v.sem_inc(s_dve.sem, 1)

                @blk.gpsimd
                def _(g):
                    g.wait_ge(s_dve.sem, s_dve.base + 1)
                    g.indirect_dma_start(found[:, :], None, hist, bass.IndirectOffsetOnAxis(fix_ix[:, 0:1], 0),
                                         bounds_check=EMPTY - 1, oob_is_err=False).then_inc(s_misc.sem, 16)
                    g.wait_ge(s_dve.sem, s_dve.base + 3)
                    g.indirect_dma_start(hist, bass.IndirectOffsetOnAxis(fix_ix[:, 0:1], 0), found[:, :], None,
                                         bounds_check=EMPTY - 1, oob_is_err=False).then_inc(s_misc.sem, 16)
                    g.wait_ge(s_misc.sem, m0 + 32)
            s_pe.close(2)
            s_dve.close(3)
            s_misc.close(32)

        def node_gathers(blk, pool, table, width):
            @blk.gpsimd
            def _(g):
                def gather(i, u):
                    hold(g, "pool", c_ix.sem, c_ix.of(i, u))
                    hold(g, "pool", c_T.sem, c_T.of(i - 1, u))
                    g.indirect_dma_start(pool[:, u, 0:width], None, table, bass.IndirectOffsetOnAxis(nix[:, u:u + 1], 0),
                                         bounds_check=EMPTY, oob_is_err=False).then_inc(s_gat[u].sem, 16)
                staged(g, NT, UN, [(0, gather)])

        def place_ix(v, rows_of):
            def stage(i, u):
                v.wait_ge(s_gat[u].sem, s_gat[u].base + i * 16)
                chain.link(v.tensor_copy(nix[:, u:u + 1], rows_of[:, bass.ds(i * UN + u, 1)]))
                v.sem_inc(c_ix.sem, 1)
            return stage

        def combine(U, w, gain, bias, nxt):
            residual = gain is not None
            with scope() as st, block() as blk:
                hT, o, y, pool = (ring(st, n) for n in ("hT", "o", "y", "pool"))
                if residual:
                    cur = ring(st, "cur")
                if nxt:
                    hT2 = ring(st, "hT2")
                    w_next, b_next = nxt
                node_gathers(blk, pool, hist, D)
                final = c_out if residual else c_z

                def small(u):
                    return bank[2 + TURNED[u]][:, 0:D]

                def turned2(u):
                    return bank[4 + TURNED[u]][:, 0:D]

                def next_U(u):
                    return bank[6 + TURNED[u]][:, 0:D]

                @blk.vector
                def _(v):
                    stats, recip, _ = norm_stages(v, None, lambda i, u: y[:, u, :])

                    def join(i, u):
                        v.wait_ge(c_mm.sem, c_mm.of(i, u))
                        v.wait_ge(c_z.sem, c_z.of(i - 1, u))
                        chain.link(v.tensor_tensor(y[:, u, :], small(u), U[:, i * UN + u, :], ALU.add))
                        if residual:
                            v.wait_ge(s_cur[u].sem, s_cur[u].base + (i * 16 + 16))
                            chain.link(v.scalar_tensor_tensor(out=y[:, u, :], in0=y[:, u, :], scalar=0.0, in1=cur[:, u, :],
                                                              op0=ALU.max, op1=ALU.add))
                        v.sem_inc(c_y.sem, 1)
                        if residual:
                            stats(i, u)

                    def scale(i, u):
                        v.wait_ge(c_z.sem, c_z.of(i, u))
                        chain.link(v.tensor_tensor(o[:, u, :], o[:, u, :], gain[:, :], ALU.mult))
                        chain.link(v.tensor_tensor(o[:, u, :], o[:, u, :], bias[:, :], ALU.add))
                        if not nxt:
                            chain.link(v.tensor_tensor(X[:, i * UN + u, :], o[:, u, :], X[:, i * UN + u, :], ALU.add))
                        v.sem_inc(c_out.sem, 1)
                    if residual:
                        staged(v, NT, UN, [(0, place_ix(v, node_ix)), (5, join), (6, recip), (7, scale)], chain, 9 if nxt else 10)
                    else:
                        staged(v, NT, UN, [(0, place_ix(v, node_ix)), (5, join)], chain, 2)

                @blk.scalar
                def _(a):
                    _, _, sqrt = norm_stages(None, a, None)

                    def evac(i, u):
                        a.wait_ge(c_T.sem, c_T.of(i, u))
                        a.wait_ge(c_mm.sem, c_mm.of(i - 1, u))
                        a.activation(hT[:, u, :], ps_T(u), ACT.Copy).then_inc(c_hT.sem, 1)

                    def free_o(i, u):
                        if nxt:
                            a.wait_ge(s_st[u].sem, s_st[u].base + i * 16)
                            a.wait_ge(c_T2.sem, c_T2.of(i - 1, u))
                        else:
                            a.wait_ge(c_out.sem, c_out.of(i - 1, u))

                    def relu(i, u):
                        a.wait_ge(c_y.sem, c_y.of(i, u))
                        free_o(i, u)
                        a.activation(o[:, u, :], y[:, u, :], ACT.Relu).then_inc(c_z.sem, 1)

                    def normal(i, u):
                        a.wait_ge(c_norm.sem, c_norm.of(i, u))
                        free_o(i, u)
                        a.activation(o[:, u, :], y[:, u, :], ACT.Identity, bias=nmr[:, u:u + 1],
                                     scale=rstd[:, u:u + 1]).then_inc(c_z.sem, 1)

                    def evac2(i, u):
                        a.wait_ge(c_T2.sem, c_T2.of(i, u))
                        a.wait_ge(c_mm2.sem, c_mm2.of(i - 1, u))
                        a.activation(hT2[:, u, :], turned2(u), ACT.Copy).then_inc(c_hT2.sem, 1)

                    def keep(i, u):
                        a.wait_ge(c_mm2.sem, c_mm2.of(i, u))
                        a.activation(U[:, i * UN + u, :], next_U(u), ACT.Copy).then_inc(c_keep.sem, 1)
                    staged(a, NT, UN, [(3, evac)] + ([(5, sqrt), (6, normal)] if residual else [(5, relu)])
                           + ([(7, evac2), (8, keep)] if nxt else []))

                @blk.tensor
                def _(pe):
                    def turn(i, u):
                        pe.wait_ge(s_gat[u].sem, s_gat[u].base + (i * 16 + 16))
                        pe.wait_ge(c_hT.sem, c_hT.of(i, prior(u, TURNED)))
                        for k in range(KC):
                            t = pe.transpose(ps_T(u)[:, k * P:(k + 1) * P], pool[:, u, k * P:(k + 1) * P], ident[:, :])
                        t.then_inc(c_T.sem, 1)

                    def multiply(i, u):
                        pe.wait_ge(c_hT.sem, c_hT.of(i, u))
                        pe.wait_ge(c_y.sem, c_y.of(i, prior(u, TURNED)))
                        for k in range(KC):
                            m = pe.matmul(small(u), hT[:, u, k * P:(k + 1) * P], w[:, k, :], start=(k == 0), stop=(k == KC - 1))
                        m.then_inc(c_mm.sem, 1)

                    def turn2(i, u):
                        pe.wait_ge(final.sem, final.of(i, u))
                        pe.wait_ge(c_hT2.sem, c_hT2.of(i, prior(u, TURNED)))
                        for k in range(KC):
                            t = pe.transpose(turned2(u)[:, k * P:(k + 1) * P], o[:, u, k * P:(k + 1) * P], ident[:, :])
                        t.then_inc(c_T2.sem, 1)

                    def multiply2(i, u):
                        pe.wait_ge(c_hT2.sem, c_hT2.of(i, u))
                        pe.wait_ge(c_keep.sem, c_keep.of(i, prior(u, TURNED)))
                        pe.matmul(next_U(u), ones[0:1, :], b_next[0:1, :], start=True, stop=False)
                        for k in range(KC):
                            m = pe.matmul(next_U(u), hT2[:, u, k * P:(k + 1) * P], w_next[:, k, :], start=False, stop=(k == KC - 1))
                        m.then_inc(c_mm2.sem, 1)
                    staged(pe, NT, UN, [(0, turn), (1, multiply)] + ([(4, turn2), (5, multiply2)] if nxt else []))

                if residual or nxt:
                    @blk.sync
                    def _(sp):
                        def load(i, u):
                            sp.wait_ge(c_y.sem, c_y.of(i - 1, u))
                            sp.dma_start(cur[:, u, :], tab_t[bass.ds(i * UN + u, 1), :, :].rearrange("a p f -> p (a f)")).then_inc(s_cur[u].sem, 16)

                        def store(i, u):
                            sp.wait_ge(final.sem, final.of(i, u))
                            sp.dma_start(tab_t[bass.ds(i * UN + u, 1), :, :].rearrange("a p f -> p (a f)"), o[:, u, :]).then_inc(s_st[u].sem, 16)
                        staged(sp, NT, UN, ([(0, load)] if residual else []) + ([(6, store)] if nxt else []))
                        if nxt:
                            for u in range(UN):
                                sp.wait_ge(s_st[u].sem, s_st[u].base + NT // UN * 16)
            for c in (c_ix, c_T, c_hT, c_mm, c_y, c_z):
                c.close(NT)
            if residual:
                for c in (c_stat, c_sd, c_norm, c_out):
                    c.close(NT)
            if nxt:
                for c in (c_T2, c_hT2, c_mm2, c_keep):
                    c.close(NT)
            for u in range(UN):
                s_gat[u].close(NT // UN * 16)
                s_cur[u].close(NT // UN * 16 * residual)
                s_st[u].close(NT // UN * 16 * bool(nxt))

        def attention_pass(KVb, Qb, s, w, tmp):
            with block() as blk:
                @blk.gpsimd
                def _(g):
                    def gather(i, b):
                        hold(g, "pool", c_eix.sem, c_eix.of(i, b, UB))
                        hold(g, "pool", s_hs[b].sem, s_hs[b].base + i * 16)
                        for k in range(J):
                            g.indirect_dma_start(KVb[b][:, k, 0:KV], None, kvtab, bass.IndirectOffsetOnAxis(ix[:, b, 0, k:k + 1], 0),
                                                 bounds_check=NT * P - 1, oob_is_err=False).then_inc(s_eg[b].sem, 16)
                            g.indirect_dma_start(Qb[b][:, k, :], None, qtab, bass.IndirectOffsetOnAxis(ix[:, b, 1, k:k + 1], 0),
                                                 bounds_check=NT * P - 1, oob_is_err=False).then_inc(s_eg[b].sem, 16)
                    staged(g, NB, UB, [(0, gather)])

                @blk.vector
                def _(v):
                    chain.link(v.memset(KVb[UB - 1][:, J - 1, D:ROW], 0.0))
                    for m in range(2):
                        chain.inc(v.tensor_copy(ix[:, m, 0, :], dst_ix[:, m * J:(m + 1) * J]))
                        chain.link(v.tensor_copy(ix[:, m, 1, :], src_ix[:, m * J:(m + 1) * J]))
                        v.sem_inc(c_eix.sem, 1)

                    def heads(ap):
                        return ap.rearrange("p (d h) -> p d h", h=HEADS)

                    def fold(i, b):
                        n = i * UB + b
                        kv, prev = KVb[b], KVb[(b - 1) % UB]
                        rs = reset[:, bass.ds(n * J, J)]
                        top_m = kv[:, :, KV:ROW]
                        v.wait_ge(s_eg[b].sem, s_eg[b].base + (i * (32 * J) + 32 * J))
                        chain.link(v.tensor_tensor(kv[:, :, 0:D], kv[:, :, 0:D], Qb[b][:, :, :], ALU.mult))
                        chain.link(v.tensor_reduce(s[:, :, :], kv[:, :, 0:D].rearrange("p j (d h) -> p j h d", h=HEADS), AX.X, ALU.add))
                        for e in range(HEADS):
                            at = chain.inc(v.tensor_tensor_scan(kv[:, :, KV + e:KV + e + 1].rearrange("p j a -> p (j a)"), rs,
                                                                s[:, :, e:e + 1].rearrange("p j a -> p (j a)"),
                                                                prev[:, J - 1, KV + e:KV + e + 1], ALU.add, ALU.max))
                        v.wait_ge(chain.sem, at)
                        chain.inc(v.tensor_tensor(w[:, 0, :, :], s[:, :, :], top_m, ALU.subtract))
                        chain.inc(v.tensor_tensor(w[:, 1, 1:J, :], kv[:, 0:J - 1, KV:ROW], kv[:, 1:J, KV:ROW], ALU.subtract))
                        chain.link(v.tensor_tensor(w[:, 1, 0, :], prev[:, J - 1, KV:ROW], kv[:, 0, KV:ROW], ALU.subtract))
                        chain.link(v.tensor_tensor(w[:, 1, :, :], w[:, 1, :, :], rs[:, :, None].to_broadcast([P, J, HEADS]), ALU.add))
                        v.sem_inc(c_w.sem, 1)
                        v.wait_ge(c_e.sem, c_e.of(i, b, UB))
                        chain.link(v.tensor_tensor(kv[:, :, D:KV].rearrange("p j (d h) -> p j d h", h=HEADS),
                                                   kv[:, :, D:KV].rearrange("p j (d h) -> p j d h", h=HEADS),
                                                   w[:, 0, :, None, :].to_broadcast([P, J, ACC // HEADS, HEADS]), ALU.mult))
                        for k in range(J):
                            before = kv[:, k - 1, D:KV] if k else prev[:, J - 1, D:KV]
                            chain.link(v.tensor_tensor(heads(tmp[:, :]), heads(before),
                                                       w[:, 1, k, None, :].to_broadcast([P, ACC // HEADS, HEADS]), ALU.mult))
                            chain.link(v.tensor_tensor(kv[:, k, D:KV], kv[:, k, D:KV], tmp[:, :], ALU.add))
                        v.sem_inc(c_batch.sem, 1)
                        nxt = (b + 2) % UB
                        chain.inc(v.tensor_copy(ix[:, nxt, 0, :], dst_ix[:, bass.ds(n * J + 2 * J, J)]))
                        chain.link(v.tensor_copy(ix[:, nxt, 1, :], src_ix[:, bass.ds(n * J + 2 * J, J)]))
                        v.sem_inc(c_eix.sem, 1)
                    staged(v, NB, UB, [(0, fold)], chain, 2 + HEADS + 4 + 1 + 2 * J + 2)

                @blk.scalar
                def _(a):
                    def expo(i, b):
                        a.wait_ge(c_w.sem, c_w.of(i, b, UB))
                        a.activation(w[:, :, :, :], w[:, :, :, :], ACT.Exp).then_inc(c_e.sem, 1)
                    staged(a, NB, UB, [(0, expo)])

                @blk.sync
                def _(sp):
                    def store(i, b):
                        sp.wait_ge(c_batch.sem, c_batch.of(i, b, UB))
                        sp.dma_start(ahist_p[:, bass.ds((i * UB + b) * J, J), :], KVb[b][:, :, D:ROW]).then_inc(s_hs[b].sem, 16)
                    staged(sp, NB, UB, [(0, store)])
                    for b in range(UB):
                        sp.wait_ge(s_hs[b].sem, s_hs[b].base + (NB // UB) * 16)
            c_eix.close(NB + 2)
            for c in (c_batch, c_w, c_e):
                c.close(NB)
            for b in range(UB):
                s_eg[b].close(NB // UB * 32 * J)
                s_hs[b].close(NB // UB * 16)

        def carry_attention(KVb):
            last = KVb[UB - 1][:, J - 1, :]
            G8 = P // HEADS
            with ExitStack() as st, block() as blk:
                spread = sb(st, "spread", [P, 2, G8, HEADS])
                mc = sb(st, "mc", [P, P + 1])
                ar = sb(st, "ar", [P, 2, P])
                part = sb(st, "part", [P, 3, P])
                sc = sb(st, "sc", [P, 3, P + 1])
                found = sb(st, "found", [P, STATE])
                top_m = sb(st, "top_m", [P, HEADS])
                e2 = sb(st, "e2", [P, 2, HEADS])
                add = sb(st, "add", [P, ACC])
                m0 = s_misc.base

                @blk.tensor
                def _(pe):
                    pe.wait_ge(s_dve.sem, s_dve.base + 1)
                    ins = (last[:, D:D + P], last[:, D + P:D + 2 * P], spread[:, 0, :, :].rearrange("p a b -> p (a b)"),
                           spread[:, 1, :, :].rearrange("p a b -> p (a b)"))
                    for k, a in enumerate(ins):
                        t = pe.transpose(bank[0][:, k * P:(k + 1) * P], a, ident[:, :])
                    t.then_inc(s_pe.sem, 1)
                    pe.wait_ge(s_dve.sem, s_dve.base + 3)
                    for k, a in enumerate((sc[:, 0, 0:P], sc[:, 1, 0:P], sc[:, 2, 0:P], mc[:, 0:P])):
                        t = pe.transpose(bank[1][:, k * P:(k + 1) * P], a, ident[:, :])
                    t.then_inc(s_pe.sem, 1)

                @blk.scalar
                def _(a):
                    a.wait_ge(s_dve.sem, s_dve.base + 2)
                    a.activation(ar[:, :, :], ar[:, :, :], ACT.Exp).then_inc(c_e.sem, 1)
                    a.wait_ge(s_dve.sem, s_dve.base + 4)
                    a.activation(e2[:, :, :], e2[:, :, :], ACT.Exp).then_inc(c_e.sem, 1)

                @blk.vector
                def _(v):
                    chain.inc(v.memset(found[:, :], 0.0))
                    for k in range(2):
                        chain.link(v.tensor_copy(spread[:, k, :, :], last[:, None, KV - HEADS + k * HEADS:KV + k * HEADS]
                                                 .to_broadcast([P, G8, HEADS])))
                    v.sem_inc(s_dve.sem, 1)
                    chain.inc(v.memset(mc[:, 0:1], NEG))
                    chain.link(v.memset(sc[:, :, 0:1], 0.0))
                    v.wait_ge(s_pe.sem, s_pe.base + 1)
                    chain.link(v.tensor_tensor_scan(mc[:, 1:P + 1], Rrow[:, :], bank[0][:, 3 * P:4 * P], NEG, ALU.add, ALU.max))
                    chain.inc(v.tensor_tensor(ar[:, 0, :], bank[0][:, 3 * P:4 * P], mc[:, 1:P + 1], ALU.subtract))
                    chain.link(v.tensor_tensor(ar[:, 1, :], mc[:, 0:P], Rrow[:, :], ALU.add))
                    chain.link(v.tensor_tensor(ar[:, 1, :], ar[:, 1, :], mc[:, 1:P + 1], ALU.subtract))
                    v.sem_inc(s_dve.sem, 1)
                    v.wait_ge(c_e.sem, c_e.base + 1)
                    for k in range(3):
                        chain.link(v.tensor_tensor(part[:, k, :], bank[0][:, k * P:(k + 1) * P], ar[:, 0, :], ALU.mult))
                    for k in range(3):
                        chain.link(v.tensor_tensor_scan(sc[:, k, 1:P + 1], ar[:, 1, :], part[:, k, :], 0.0, ALU.mult, ALU.add))
                    v.sem_inc(s_dve.sem, 1)
                    v.wait_ge(s_pe.sem, s_pe.base + 2)
                    v.wait_ge(s_misc.sem, m0 + 16)
                    chain.link(v.tensor_tensor(top_m[:, :], bank[1][:, 3 * P:3 * P + HEADS], found[:, ACC:STATE], ALU.max))
                    chain.inc(v.tensor_tensor(e2[:, 0, :], found[:, ACC:STATE], top_m[:, :], ALU.subtract))
                    chain.link(v.tensor_tensor(e2[:, 1, :], bank[1][:, 3 * P:3 * P + HEADS], top_m[:, :], ALU.subtract))
                    v.sem_inc(s_dve.sem, 1)
                    v.wait_ge(c_e.sem, c_e.base + 2)

                    def by_head(ap):
                        return ap.rearrange("p (d h) -> p d h", h=HEADS)

                    def factor(k):
                        return e2[:, k, None, :].to_broadcast([P, ACC // HEADS, HEADS])
                    chain.inc(v.tensor_tensor(by_head(found[:, 0:ACC]), by_head(found[:, 0:ACC]), factor(0), ALU.mult))
                    chain.link(v.tensor_tensor(by_head(add[:, :]), by_head(bank[1][:, 0:ACC]), factor(1), ALU.mult))
                    chain.link(v.tensor_tensor(found[:, 0:ACC], found[:, 0:ACC], add[:, :], ALU.add))
                    v.sem_inc(s_dve.sem, 1)

                @blk.gpsimd
                def _(g):
                    g.wait_ge(s_dve.sem, s_dve.base + 1)
                    g.indirect_dma_start(found[:, :], None, ahist, bass.IndirectOffsetOnAxis(fix_ix[:, 0:1], 0),
                                         bounds_check=EMPTY - 1, oob_is_err=False).then_inc(s_misc.sem, 16)
                    g.wait_ge(s_dve.sem, s_dve.base + 5)
                    g.indirect_dma_start(ahist, bass.IndirectOffsetOnAxis(fix_ix[:, 0:1], 0), found[:, :], None,
                                         bounds_check=EMPTY - 1, oob_is_err=False).then_inc(s_misc.sem, 16)
                    g.wait_ge(s_misc.sem, m0 + 32)
            s_pe.close(2)
            s_dve.close(5)
            c_e.close(2)
            s_misc.close(32)

        def finish(w, bias):
            with ExitStack() as st, block() as blk:
                rz = sb(st, "rz", [P, UN, HEADS])
                h, hT, o, pool = ring(st, "h"), ring(st, "hT"), ring(st, "o"), ring(st, "pool", STATE)
                node_gathers(blk, pool, ahist, STATE)

                @blk.vector
                def _(v):
                    def divide(i, u):
                        v.wait_ge(s_gat[u].sem, s_gat[u].base + (i * 16 + 16))
                        chain.link(v.reciprocal(rz[:, u, :], pool[:, u, D:ACC]))
                        chain.link(v.tensor_tensor(h[:, u, :].rearrange("p (d h) -> p d h", h=HEADS),
                                                   pool[:, u, 0:D].rearrange("p (d h) -> p d h", h=HEADS),
                                                   rz[:, u, None, :].to_broadcast([P, HD, HEADS]), ALU.mult))
                        v.sem_inc(c_h.sem, 1)

                    def join(i, u):
                        v.wait_ge(c_mm.sem, c_mm.of(i, u))
                        v.wait_ge(s_st[u].sem, s_st[u].base + i * 16)
                        chain.link(v.tensor_tensor(o[:, u, :], ps_small(u), bias[:, :], ALU.add))
                        chain.link(v.tensor_tensor(o[:, u, :], o[:, u, :], X[:, bass.ds(i * UN + u, 1), :].rearrange("p a f -> p (a f)"), ALU.add))
                        v.sem_inc(c_out.sem, 1)
                    staged(v, NT, UN, [(0, place_ix(v, node_ix2)), (3, divide), (6, join)], chain, 5)

                @blk.scalar
                def _(a):
                    def evac(i, u):
                        a.wait_ge(c_T.sem, c_T.of(i, u))
                        a.wait_ge(c_mm.sem, c_mm.of(i - 1, u))
                        a.activation(hT[:, u, :], ps_T(u), ACT.Copy).then_inc(c_hT.sem, 1)
                    staged(a, NT, UN, [(0, evac)])

                @blk.tensor
                def _(pe):
                    def turn(i, u):
                        pe.wait_ge(c_h.sem, c_h.of(i, u))
                        pe.wait_ge(c_hT.sem, c_hT.of(i, prior(u, TURNED)))
                        for k in range(KC):
                            t = pe.transpose(ps_T(u)[:, k * P:(k + 1) * P], h[:, u, k * P:(k + 1) * P], ident[:, :])
                        t.then_inc(c_T.sem, 1)

                    def multiply(i, u):
                        pe.wait_ge(c_hT.sem, c_hT.of(i, u))
                        pe.wait_ge(c_out.sem, c_out.of(i, prior(u, PRODUCT)))
                        for k in range(KC):
                            m = pe.matmul(ps_small(u), hT[:, u, k * P:(k + 1) * P], w[:, k, :], start=(k == 0), stop=(k == KC - 1))
                        m.then_inc(c_mm.sem, 1)
                    staged(pe, NT, UN, [(0, turn), (1, multiply)])

                @blk.sync
                def _(sp):
                    def store(i, u):
                        sp.wait_ge(c_out.sem, c_out.of(i, u))
                        if isinstance(i, int) and i * UN + u == NT - 1:
                            sp.dma_start(out[(NT - 1) * P:N, :], o[0:TAIL, u, :]).then_inc(s_st[u].sem, 16)
                        else:
                            sp.dma_start(out[bass.ds((i * UN + u) * P, P), :], o[:, u, :]).then_inc(s_st[u].sem, 16)
                    staged(sp, NT, UN, [(UN, store)])
                    for u in range(UN):
                        sp.wait_ge(s_st[u].sem, s_st[u].base + NT // UN * 16)

        load_base = [loads * 16]

        def load(pairs):
            with block() as blk:
                @blk.sync
                def _(sp):
                    for dest, source in pairs:
                        sp.dma_start(dest, source).then_inc(s_load, 16)
                        load_base[0] += 16
                    sp.wait_ge(s_load, load_base[0])

        def chunks(w):
            return w.rearrange("(k p) n -> p k n", p=P)

        with scope() as l0:
            def mat(name):
                return sb(l0, name, [P, KC, D])

            def vec(name):
                return sb(l0, name, [P, D])
            U = sb(l0, "U", [P, NT, D])
            w_p1, w_m1a, w_m1b, w_m2a, w_m2b, w_m3a, w_m3b = (mat(n) for n in ("w_p1", "w_m1a", "w_m1b", "w_m2a", "w_m2b",
                                                                            "w_m3a", "w_m3b"))
            v_p1, v_m1, v_g2, v_b2, v_g3, v_b3 = (vec(n) for n in ("v_p1", "v_m1", "v_g2", "v_b2", "v_g3", "v_b3"))
            r_m2, r_m3 = sb(l0, "r_m2", [1, D]), sb(l0, "r_m3", [1, D])
            load([(w_p1[:, :, :], chunks(wp1)), (w_m1a[:, :, :], chunks(wm1[0:D, :])), (w_m1b[:, :, :], chunks(wm1[D:2 * D, :])),
                  (w_m2a[:, :, :], chunks(wm2[0:D, :])), (w_m2b[:, :, :], chunks(wm2[D:2 * D, :])),
                  (w_m3a[:, :, :], chunks(wm3[0:D, :])), (w_m3b[:, :, :], chunks(wm3[D:2 * D, :])),
                  (v_p1[:, :], rows(bp1)), (v_m1[:, :], rows(bm1)), (v_g2[:, :], rows(g2)), (v_b2[:, :], rows(b2)),
                  (v_g3[:, :], rows(g3)), (v_b3[:, :], rows(b3)), (r_m2[:, :], rows(bm2, 1)), (r_m3[:, :], rows(bm3, 1))])

            with scope() as t:
                o = ring(t, "o")

                def emit1(v, i, u):
                    chain.inc(v.tensor_tensor(U[:, i * UN + u, :], ps_small(u), v_m1[:, :], ALU.add))
                    chain.link(v.tensor_tensor(o[:, u, :], ps_wide(u)[:, 0:D], v_p1[:, :], ALU.add))
                    chain.link(v.tensor_scalar(o[:, u, :], o[:, u, :], 0.0, None, ALU.max))

                def store1(sp, i, u):
                    sp.dma_start(tab_t[bass.ds(i * UN + u, 1), :, :].rearrange("a p f -> p (a f)"), o[:, u, :]).then_inc(s_st[u].sem, 16)
                project([(lambda k: w_m1a[:, k, :], ps_small), (lambda k: w_p1[:, k, :], lambda u: ps_wide(u)[:, 0:D])],
                        emit1, 1, store1, 3)

            with scope() as g:
                G = [sb(g, f"G{b}", [P, J, D]) for b in range(UB)]
                edge_marks(dst_ix)
                with scope() as c:
                    degrees = Degrees(c)
                    max_pass(G, degrees)
                    find_rows(degrees.cnt)
                carry_max(G)
                combine(U, w_m1b, None, None, (w_m2a, r_m2))
                place = sb(g, "place", [P, CH])
                with scope() as c:
                    max_pass(G, Ranks(c, place))
                carry_max(G)
                combine(U, w_m2b, v_g2, v_b2, (w_m3a, r_m3))
                with scope() as c:
                    max_pass(G, Permute(c, place))
                carry_max(G)
                combine(U, w_m3b, v_g3, v_b3, None)
        sources_in_order()
        edge_marks(src_ix)

        with scope() as l1:
            w_q, w_o = sb(l1, "w_q", [P, KC, D]), sb(l1, "w_o", [P, KC, D])
            w_kv = sb(l1, "w_kv", [P, KC, 2 * D])
            v_q, v_o, v_kv = sb(l1, "v_q", [P, D]), sb(l1, "v_o", [P, D]), sb(l1, "v_kv", [P, 2 * D])
            load([(w_q[:, :, :], chunks(wq)), (w_o[:, :, :], chunks(wo)), (w_kv[:, :, 0:D], chunks(wk)), (w_kv[:, :, D:2 * D], chunks(wv)),
                  (v_q[:, :], rows(bq)), (v_o[:, :], rows(bo)), (v_kv[:, 0:D], rows(bk)), (v_kv[:, D:2 * D], rows(bv))])
            with scope() as t:
                okv, o = ring(t, "okv", KV), ring(t, "o")
                SC = float(HD) ** -0.5
                with block() as blk:
                    @blk.vector
                    def _(v):
                        chain.inc(v.memset(okv[:, :, 2 * D:KV], 1.0))
                        chain.link(v.tensor_scalar(v_q[:, :], v_q[:, :], SC, None, ALU.mult))

                def emit2(v, i, u):
                    chain.inc(v.tensor_tensor(okv[:, u, 0:2 * D], ps_wide(u), v_kv[:, :], ALU.add))
                    chain.link(v.scalar_tensor_tensor(out=o[:, u, :], in0=ps_small(u), scalar=SC, in1=v_q[:, :], op0=ALU.mult, op1=ALU.add))

                def store2(sp, i, u):
                    sp.dma_start(qtab_t[bass.ds(i * UN + u, 1), :, :].rearrange("a p f -> p (a f)"), o[:, u, :]).then_inc(s_st[u].sem, 16)
                    sp.dma_start(kvtab_t[bass.ds(i * UN + u, 1), :, :].rearrange("a p f -> p (a f)"), okv[:, u, :]).then_inc(s_st[u].sem, 16)
                project([(lambda k: w_q[:, k, :], ps_small), (lambda k: w_kv[:, k, :], ps_wide)], emit2, 2, store2, 2)
            with scope() as a:
                KVb = [sb(a, f"KV{b}", [P, J, ROW]) for b in range(UB)]
                with scope() as q:
                    Qb = [sb(q, f"Q{b}", [P, J, D]) for b in range(UB)]
                    s, w, tmp = sb(q, "s", [P, J, HEADS]), sb(q, "w", [P, 2, J, HEADS]), sb(q, "tmp", [P, ACC])
                    attention_pass(KVb, Qb, s, w, tmp)
                carry_attention(KVb)
            finish(w_o, v_o)


_INS = [("x", "x"), ("src", "src"), ("dst", "dst"), ("wp1", "L0_gnn_Wp1"), ("bp1", "L0_gnn_bp1"), ("wm1", "L0_gnn_Wm1"),
        ("bm1", "L0_gnn_bm1"), ("wm2", "L0_gnn_Wm2"), ("bm2", "L0_gnn_bm2"), ("wm3", "L0_gnn_Wm3"), ("bm3", "L0_gnn_bm3"),
        ("g2", "L0_gnn_ln2_g"), ("b2", "L0_gnn_ln2_b"), ("g3", "L0_gnn_ln3_g"), ("b3", "L0_gnn_ln3_b"),
        ("wq", "L1_gnn_Wq"), ("bq", "L1_gnn_bq"), ("wk", "L1_gnn_Wk"), ("bk", "L1_gnn_bk"), ("wv", "L1_gnn_Wv"),
        ("bv", "L1_gnn_bv"), ("wo", "L1_gnn_Wo"), ("bo", "L1_gnn_bo")]
_TRANSPOSED = ("wp1", "wm1", "wm2", "wm3")


def kernel(**inputs):
    import numpy as np
    import concourse.bacc as bacc
    from concourse.bass_utils import run_bass_kernel_spmd

    nc = bacc.Bacc("TRN2", target_bir_lowering=False, num_devices=1)
    arrays, args = {}, {}
    for short, name in _INS:
        a = np.asarray(inputs[name])
        a = np.ascontiguousarray(a.T if short in _TRANSPOSED else a)
        arrays[f"in_{short}"] = a
        args[short] = nc.dram_tensor(f"in_{short}", a.shape, mybir.dt.from_np(a.dtype), kind="ExternalInput").ap()
    n, d = inputs["x"].shape
    out = nc.dram_tensor("out_0", (n, d), F32, kind="ExternalOutput").ap()
    gnn_kernel(nc, out=out, **args)
    r = run_bass_kernel_spmd(nc, [arrays], core_ids=[0])
    return r.results[0]["out_0"]
```

```python
from contextlib import ExitStack, contextmanager

import concourse.bass as bass
from concourse import mybir

F32, BF16, I32, I16 = mybir.dt.float32, mybir.dt.bfloat16, mybir.dt.int32, mybir.dt.int16
ALU, ACT, AX = mybir.AluOpType, mybir.ActivationFunctionType, mybir.AxisListType

P = 128
D = 256
KC = D // P
HEADS = 8
HD = D // HEADS
EPS = 1e-5
NEG = -1e30
FAR = 1_000_000.0
ACC = D + HEADS
KV = D + ACC
STATE = ACC + HEADS
SLOT = 4
R = 3
UN = 7
J = 9
UB = 3


class Count:

    def __init__(self, sem, start=0):
        self.sem, self.base = sem, start

    def of(self, i, u, per=UN):
        return self.base + (i * per + (u + 1))

    def close(self, n):
        self.base += n


class Chain:

    def __init__(self, eng, sem):
        self.eng, self.sem, self.base, self.term = eng, sem, 0, 0

    def inc(self, ins):
        ins.then_inc(self.sem, 1)
        self.base += 1
        return self.base + self.term

    def link(self, ins):
        self.eng.wait_ge(self.sem, self.inc(ins))

    @contextmanager
    def body(self, i, per, times):
        start, self.term = self.base, i * per
        yield
        assert self.base - start == per, (self.base - start, per)
        self.base, self.term = start + per * times, 0


def staged(eng, steps, un, stages, chain=None, links=0):
    turns = steps // un
    assert turns * un == steps
    late = -(-max(delay for delay, _ in stages) // un)

    def turn(i, edge):
        for u in range(un):
            for delay, stage in stages:
                d, uu = divmod(u - delay, un)
                if edge and not 0 <= i * un + u - delay < steps:
                    continue
                stage(i + d, uu)

    first = 1 + late
    for i in range(first):
        turn(i, True)
    with eng.Fori(first, turns) as i:
        if chain is None:
            turn(i, False)
        else:
            with chain.body(i - first, links * un, turns - first):
                turn(i, False)
    for i in range(turns, turns + late):
        turn(i, True)


def gnn_kernel(nc, x, src, dst, wp1, bp1, wm1, bm1, wm2, bm2, wm3, bm3, g2, b2, g3, b3,
               wq, bq, wk, bk, wv, bv, wo, bo, out):
    N, E = x.shape[0], src.shape[0]
    NT = -(-N // P)
    NT = -(-NT // UN) * UN
    TAIL = N - (NT - 1) * P
    NB = -(-(-(-E // P)) // J)
    NB = -(-NB // UB) * UB
    CH = NB * J
    LASTE = E - (P - 1) * CH
    EMPTY = P * CH
    PAD = NT * P - 1
    RP = -(-(-(-(E + (SLOT - 1) * N) // SLOT)) // P)
    NBA = -(-(-(-RP // R)) // UB) * UB
    RP = NBA * R
    SL = RP * SLOT
    NOROW = P * RP
    assert 0 < TAIL < P and 0 < LASTE < CH and PAD >= N

    tab = nc.dram_tensor("tab", [NT * P, D], F32, kind="Internal").ap()
    hist = nc.dram_tensor("hist", [EMPTY + 1, D], F32, kind="Internal").ap()
    kvtab = nc.dram_tensor("kvtab", [NT * P, KV], F32, kind="Internal").ap()
    qtab = nc.dram_tensor("qtab", [NT * P, D], F32, kind="Internal").ap()
    ahist = nc.dram_tensor("ahist", [NOROW + 1, STATE], F32, kind="Internal").ap()
    tab_t = tab.rearrange("(t p) f -> t p f", p=P)
    kvtab_t = kvtab.rearrange("(t p) f -> t p f", p=P)
    qtab_t = qtab.rearrange("(t p) f -> t p f", p=P)
    hist_p = hist[0:EMPTY, :].rearrange("(p j) f -> p j f", p=P)
    ahist_p = ahist[0:NOROW, :].rearrange("(p j) f -> p j f", p=P)

    def rows(v, n=P):
        return bass.AP(tensor=v.tensor, offset=v.offset, ap=[[0, n], [1, v.shape[0]]])

    with ExitStack() as top:
        def scope():
            return ExitStack()

        names = {}

        def sb(stack, name, shape, dt=F32):
            names[name] = names.get(name, 0) + 1
            return stack.enter_context(nc.sbuf_tensor(f"{name}_{names[name]}", shape, dt))

        def sem(name):
            return top.enter_context(nc.semaphore(name))

        X = sb(top, "X", [P, NT, D])
        src_ix = sb(top, "src_ix", [P, CH + 2 * J], I32)
        dst_ix = sb(top, "dst_ix", [P, max(CH + 2 * J, SL + UB * R * SLOT)], I32)
        reset = sb(top, "reset", [P, CH])
        ident = sb(top, "ident", [P, P])
        node_ix = sb(top, "node_ix", [P, NT], I32)
        node_ix2 = sb(top, "node_ix2", [P, NT], I32)
        fix_ix = sb(top, "fix_ix", [P, 1], I32)
        Rrow = sb(top, "Rrow", [P, P])
        eps = sb(top, "eps", [P, 1])
        ix = sb(top, "ix", [P, UB, R * SLOT + R], I32)
        nix = sb(top, "nix", [P, UN], I32)
        stat = sb(top, "stat", [P, UN, 6])
        mv = sb(top, "mv", [P, UN, 2])
        sd = sb(top, "sd", [P, UN])
        rstd = sb(top, "rstd", [P, UN])
        nmr = sb(top, "nmr", [P, UN])
        rows_upto = sb(top, "rows_upto", [P, NT])
        rows_own = sb(top, "rows_own", [P, NT])
        bank = [top.enter_context(nc.psum_tensor(f"bank{n}", [P, 512], F32)) for n in range(8)]

        s_const = sem("s_const")
        const_base = [10]
        s_load = sem("s_load")
        s_misc = Count(sem("s_misc"))
        s_misc2 = Count(sem("s_misc2"))
        c_stat, c_sd, c_norm, c_h, c_T, c_hT, c_mm, c_y, c_z, c_out, c_ix = (
            Count(sem(n), UN) for n in ("c_stat", "c_sd", "c_norm", "c_h", "c_T", "c_hT", "c_mm", "c_y", "c_z",
                                    "c_out", "c_ix"))
        c_T2, c_hT2, c_mm2, c_keep = (Count(sem(n), UN) for n in ("c_T2", "c_hT2", "c_mm2", "c_keep"))
        counts = (c_stat, c_sd, c_norm, c_h, c_T, c_hT, c_mm, c_y, c_z, c_out, c_ix, c_T2, c_hT2, c_mm2, c_keep)
        s_gat = [Count(sem(f"s_gat{u}")) for u in range(UN)]
        s_cur = [Count(sem(f"s_cur{u}")) for u in range(UN)]
        s_st = [Count(sem(f"s_st{u}")) for u in range(UN)]
        s_eg = [Count(sem(f"s_eg{b}")) for b in range(UB)]
        s_hs = [Count(sem(f"s_hs{b}")) for b in range(UB)]
        c_eix, c_batch, c_w, c_e = (Count(sem(n)) for n in ("c_eix", "c_batch", "c_w", "c_e"))
        s_held = {"vector": sem("s_held_v"), "pool": sem("s_held_p")}
        s_pe = Count(sem("s_pe"))
        s_dve = Count(sem("s_dve"))
        chain = Chain(nc.vector, sem("chain"))

        def block():
            return nc.Block()

        def ring(stack, name, width=D):
            return sb(stack, name, [P, UN, width])

        def hold(eng, who, sem, value):
            eng.wait_ge(sem, value)
            eng.sem_inc(s_held[who], 1)

        TURNED = (0, 1, 0, 1, 0, 1, 0)
        PRODUCT = (0, 1, 2, 0, 1, 2, 1)

        def prior(u, ring):
            return next(v for v in range(u - 1, u - UN - 1, -1) if ring[v % UN] == ring[u])

        def ps_T(u):
            return bank[TURNED[u]][:, 0:D]

        def ps_small(u):
            return bank[2 + 2 * PRODUCT[u]][:, 0:D]

        def ps_wide(u):
            return bank[3 + 2 * PRODUCT[u]][:, :]

        ones = sb(top, "ones", [P, P])
        keys_of = {w: nc.dram_tensor(f"keys{w}", [P * w + 2], I32, kind="Internal").ap() for w in (CH, RP)}

        with scope() as st0:
            zrow = sb(st0, "zrow", [1, D + STATE])
            pad2 = sb(st0, "pad2", [1, 2], I32)
            with block() as blk:
                @blk.gpsimd
                def _(g):
                    g.memset(ident[:, :], 0.0).then_inc(s_const, 1)
                    g.memset(ones[:, :], 1.0).then_inc(s_const, 1)
                    g.memset(src_ix[:, :], PAD).then_inc(s_const, 1)
                    g.memset(dst_ix[:, :], PAD).then_inc(s_const, 1)
                    g.memset(pad2[:, :], PAD).then_inc(s_const, 1)
                    g.memset(X[:, NT - 1, :], 0.0).then_inc(s_const, 1)
                    g.memset(eps[:, :], EPS).then_inc(s_const, 1)
                    g.memset(zrow[:, :], 0.0).then_inc(s_const, 1)
                    g.wait_ge(s_const, 8)
                    g.memset(zrow[:, D + D:D + ACC], 1.0).then_inc(s_const, 1)
                    g.affine_select(out=ident[:, :], in_=ident[:, :], compare_op=ALU.not_equal, fill=1.0,
                                    base=0, pattern=[[-1, P]], channel_multiplier=1).then_inc(s_const, 1)

                @blk.sync
                def _(sp):
                    for c in counts:
                        sp.sem_inc(c.sem, UN)
                    sp.wait_ge(s_const, 10)
                    full = (P - 1) * CH
                    for dest, v in ((src_ix, src), (dst_ix, dst)):
                        sp.dma_start(dest[0:P - 1, 0:CH], v[0:full].rearrange("(p j) -> p j", j=CH)).then_inc(s_load, 16)
                        sp.dma_start(dest[P - 1:P, 0:LASTE], v[full:E].rearrange("(p j) -> p j", p=1)).then_inc(s_load, 16)
                    sp.dma_start(X[:, 0:NT - 1, :], x[0:(NT - 1) * P, :].rearrange("(t p) f -> p t f", p=P)).then_inc(s_load, 16)
                    sp.dma_start(X[0:TAIL, NT - 1, :], x[(NT - 1) * P:N, :]).then_inc(s_load, 16)
                    sp.dma_start(hist[EMPTY:EMPTY + 1, :], zrow[:, 0:D]).then_inc(s_load, 16)
                    sp.dma_start(ahist[NOROW:NOROW + 1, :], zrow[:, D:D + STATE]).then_inc(s_load, 16)
                    for w, keys in keys_of.items():
                        sp.dma_start(keys[0:1].rearrange("(a b) -> a b", a=1), pad2[:, 0:1]).then_inc(s_load, 16)
                        sp.dma_start(keys[P * w + 1:P * w + 2].rearrange("(a b) -> a b", a=1), pad2[:, 1:2]).then_inc(s_load, 16)
                    sp.wait_ge(s_load, 16 * 12)
            loads = 12

        def edge_marks(order, CH):
            keys = keys_of[CH]
            with scope() as st, block() as blk:
                near = sb(st, "near", [P, CH + 2], I32)
                nearf = sb(st, "nearf", [P, CH + 2])
                jp = sb(st, "jp", [P, CH])
                jpi = sb(st, "jpi", [P, CH], I32)
                neq = sb(st, "neq", [P, CH + 1])
                first_i = sb(st, "first_i", [P, 1], I32)
                firstf = sb(st, "firstf", [P, 1])
                end = sb(st, "end", [P, 1])
                flag = sb(st, "flag", [P, 1])
                flagw = sb(st, "flagw", [P, P])
                const0, m0 = const_base[0], s_misc2.base
                const_base[0] += 2

                @blk.gpsimd
                def _(g):
                    g.iota(jpi[:, :], [[1, CH]], base=0, channel_multiplier=0).then_inc(s_const, 1)
                    g.iota(first_i[:, :], [[0, 1]], base=0, channel_multiplier=CH).then_inc(s_const, 1)

                @blk.sync
                def _(sp):
                    sp.dma_start(keys[1:P * CH + 1].rearrange("(p j) -> p j", j=CH), order[:, 0:CH]).then_inc(s_misc2.sem, 16)
                    sp.wait_ge(s_misc2.sem, m0 + 16)
                    sp.dma_start(near[:, :], bass.AP(tensor=keys.tensor, offset=keys.offset, ap=[[CH, P], [1, CH + 2]])).then_inc(s_misc2.sem, 16)

                @blk.vector
                def _(v):
                    v.wait_ge(s_const, const0 + 2)
                    chain.link(v.tensor_copy(jp[:, :], jpi[:, :]))
                    chain.link(v.tensor_copy(firstf[:, :], first_i[:, :]))
                    v.wait_ge(s_misc2.sem, m0 + 32)
                    chain.link(v.tensor_copy(nearf[:, :], near[:, :]))
                    chain.link(v.tensor_tensor(neq[:, :], nearf[:, 0:CH + 1], nearf[:, 1:CH + 2], ALU.not_equal))
                    chain.link(v.tensor_scalar(reset[:, 0:CH], neq[:, 0:CH], NEG, None, ALU.mult))
                    chain.link(v.memset(reset[:, 0:1], NEG))
                    chain.link(v.tensor_scalar(jp[:, :], jp[:, :], FAR, None, ALU.add))
                    chain.link(v.scalar_tensor_tensor(out=jp[:, :], in0=neq[:, 1:CH + 1], scalar=-FAR, in1=jp[:, :],
                                                      op0=ALU.mult, op1=ALU.add))
                    chain.link(v.tensor_reduce(end[:, :], jp[:, :], AX.X, ALU.min))
                    chain.link(v.scalar_tensor_tensor(out=end[:, :], in0=neq[:, 0:1], scalar=FAR,
                                                      in1=end[:, :], op0=ALU.mult, op1=ALU.add))
                    chain.link(v.tensor_tensor(end[:, :], end[:, :], firstf[:, :], ALU.add))
                    chain.link(v.tensor_copy(fix_ix[:, :], end[:, :]))
                    chain.link(v.tensor_tensor(flag[:, :], nearf[:, 1:2], nearf[:, CH:CH + 1], ALU.not_equal))
                    chain.link(v.tensor_tensor(flag[:, :], flag[:, :], neq[:, 0:1], ALU.max))
                    chain.link(v.tensor_scalar(flagw[:, :], ones[:, :], flag[:, 0:1], None, ALU.mult))
                    v.sem_inc(s_dve.sem, 1)
                    v.wait_ge(s_pe.sem, s_pe.base + 1)
                    chain.link(v.tensor_scalar(Rrow[:, :], bank[0][:, 0:P], NEG, None, ALU.mult))

                @blk.tensor
                def _(pe):
                    pe.wait_ge(s_dve.sem, s_dve.base + 1)
                    pe.matmul(bank[0][:, 0:P], flagw[:, :], ident[:, :], start=True, stop=True).then_inc(s_pe.sem, 1)
            s_dve.close(1)
            s_pe.close(1)
            s_misc2.close(32)

        def norm_stages(v, a, of_y):
            def stats(i, u):
                hold(v, "vector", chain.sem, chain.inc(v.bn_stats(stat[:, u, :], of_y(i, u))))
                chain.inc(v.bn_aggr(mv[:, u, :], stat[:, u, :]))
                v.wait_ge(chain.sem, chain.base + chain.term)
                v.sem_inc(c_stat.sem, 1)

            def recip(i, u):
                v.wait_ge(c_sd.sem, c_sd.of(i, u))
                chain.link(v.reciprocal(rstd[:, u:u + 1], sd[:, u:u + 1]))
                chain.link(v.scalar_tensor_tensor(out=nmr[:, u:u + 1], in0=mv[:, u, 0:1], scalar=-1.0,
                                                  in1=rstd[:, u:u + 1], op0=ALU.mult, op1=ALU.mult))
                v.sem_inc(c_norm.sem, 1)

            def sqrt(i, u):
                a.wait_ge(c_stat.sem, c_stat.of(i, u))
                a.activation(sd[:, u:u + 1], mv[:, u, 1:2], ACT.Sqrt, bias=eps[:, 0:1]).then_inc(c_sd.sem, 1)
            return stats, recip, sqrt

        def project(weights, emit, stores, store_sp, per_out):
            with scope() as st, block() as blk:
                h, hT = ring(st, "h"), ring(st, "hT")
                @blk.vector
                def _(v):
                    stats, recip, _ = norm_stages(v, None, lambda i, u: X[:, i * UN + u, :])

                    def finish(i, u):
                        v.wait_ge(c_mm.sem, c_mm.of(i, u))
                        if stores:
                            v.wait_ge(s_st[u].sem, s_st[u].base + i * 16 * stores)
                        emit(v, i, u)
                        v.sem_inc(c_out.sem, 1)
                    staged(v, NT, UN, [(0, stats), (1, recip), (4, finish)], chain, 4 + per_out)

                @blk.scalar
                def _(a):
                    _, _, sqrt = norm_stages(None, a, None)

                    def relu(i, u):
                        a.wait_ge(c_norm.sem, c_norm.of(i, u))
                        a.wait_ge(c_T.sem, c_T.of(i - 1, u))
                        a.activation(h[:, u, :], X[:, i * UN + u, :], ACT.Relu, bias=nmr[:, u:u + 1],
                                     scale=rstd[:, u:u + 1]).then_inc(c_h.sem, 1)

                    def evac(i, u):
                        a.wait_ge(c_T.sem, c_T.of(i, u))
                        a.wait_ge(c_mm.sem, c_mm.of(i - 1, u))
                        a.activation(hT[:, u, :], ps_T(u), ACT.Copy).then_inc(c_hT.sem, 1)
                    staged(a, NT, UN, [(0, sqrt), (2, relu), (3, evac)])

                @blk.tensor
                def _(pe):
                    def turn(i, u):
                        pe.wait_ge(c_h.sem, c_h.of(i, u))
                        pe.wait_ge(c_hT.sem, c_hT.of(i, prior(u, TURNED)))
                        for k in range(KC):
                            t = pe.transpose(ps_T(u)[:, k * P:(k + 1) * P], h[:, u, k * P:(k + 1) * P], ident[:, :])
                        t.then_inc(c_T.sem, 1)

                    def multiply(i, u):
                        pe.wait_ge(c_hT.sem, c_hT.of(i, u))
                        pe.wait_ge(c_out.sem, c_out.of(i, prior(u, PRODUCT)))
                        for w, place in weights:
                            for k in range(KC):
                                m = pe.matmul(place(u), hT[:, u, k * P:(k + 1) * P], w(k), start=(k == 0), stop=(k == KC - 1))
                        m.then_inc(c_mm.sem, 1)
                    staged(pe, NT, UN, [(0, turn), (1, multiply)])

                if stores:
                    @blk.sync
                    def _(sp):
                        def store(i, u):
                            sp.wait_ge(c_out.sem, c_out.of(i, u))
                            store_sp(sp, i, u)
                        staged(sp, NT, UN, [(0, store)])
                        for u in range(UN):
                            sp.wait_ge(s_st[u].sem, s_st[u].base + (NT // UN) * 16 * stores)
            for c in (c_stat, c_sd, c_norm, c_h, c_T, c_hT, c_mm, c_out):
                c.close(NT)
            for c in s_st:
                c.close((NT // UN) * 16 * stores)

        def max_pass(G, side):
            with block() as blk:
                @blk.gpsimd
                def _(g):
                    def gather(i, b):
                        hold(g, "pool", c_eix.sem, c_eix.of(i, b, UB))
                        hold(g, "pool", s_hs[b].sem, s_hs[b].base + i * 16)
                        for k in range(J):
                            g.indirect_dma_start(G[b][:, k, :], None, tab, bass.IndirectOffsetOnAxis(ix[:, b, k:k + 1], 0),
                                                 bounds_check=NT * P - 1, oob_is_err=False).then_inc(s_eg[b].sem, 16)
                    staged(g, NB, UB, [(0, gather)])

                @blk.vector
                def _(v):
                    chain.link(v.memset(G[UB - 1][:, J - 1, :], 0.0))
                    for m in range(2):
                        v.tensor_copy(ix[:, m, 0:J], src_ix[:, m * J:(m + 1) * J]).then_inc(c_eix.sem, 1)
                    done = [0]

                    def fold(k):
                        def stage(i, b):
                            n = i * UB + b
                            if k == 0:
                                v.wait_ge(s_eg[b].sem, s_eg[b].base + (i * (16 * J) + 16 * J))
                                if not is_first(i, b):
                                    v.wait_ge(c_batch.sem, c_batch.of(i, b - 1, UB))
                            before = G[b][:, k - 1, :] if k else G[(b - 1) % UB][:, J - 1, :]
                            ins = v.scalar_tensor_tensor(out=G[b][:, k, :], in0=before, scalar=reset[:, bass.ds(n * J + k, 1)],
                                                         in1=G[b][:, k, :], op0=ALU.add, op1=ALU.max)
                            if k == J - 1:
                                ins.then_inc(c_batch.sem, 1)
                            else:
                                done[0] = chain.inc(ins)
                        return stage

                    def folded(k):
                        def stage(i, b):
                            if k < J - 1:
                                v.wait_ge(chain.sem, done[0])
                            if k == 0:
                                v.tensor_copy(ix[:, (b + 2) % UB, 0:J], src_ix[:, bass.ds((i * UB + b) * J + 2 * J, J)]).then_inc(c_eix.sem, 1)
                        return stage
                    fillers = side.vector(v)
                    stages = []
                    for k in range(J):
                        stages += [(0, fold(k))] + fillers.get(k, []) + [(0, folded(k))]
                    staged(v, NB, UB, stages, chain, J - 1 + side.links)

                @blk.sync
                def _(sp):
                    def store(i, b):
                        sp.wait_ge(c_batch.sem, c_batch.of(i, b, UB))
                        sp.dma_start(hist_p[:, bass.ds((i * UB + b) * J, J), :], G[b][:, :, :]).then_inc(s_hs[b].sem, 16)
                    staged(sp, NB, UB, [(0, store)])
                    for b in range(UB):
                        sp.wait_ge(s_hs[b].sem, s_hs[b].base + (NB // UB) * 16)

                @blk.tensor
                def _(pe):
                    staged(pe, NB, UB, side.tensor(pe))

                if side.scalar is not None:
                    @blk.scalar
                    def _(a):
                        staged(a, NB, UB, side.scalar(a))
            c_eix.close(NB + 2)
            c_batch.close(NB)
            for b in range(UB):
                s_eg[b].close(NB // UB * 16 * J)
                s_hs[b].close(NB // UB * 16)
            side.close()

        def is_first(i, b, k=0, first=1):
            return isinstance(i, int) and i * UB + b < first and k == 0

        def times(i, b, per, k=None):
            return i * (UB * per) + (b * per + (per if k is None else k))

        def spread_key(v, key, n, width):
            return key[:, bass.ds(n * J, J)][:, :, None].to_broadcast([P, J, width])

        def split_keys(v, key_ix, ti, lo, hi):
            chain.link(v.tensor_scalar(ti[:, :], key_ix[:, 0:CH], P - 1, None, ALU.bitwise_and))
            chain.link(v.tensor_copy(lo[:, :], ti[:, :]))
            chain.link(v.tensor_scalar(ti[:, :], key_ix[:, 0:CH], P.bit_length() - 1, None, ALU.logical_shift_right))
            chain.link(v.tensor_copy(hi[:, :], ti[:, :]))

        class Degrees:
            links = 0

            def __init__(self, st):
                self.cnt = [sb(st, "cnt", [P, NT]) for _ in range(2)]
                self.low = [sb(st, "low", [P, J, P], BF16) for _ in range(2)]
                self.high = [sb(st, "high", [P, J, NT], BF16) for _ in range(2)]
                self.iota = sb(st, "iota", [P, P], BF16)
                self.lo = [sb(st, "lo", [P, CH], BF16) for _ in range(2)]
                self.hi = [sb(st, "hi", [P, CH], BF16) for _ in range(2)]
                self.oh, self.mm, self.added = sem("deg_oh"), sem("deg_mm"), sem("deg_added")
                self.ti = sb(st, "ti", [P, CH], I32)
                const0 = const_base[0]
                const_base[0] += 1
                with block() as blk:
                    @blk.gpsimd
                    def _(g):
                        g.iota(self.ti[:, 0:P], [[1, P]], base=0, channel_multiplier=0).then_inc(s_const, 1)

                    @blk.vector
                    def _(v):
                        v.wait_ge(s_const, const0 + 1)
                        chain.link(v.tensor_copy(self.iota[:, :], self.ti[:, 0:P]))
                        for k, key in enumerate((dst_ix, src_ix)):
                            chain.inc(v.memset(self.cnt[k][:, :], 0.0))
                            split_keys(v, key, self.ti, self.lo[k], self.hi[k])

            def vector(self, v):
                def add(i, b):
                    v.wait_ge(self.mm, times(i, b, 1))
                    for k in range(2):
                        v.tensor_tensor(self.cnt[k][:, :], bank[k][:, 0:NT], self.cnt[k][:, :], ALU.add).then_inc(self.added, 1)

                def make_low(k):
                    return lambda i, b: v.tensor_tensor(self.low[k][:, :, :], self.iota[:, None, :].to_broadcast([P, J, P]),
                                                        spread_key(v, self.lo[k], i * UB + b, P), ALU.is_equal).then_inc(self.oh, 1)

                def make_high(k):
                    return lambda i, b: v.tensor_tensor(self.high[k][:, :, :], self.iota[:, None, 0:NT].to_broadcast([P, J, NT]),
                                                        spread_key(v, self.hi[k], i * UB + b, NT), ALU.is_equal).then_inc(self.oh, 1)
                return {2: [(1, add)], 3: [(0, make_low(0))], 4: [(0, make_high(0))], 5: [(0, make_low(1))], 6: [(0, make_high(1))]}

            def tensor(self, pe):
                def count(i, b):
                    pe.wait_ge(self.oh, times(i, b, 4))
                    if not is_first(i, b):
                        pe.wait_ge(self.added, times(i, b - 1, 2))
                    for n in range(2):
                        for k in range(J):
                            m = pe.matmul(bank[n][:, 0:NT], self.low[n][:, k, :], self.high[n][:, k, :], start=(k == 0), stop=(k == J - 1))
                    m.then_inc(self.mm, 1)
                return [(0, count)]

            scalar = None

            def close(self):
                pass

        class Ranks:
            links = 1

            def __init__(self, st, place):
                self.place = place
                self.low = [sb(st, "low", [P, J, P], BF16) for _ in range(UB)]
                self.high = [sb(st, "high", [P, J, NT], BF16) for _ in range(UB)]
                self.lowT = [sb(st, "lowT", [P, J, P]) for _ in range(UB)]
                self.lowTb = sb(st, "lowTb", [P, J, P], BF16)
                self.same = sb(st, "same", [P, J, P], BF16)
                self.next = [sb(st, "next", [P, J + 1, NT]) for _ in range(UB)]
                self.first = sb(st, "first", [P, NT])
                self.iota = sb(st, "iota", [P, P], BF16)
                self.identb = sb(st, "identb", [P, P], BF16)
                self.upper = sb(st, "upper", [P, P])
                self.pick = sb(st, "pick", [P, J, NT])
                self.lo, self.hi = sb(st, "lo", [P, CH], BF16), sb(st, "hi", [P, CH], BF16)
                self.c = {n: sem("rank_" + n) for n in ("oh", "turn", "lowT", "pair", "same", "count", "next", "sum", "place")}
                const0 = const_base[0]
                const_base[0] += 2
                with scope() as t, block() as blk:
                    ti = sb(t, "ti", [P, CH], I32)

                    @blk.gpsimd
                    def _(g):
                        g.iota(ti[:, 0:P], [[1, P]], base=0, channel_multiplier=0).then_inc(s_const, 1)
                        g.affine_select(out=self.upper[:, :], in_=ones[:, :], compare_op=ALU.is_gt, fill=0.0, base=0,
                                        pattern=[[1, P]], channel_multiplier=-1).then_inc(s_const, 1)

                    @blk.vector
                    def _(v):
                        v.wait_ge(s_const, const0 + 2)
                        chain.link(v.tensor_copy(self.iota[:, :], ti[:, 0:P]))
                        chain.link(v.tensor_copy(self.identb[:, :], ident[:, :]))
                        chain.link(v.tensor_tensor(self.first[:, :], rows_upto[:, :], rows_own[:, :], ALU.subtract))
                        chain.link(v.tensor_scalar(self.first[:, :], self.first[:, :], float(SLOT), None, ALU.mult))
                        split_keys(v, src_ix, ti, self.lo, self.hi)

            def vector(self, v):
                c = self.c

                def make_low(i, b):
                    v.tensor_tensor(self.low[b][:, :, :], self.iota[:, None, :].to_broadcast([P, J, P]),
                                    spread_key(v, self.lo, i * UB + b, P), ALU.is_equal).then_inc(c["oh"], 1)

                def make_high(i, b):
                    v.tensor_tensor(self.high[b][:, :, :], self.iota[:, None, 0:NT].to_broadcast([P, J, NT]),
                                    spread_key(v, self.hi, i * UB + b, NT), ALU.is_equal).then_inc(c["oh"], 1)

                def mask(q):
                    def stage(i, b):
                        k, n = 4 * q, min(4, J - 4 * q)
                        if q == 0:
                            v.wait_ge(c["pair"], times(i, b, 1))
                        v.tensor_tensor(self.same[:, k:k + n, :], bank[2 + q][:, 0:n * P].rearrange("p (k e) -> p k e", e=P),
                                        self.upper[:, None, :].to_broadcast([P, n, P]), ALU.mult).then_inc(c["same"], 1)
                    return stage

                picked = [0]

                def choose(i, b):
                    v.wait_ge(c["sum"], times(i, b, 1))
                    picked[0] = chain.inc(v.tensor_tensor(self.pick[:, :, :], bank[5][:, 0:J * NT].rearrange("p (k t) -> p k t", t=NT),
                                              self.high[b][:, :, :], ALU.mult))

                def chosen(i, b):
                    v.wait_ge(chain.sem, picked[0])
                    v.tensor_reduce(self.place[:, bass.ds((i * UB + b) * J, J)], self.pick[:, :, :], AX.X, ALU.add).then_inc(c["place"], 1)
                return {0: [(3, choose)], 1: [(0, make_low)], 2: [(3, chosen)], 3: [(0, make_high)],
                        4: [(2, mask(0))], 5: [(2, mask(1))], 6: [(2, mask(2))]}

            def scalar(self, a):
                c = self.c

                def copy_low(i, b):
                    a.wait_ge(c["turn"], times(i, b, 1))
                    if not is_first(i, b):
                        a.wait_ge(c["pair"], times(i, b - 1, 1))
                    for to in (self.lowTb, self.lowT[b]):
                        for k in range(0, J, 8):
                            n = min(8, J - k)
                            m = a.activation(to[:, k:k + n, :], self.bf(k // 8)[:, 0:n * P].rearrange("p (k e) -> p k e", e=P), ACT.Copy)
                            m.then_inc(c["lowT"], 1)

                def copy_next(i, b):
                    a.wait_ge(c["count"], times(i, b, 1))
                    a.activation(self.next[b][:, :, :], bank[6][:, 0:(J + 1) * NT].rearrange("p (k t) -> p k t", t=NT), ACT.Copy).then_inc(c["next"], 1)
                return [(0, copy_next), (0, copy_low)]

            def bf(self, n):
                return bank[n][:, :].bitcast(BF16)

            def tensor(self, pe):
                c = self.c

                def count(i, b):
                    pe.wait_ge(c["oh"], times(i, b, 2))
                    before = self.first[:, :]
                    if not is_first(i, b):
                        pe.wait_ge(c["next"], times(i, b - 1, 1))
                        before = self.next[(b - 1) % UB][:, J, :]
                    pe.matmul(bank[6][:, 0:(J + 1) * NT], ident[:, :], before[:, None, :].to_broadcast([P, J + 1, NT]), start=True, stop=False,
                              skip_group_check=True)
                    for k in range(J):
                        m = pe.matmul(bank[6][:, (k + 1) * NT:(J + 1) * NT], self.low[b][:, k, :],
                                      self.high[b][:, k:k + 1, :].to_broadcast([P, J - k, NT]), start=False, stop=(k == J - 1),
                                      skip_group_check=True)
                    m.then_inc(c["count"], 1)

                def turn(i, b):
                    if not is_first(i, b):
                        pe.wait_ge(c["lowT"], times(i, b - 1, 4))
                    for k in range(J):
                        t = pe.transpose(self.bf(k // 8)[:, (k % 8) * P:(k % 8 + 1) * P], self.low[b][:, k, :], self.identb[:, :])
                    t.then_inc(c["turn"], 1)

                def pair(i, b):
                    pe.wait_ge(c["lowT"], times(i, b, 4))
                    if not is_first(i, b):
                        pe.wait_ge(c["same"], times(i, b - 1, 3))
                    for k in range(J):
                        t = pe.matmul(bank[2 + k // 4][:, (k % 4) * P:(k % 4 + 1) * P], self.lowTb[:, k, :], self.lowTb[:, k, :],
                                      start=True, stop=True)
                    t.then_inc(c["pair"], 1)

                def add_up(i, b):
                    pe.wait_ge(c["same"], times(i, b, 3))
                    pe.wait_ge(c["next"], times(i, b, 1))
                    if not is_first(i, b):
                        pe.wait_ge(c["place"], times(i, b - 1, 1))
                    for k in range(J):
                        to = bank[5][:, k * NT:(k + 1) * NT]
                        pe.matmul(to, self.same[:, k, :], self.high[b][:, k, :], start=True, stop=False)
                        m = pe.matmul(to, self.lowT[b][:, k, :], self.next[b][:, k, :], start=False, stop=True)
                    m.then_inc(c["sum"], 1)
                return [(0, count), (0, turn), (1, pair), (2, add_up)]

            def close(self):
                pass

        class Permute:
            links = 1
            RG = 3

            def __init__(self, st, place):
                self.row, self.lo, self.hi = (sb(st, n, [P, CH], BF16) for n in ("row", "lo", "hi"))
                self.off = sb(st, "off", [P, CH])
                self.iota = sb(st, "iota", [P, SL + 1])
                self.iotab = sb(st, "iotab", [P, P], BF16)
                self.rows_made, self.signs_made, self.mm = sem("perm_rows"), sem("perm_signs"), sem("perm_mm")
                self.cuts = ((0, 512), (512, SL + 1))
                const0 = const_base[0]
                const_base[0] += 1
                with scope() as t, block() as blk:
                    ti = sb(t, "ti", [P, SL + 1], I32)
                    tf, quot, rest = (sb(t, n, [P, CH]) for n in ("tf", "quot", "rest"))

                    @blk.gpsimd
                    def _(g):
                        g.iota(ti[:, :], [[1, SL + 1]], base=-1, channel_multiplier=0).then_inc(s_const, 1)

                    @blk.vector
                    def _(v):
                        v.wait_ge(s_const, const0 + 1)
                        chain.inc(v.tensor_copy(self.iotab[:, :], ti[:, 1:P + 1]))
                        chain.link(v.tensor_copy(self.iota[:, :], ti[:, :]))
                        split_keys(v, dst_ix, ti[:, 0:CH], self.lo, self.hi)
                        chain.link(v.tensor_scalar(self.lo[:, :], self.lo[:, :], 1.0, None, ALU.add))
                        divide(v, place[:, :], SL, quot[:, :], rest[:, :], ti[:, 0:CH], tf[:, :])
                        chain.link(v.tensor_copy(self.row[:, :], quot[:, :]))
                        chain.link(v.tensor_scalar(self.off[:, :], rest[:, :], -1.0, 0.5, ALU.mult, ALU.add))
                self.signs = sb(st, "signs", [P, self.RG, SL + 1], BF16)
                self.hot = sb(st, "hot", [P, J, P], BF16)
                self.vals = sb(st, "vals", [P, UB, 2, J, P], BF16)

            def vector(self, v):
                def make(i, b):
                    chain.inc(v.tensor_tensor(self.hot[:, :, :], self.iotab[:, None, :].to_broadcast([P, J, P]),
                                              spread_key(v, self.row, i * UB + b, P), ALU.is_equal))

                def value(m, key):
                    def stage(i, b):
                        if m == 0 and not is_first(i, b, 0, UB):
                            v.wait_ge(self.mm, times(i - 1, b, J))
                        v.tensor_tensor(self.vals[:, b, m, :, :], self.hot[:, :, :], spread_key(v, key, i * UB + b, P),
                                        ALU.mult).then_inc(self.rows_made, 1)
                    return stage
                return {0: [(0, make)], 2: [(0, value(0, self.lo))], 4: [(0, value(1, self.hi))]}

            def scalar(self, a):
                def sign(i, b):
                    for k in range(J):
                        r = k % self.RG
                        if not (is_first(i, b) and k < self.RG):
                            a.wait_ge(self.mm, times(i, b, J, k - self.RG + 1))
                        a.activation(self.signs[:, r, :], self.iota[:, :], ACT.Sign,
                                     bias=self.off[:, bass.ds((i * UB + b) * J + k, 1)]).then_inc(self.signs_made, 1)
                return [(0, sign)]

            def tensor(self, pe):
                def put(i, b):
                    pe.wait_ge(self.rows_made, times(i, b, 2))
                    for k in range(J):
                        r = k % self.RG
                        pe.wait_ge(self.signs_made, times(i, b, J, k + 1))
                        for m in range(2):
                            for half, (c0, c1) in enumerate(self.cuts):
                                t = pe.matmul(bank[2 * m + half][:, 0:c1 - c0], self.vals[:, b, m, k, :], self.signs[:, r, c0:c1],
                                              start=is_first(i, b, k), stop=True, skip_group_check=True)
                        t.then_inc(self.mm, 1)
                return [(0, put)]

            def close(self):
                total = self.iota
                with block() as blk:
                    @blk.vector
                    def _(v):
                        for half, (c0, c1) in enumerate(self.cuts):
                            chain.link(v.tensor_copy(total[:, c0:c1], bank[half][:, 0:c1 - c0]))
                            chain.link(v.scalar_tensor_tensor(out=total[:, c0:c1], in0=bank[2 + half][:, 0:c1 - c0], scalar=float(P),
                                                              in1=total[:, c0:c1], op0=ALU.mult, op1=ALU.add))
                        chain.link(v.tensor_scalar(total[:, :], total[:, :], 0.5, None, ALU.mult))
                        chain.link(v.tensor_tensor(dst_ix[:, 0:SL], total[:, 1:SL + 1], total[:, 0:SL], ALU.subtract))

        def divide(v, a, by, quot, rest, ti, tf):
            chain.link(v.tensor_scalar(tf, a, 1.0 / by, None, ALU.mult))
            chain.link(v.tensor_copy(ti, tf))
            chain.link(v.tensor_copy(quot, ti))
            chain.link(v.scalar_tensor_tensor(out=rest, in0=quot, scalar=-float(by), in1=a, op0=ALU.mult, op1=ALU.add))
            for op, bound, step in ((ALU.is_lt, 0.0, -1.0), (ALU.is_ge, float(by), 1.0)):
                chain.link(v.tensor_scalar(tf, rest, bound, step, op, ALU.mult))
                chain.link(v.tensor_tensor(quot, quot, tf, ALU.add))
                chain.link(v.scalar_tensor_tensor(out=rest, in0=tf, scalar=-float(by), in1=rest, op0=ALU.mult, op1=ALU.add))

        def nodes_of_rows(empty):
            with scope() as st:
                quot, rest = sb(st, "quot", [P, NT]), sb(st, "rest", [P, NT])
                row, col = sb(st, "row", [P, NT], BF16), sb(st, "col", [P, NT], BF16)
                iota = sb(st, "iota", [P, RP], BF16)
                eq, gt = sb(st, "eq", [P, NT, P], BF16), sb(st, "gt", [P, NT, P], BF16)
                ge = sb(st, "ge", [P, NT, RP], BF16)
                all1 = sb(st, "all1", [P, RP], BF16)
                node = sb(st, "node", [P, RP])
                ti = sb(st, "ti", [P, RP], I32)
                tf = sb(st, "tf", [P, NT])
                slot = sb(st, "slot", [P, SL])
                const0 = const_base[0]
                const_base[0] += 1
                with block() as blk:
                    @blk.gpsimd
                    def _(g):
                        g.iota(ti[:, :], [[1, RP]], base=0, channel_multiplier=0).then_inc(s_const, 1)

                    @blk.vector
                    def _(v):
                        v.wait_ge(s_const, const0 + 1)
                        chain.inc(v.memset(all1[:, :], 1.0))
                        chain.link(v.tensor_copy(iota[:, :], ti[:, :]))
                        divide(v, rows_upto[:, :], RP, quot[:, :], rest[:, :], ti[:, 0:NT], tf[:, :])
                        chain.inc(v.tensor_copy(row[:, :], quot[:, :]))
                        chain.link(v.tensor_copy(col[:, :], rest[:, :]))
                        for to, key, op, width in ((gt, row, ALU.is_gt, P), (eq, row, ALU.is_equal, P), (ge, col, ALU.is_ge, RP)):
                            chain.link(v.tensor_tensor(to[:, :, :], iota[:, None, 0:width].to_broadcast([P, NT, width]),
                                                       key[:, :, None].to_broadcast([P, NT, width]), op))
                        v.sem_inc(s_dve.sem, 1)
                        chain.link(v.tensor_copy(slot[:, :], dst_ix[:, 0:SL]))
                        chain.link(v.tensor_scalar(empty[:, :], slot[:, :], 0.0, NEG, ALU.is_equal, ALU.mult))
                        chain.link(v.tensor_scalar(slot[:, :], slot[:, :], -1.0, 0.0, ALU.add, ALU.max))
                        chain.link(v.tensor_copy(dst_ix[:, 0:SL], slot[:, :]))
                        v.wait_ge(s_pe.sem, s_pe.base + 1)
                        chain.link(v.tensor_scalar(node[:, :], bank[0][:, 0:RP], float(PAD), None, ALU.min))
                        chain.link(v.tensor_copy(src_ix[:, 0:RP], node[:, :]))

                    @blk.tensor
                    def _(pe):
                        pe.wait_ge(s_dve.sem, s_dve.base + 1)
                        for t in range(NT):
                            pe.matmul(bank[0][:, 0:RP], gt[:, t, :], all1[:, :], start=(t == 0), stop=False)
                            m = pe.matmul(bank[0][:, 0:RP], eq[:, t, :], ge[:, t, :], start=False, stop=(t == NT - 1))
                        m.then_inc(s_pe.sem, 1)
                s_dve.close(1)
                s_pe.close(1)

        def find_rows(degrees):
            by_dst, by_src = degrees.cnt
            with ExitStack() as st, block() as blk:
                upto = sb(st, "upto", [P, P])
                tot, cum, has = sb(st, "tot", [P, 2, NT]), sb(st, "cum", [P, 2, NT]), sb(st, "has", [P, NT])
                ti = sb(st, "ti", [P, NT], I32)
                const0 = const_base[0]
                const_base[0] += 1

                @blk.gpsimd
                def _(g):
                    g.affine_select(out=upto[:, :], in_=ones[:, :], compare_op=ALU.is_ge, fill=0.0, base=0,
                                    pattern=[[1, P]], channel_multiplier=-1).then_inc(s_const, 1)

                @blk.tensor
                def _(pe):
                    pe.wait_ge(s_const, const0 + 1)
                    pe.wait_ge(s_dve.sem, s_dve.base + 1)
                    for k, own in enumerate((by_dst, rows_own)):
                        pe.matmul(bank[2 * k][:, 0:NT], upto[:, :], own[:, :], start=True, stop=True)
                        m = pe.matmul(bank[2 * k + 1][:, 0:NT], ones[:, :], own[:, :], start=True, stop=True)
                    m.then_inc(s_pe.sem, 1)

                @blk.vector
                def _(v):
                    chain.link(v.tensor_scalar(ti[:, :], by_src[:, :], SLOT - 1.0, None, ALU.add))
                    chain.link(v.tensor_scalar(ti[:, :], ti[:, :], SLOT.bit_length() - 1, None, ALU.logical_shift_right))
                    chain.link(v.tensor_copy(rows_own[:, :], ti[:, :]))
                    v.sem_inc(s_dve.sem, 1)
                    v.wait_ge(s_pe.sem, s_pe.base + 1)
                    for k, (own, none, dest) in enumerate(((by_dst, EMPTY, node_ix), (rows_own, NOROW, node_ix2))):
                        c, t = cum[:, k, :], tot[:, k, :]
                        chain.link(v.tensor_copy(t, bank[2 * k + 1][:, 0:NT]))
                        chain.link(v.tensor_tensor_scan(c, ones[:, 0:NT], t, 0.0, ALU.mult, ALU.add))
                        chain.link(v.tensor_tensor(c, c, t, ALU.subtract))
                        chain.link(v.tensor_tensor(c, bank[2 * k][:, 0:NT], c, ALU.add))
                        if k:
                            chain.inc(v.tensor_copy(rows_upto[:, :], c))
                        chain.link(v.tensor_scalar(has[:, :], own[:, :], 0.0, None, ALU.is_gt))
                        chain.link(v.tensor_scalar(c, c, -1.0 - none, None, ALU.add))
                        chain.link(v.tensor_tensor(c, c, has[:, :], ALU.mult))
                        chain.link(v.tensor_scalar(c, c, float(none), float(none), ALU.add, ALU.min))
                        chain.link(v.tensor_copy(dest[:, :], c))
            s_dve.close(1)
            s_pe.close(1)

        def carry_max(G):
            last = G[UB - 1][:, J - 1, :]
            with ExitStack() as st, block() as blk:
                scanned = sb(st, "scanned", [P, KC, P])
                found = sb(st, "found", [P, D])
                m0 = s_misc.base

                @blk.tensor
                def _(pe):
                    for k in range(KC):
                        t = pe.transpose(bank[0][:, k * P:(k + 1) * P], last[:, k * P:(k + 1) * P], ident[:, :])
                    t.then_inc(s_pe.sem, 1)
                    pe.wait_ge(s_dve.sem, s_dve.base + 2)
                    for k in range(KC):
                        t = pe.transpose(bank[1][:, k * P:(k + 1) * P], scanned[:, k, :], ident[:, :])
                    t.then_inc(s_pe.sem, 1)

                @blk.vector
                def _(v):
                    chain.link(v.memset(found[:, :], 0.0))
                    v.sem_inc(s_dve.sem, 1)
                    chain.link(v.memset(scanned[:, :, 0:1], NEG))
                    v.wait_ge(s_pe.sem, s_pe.base + 1)
                    for k in range(KC):
                        chain.link(v.tensor_tensor_scan(scanned[:, k, 1:P], Rrow[:, 0:P - 1], bank[0][:, k * P:(k + 1) * P - 1],
                                                        NEG, ALU.add, ALU.max))
                    v.sem_inc(s_dve.sem, 1)
                    v.wait_ge(s_pe.sem, s_pe.base + 2)
                    v.wait_ge(s_misc.sem, m0 + 16)
                    chain.link(v.tensor_tensor(found[:, :], bank[1][:, 0:D], found[:, :], ALU.max))
                    v.sem_inc(s_dve.sem, 1)

                @blk.gpsimd
                def _(g):
                    g.wait_ge(s_dve.sem, s_dve.base + 1)
                    g.indirect_dma_start(found[:, :], None, hist, bass.IndirectOffsetOnAxis(fix_ix[:, 0:1], 0),
                                         bounds_check=EMPTY - 1, oob_is_err=False).then_inc(s_misc.sem, 16)
                    g.wait_ge(s_dve.sem, s_dve.base + 3)
                    g.indirect_dma_start(hist, bass.IndirectOffsetOnAxis(fix_ix[:, 0:1], 0), found[:, :], None,
                                         bounds_check=EMPTY - 1, oob_is_err=False).then_inc(s_misc.sem, 16)
                    g.wait_ge(s_misc.sem, m0 + 32)
            s_pe.close(2)
            s_dve.close(3)
            s_misc.close(32)

        def node_gathers(blk, pool, table, width, last):
            @blk.gpsimd
            def _(g):
                def gather(i, u):
                    hold(g, "pool", c_ix.sem, c_ix.of(i, u))
                    hold(g, "pool", c_T.sem, c_T.of(i - 1, u))
                    g.indirect_dma_start(pool[:, u, 0:width], None, table, bass.IndirectOffsetOnAxis(nix[:, u:u + 1], 0),
                                         bounds_check=last, oob_is_err=False).then_inc(s_gat[u].sem, 16)
                staged(g, NT, UN, [(0, gather)])

        def place_ix(v, rows_of):
            def stage(i, u):
                v.wait_ge(s_gat[u].sem, s_gat[u].base + i * 16)
                chain.link(v.tensor_copy(nix[:, u:u + 1], rows_of[:, bass.ds(i * UN + u, 1)]))
                v.sem_inc(c_ix.sem, 1)
            return stage

        def combine(U, w, gain, bias, nxt):
            residual = gain is not None
            with scope() as st, block() as blk:
                hT, o, y, pool = (ring(st, n) for n in ("hT", "o", "y", "pool"))
                if residual:
                    cur = ring(st, "cur")
                if nxt:
                    hT2 = ring(st, "hT2")
                    w_next, b_next = nxt
                node_gathers(blk, pool, hist, D, EMPTY)
                final = c_out if residual else c_z

                def small(u):
                    return bank[2 + TURNED[u]][:, 0:D]

                def turned2(u):
                    return bank[4 + TURNED[u]][:, 0:D]

                def next_U(u):
                    return bank[6 + TURNED[u]][:, 0:D]

                @blk.vector
                def _(v):
                    stats, recip, _ = norm_stages(v, None, lambda i, u: y[:, u, :])

                    def join(i, u):
                        v.wait_ge(c_mm.sem, c_mm.of(i, u))
                        v.wait_ge(c_z.sem, c_z.of(i - 1, u))
                        chain.link(v.tensor_tensor(y[:, u, :], small(u), U[:, i * UN + u, :], ALU.add))
                        if residual:
                            v.wait_ge(s_cur[u].sem, s_cur[u].base + (i * 16 + 16))
                            chain.link(v.scalar_tensor_tensor(out=y[:, u, :], in0=y[:, u, :], scalar=0.0, in1=cur[:, u, :],
                                                              op0=ALU.max, op1=ALU.add))
                        v.sem_inc(c_y.sem, 1)
                        if residual:
                            stats(i, u)

                    def scale(i, u):
                        v.wait_ge(c_z.sem, c_z.of(i, u))
                        chain.link(v.tensor_tensor(o[:, u, :], o[:, u, :], gain[:, :], ALU.mult))
                        chain.link(v.tensor_tensor(o[:, u, :], o[:, u, :], bias[:, :], ALU.add))
                        if not nxt:
                            chain.link(v.tensor_tensor(X[:, i * UN + u, :], o[:, u, :], X[:, i * UN + u, :], ALU.add))
                        v.sem_inc(c_out.sem, 1)
                    if residual:
                        staged(v, NT, UN, [(0, place_ix(v, node_ix)), (5, join), (6, recip), (7, scale)], chain, 9 if nxt else 10)
                    else:
                        staged(v, NT, UN, [(0, place_ix(v, node_ix)), (5, join)], chain, 2)

                @blk.scalar
                def _(a):
                    _, _, sqrt = norm_stages(None, a, None)

                    def evac(i, u):
                        a.wait_ge(c_T.sem, c_T.of(i, u))
                        a.wait_ge(c_mm.sem, c_mm.of(i - 1, u))
                        a.activation(hT[:, u, :], ps_T(u), ACT.Copy).then_inc(c_hT.sem, 1)

                    def free_o(i, u):
                        if nxt:
                            a.wait_ge(s_st[u].sem, s_st[u].base + i * 16)
                            a.wait_ge(c_T2.sem, c_T2.of(i - 1, u))
                        else:
                            a.wait_ge(c_out.sem, c_out.of(i - 1, u))

                    def relu(i, u):
                        a.wait_ge(c_y.sem, c_y.of(i, u))
                        free_o(i, u)
                        a.activation(o[:, u, :], y[:, u, :], ACT.Relu).then_inc(c_z.sem, 1)

                    def normal(i, u):
                        a.wait_ge(c_norm.sem, c_norm.of(i, u))
                        free_o(i, u)
                        a.activation(o[:, u, :], y[:, u, :], ACT.Identity, bias=nmr[:, u:u + 1],
                                     scale=rstd[:, u:u + 1]).then_inc(c_z.sem, 1)

                    def evac2(i, u):
                        a.wait_ge(c_T2.sem, c_T2.of(i, u))
                        a.wait_ge(c_mm2.sem, c_mm2.of(i - 1, u))
                        a.activation(hT2[:, u, :], turned2(u), ACT.Copy).then_inc(c_hT2.sem, 1)

                    def keep(i, u):
                        a.wait_ge(c_mm2.sem, c_mm2.of(i, u))
                        a.activation(U[:, i * UN + u, :], next_U(u), ACT.Copy).then_inc(c_keep.sem, 1)
                    staged(a, NT, UN, [(3, evac)] + ([(5, sqrt), (6, normal)] if residual else [(5, relu)])
                           + ([(7, evac2), (8, keep)] if nxt else []))

                @blk.tensor
                def _(pe):
                    def turn(i, u):
                        pe.wait_ge(s_gat[u].sem, s_gat[u].base + (i * 16 + 16))
                        pe.wait_ge(c_hT.sem, c_hT.of(i, prior(u, TURNED)))
                        for k in range(KC):
                            t = pe.transpose(ps_T(u)[:, k * P:(k + 1) * P], pool[:, u, k * P:(k + 1) * P], ident[:, :])
                        t.then_inc(c_T.sem, 1)

                    def multiply(i, u):
                        pe.wait_ge(c_hT.sem, c_hT.of(i, u))
                        pe.wait_ge(c_y.sem, c_y.of(i, prior(u, TURNED)))
                        for k in range(KC):
                            m = pe.matmul(small(u), hT[:, u, k * P:(k + 1) * P], w[:, k, :], start=(k == 0), stop=(k == KC - 1))
                        m.then_inc(c_mm.sem, 1)

                    def turn2(i, u):
                        pe.wait_ge(final.sem, final.of(i, u))
                        pe.wait_ge(c_hT2.sem, c_hT2.of(i, prior(u, TURNED)))
                        for k in range(KC):
                            t = pe.transpose(turned2(u)[:, k * P:(k + 1) * P], o[:, u, k * P:(k + 1) * P], ident[:, :])
                        t.then_inc(c_T2.sem, 1)

                    def multiply2(i, u):
                        pe.wait_ge(c_hT2.sem, c_hT2.of(i, u))
                        pe.wait_ge(c_keep.sem, c_keep.of(i, prior(u, TURNED)))
                        pe.matmul(next_U(u), ones[0:1, :], b_next[0:1, :], start=True, stop=False)
                        for k in range(KC):
                            m = pe.matmul(next_U(u), hT2[:, u, k * P:(k + 1) * P], w_next[:, k, :], start=False, stop=(k == KC - 1))
                        m.then_inc(c_mm2.sem, 1)
                    staged(pe, NT, UN, [(0, turn), (1, multiply)] + ([(4, turn2), (5, multiply2)] if nxt else []))

                if residual or nxt:
                    @blk.sync
                    def _(sp):
                        def load(i, u):
                            sp.wait_ge(c_y.sem, c_y.of(i - 1, u))
                            sp.dma_start(cur[:, u, :], tab_t[bass.ds(i * UN + u, 1), :, :].rearrange("a p f -> p (a f)")).then_inc(s_cur[u].sem, 16)

                        def store(i, u):
                            sp.wait_ge(final.sem, final.of(i, u))
                            sp.dma_start(tab_t[bass.ds(i * UN + u, 1), :, :].rearrange("a p f -> p (a f)"), o[:, u, :]).then_inc(s_st[u].sem, 16)
                        staged(sp, NT, UN, ([(0, load)] if residual else []) + ([(6, store)] if nxt else []))
                        if nxt:
                            for u in range(UN):
                                sp.wait_ge(s_st[u].sem, s_st[u].base + NT // UN * 16)
            for c in (c_ix, c_T, c_hT, c_mm, c_y, c_z):
                c.close(NT)
            if residual:
                for c in (c_stat, c_sd, c_norm, c_out):
                    c.close(NT)
            if nxt:
                for c in (c_T2, c_hT2, c_mm2, c_keep):
                    c.close(NT)
            for u in range(UN):
                s_gat[u].close(NT // UN * 16)
                s_cur[u].close(NT // UN * 16 * residual)
                s_st[u].close(NT // UN * 16 * bool(nxt))

        def attention_pass(st, state, empty):
            kvs = [sb(st, f"kv{b}", [P, R * SLOT, KV]) for b in range(UB)]
            qs = [sb(st, f"q{b}", [P, R, D]) for b in range(UB)]
            s = sb(st, "s", [P, R, SLOT, HEADS])
            row_max = sb(st, "row_max", [P, R, HEADS])
            w = sb(st, "w", [P, UB, R * SLOT + R, HEADS])
            tmp = sb(st, "tmp", [P, ACC])
            c_weighted, c_summed = sem("att_weighted"), sem("att_summed")
            GATHERS = R * SLOT + R
            EXPS = R + 1

            def ps_row(b, r):
                return bank[(b * R + r) % 8][:, 0:ACC]

            def heads(ap):
                return ap.rearrange("p (d h) -> p d h", h=HEADS)

            with block() as blk:
                @blk.gpsimd
                def _(g):
                    def gather(i, b):
                        hold(g, "pool", c_eix.sem, c_eix.base + times(i, b, 2))
                        for r in range(R):
                            g.indirect_dma_start(qs[b][:, r, :], None, qtab, bass.IndirectOffsetOnAxis(ix[:, b, R * SLOT + r:R * SLOT + r + 1], 0),
                                                 bounds_check=NT * P - 1, oob_is_err=False).then_inc(s_eg[b].sem, 16)
                        for k in range(R * SLOT):
                            g.indirect_dma_start(kvs[b][:, k, :], None, kvtab, bass.IndirectOffsetOnAxis(ix[:, b, k:k + 1], 0),
                                                 bounds_check=NT * P - 1, oob_is_err=False).then_inc(s_eg[b].sem, 16)
                    staged(g, NBA, UB, [(0, gather)])

                @blk.vector
                def _(v):
                    def place(b, n):
                        v.tensor_copy(ix[:, b, 0:R * SLOT], dst_ix[:, bass.ds(n * (R * SLOT), R * SLOT)]).then_inc(c_eix.sem, 1)
                        v.tensor_copy(ix[:, b, R * SLOT:R * SLOT + R], src_ix[:, bass.ds(n * R, R)]).then_inc(c_eix.sem, 1)
                    chain.link(v.memset(state[UB - 1][:, R - 1, :], 0.0))
                    for m in range(UB):
                        place(m, m)

                    def score(i, b):
                        n = i * UB + b
                        kv, q, top_m = kvs[b], qs[b], state[b][:, :, ACC:STATE]
                        v.wait_ge(s_eg[b].sem, s_eg[b].base + (i * (16 * GATHERS) + 16 * GATHERS))
                        v.wait_ge(s_hs[b].sem, s_hs[b].base + i * 16)
                        keys = kv[:, :, 0:D].rearrange("p (r e) f -> p r e f", e=SLOT)
                        chain.link(v.tensor_tensor(keys, keys, q[:, :, None, :].to_broadcast([P, R, SLOT, D]), ALU.mult))
                        chain.link(v.tensor_reduce(s[:, :, :, :].rearrange("p r e h -> p (r e) h"),
                                                   kv[:, :, 0:D].rearrange("p k (d h) -> p k h d", h=HEADS), AX.X, ALU.add))
                        flat = s[:, :, :, :].rearrange("p r e h -> p (r e) h")
                        chain.link(v.tensor_tensor(flat, flat, empty[:, bass.ds(n * (R * SLOT), R * SLOT)][:, :, None]
                                                   .to_broadcast([P, R * SLOT, HEADS]), ALU.add))
                        chain.link(v.tensor_reduce(row_max[:, :, :], s[:, :, :, :].rearrange("p r e h -> p r h e"), AX.X, ALU.max))

                        def before(r):
                            return top_m[:, r - 1, :] if r else state[(b - 1) % UB][:, R - 1, ACC:STATE]
                        for r in range(R):
                            chain.link(v.scalar_tensor_tensor(out=top_m[:, r, :], in0=before(r), scalar=reset[:, bass.ds(n * R + r, 1)],
                                                              in1=row_max[:, r, :], op0=ALU.add, op1=ALU.max))
                        for r in range(R):
                            v.scalar_tensor_tensor(out=w[:, b, R * SLOT + r, :], in0=before(r), scalar=reset[:, bass.ds(n * R + r, 1)],
                                                   in1=top_m[:, r, :], op0=ALU.add, op1=ALU.subtract).then_inc(c_w.sem, 1)
                        v.tensor_tensor(w[:, b, 0:R * SLOT, :].rearrange("p (r e) h -> p r e h", e=SLOT), s[:, :, :, :],
                                        top_m[:, :, None, :].to_broadcast([P, R, SLOT, HEADS]), ALU.subtract).then_inc(c_w.sem, 1)

                    def weigh(i, b, r):
                        vals = kvs[b][:, r * SLOT:(r + 1) * SLOT, D:KV].rearrange("p e (d h) -> p e d h", h=HEADS)
                        v.tensor_tensor(vals, vals, w[:, b, r * SLOT:(r + 1) * SLOT, None, :].to_broadcast([P, SLOT, ACC // HEADS, HEADS]),
                                        ALU.mult).then_inc(c_weighted, 1)

                    done = [0]

                    def scale(r):
                        def stage(i, b):
                            if r == 0:
                                v.wait_ge(c_summed, times(i, b, 1))
                                if not is_first(i, b):
                                    v.wait_ge(c_batch.sem, c_batch.of(i, b - 1, UB))
                            before = state[b][:, r - 1, 0:ACC] if r else state[(b - 1) % UB][:, R - 1, 0:ACC]
                            chain.link(v.tensor_tensor(heads(tmp[:, :]), heads(before),
                                                       w[:, b, R * SLOT + r, None, :].to_broadcast([P, ACC // HEADS, HEADS]), ALU.mult))
                            ins = v.tensor_tensor(state[b][:, r, 0:ACC], ps_row(b, r), tmp[:, :], ALU.add)
                            if r == R - 1:
                                ins.then_inc(c_batch.sem, 1)
                            else:
                                done[0] = chain.inc(ins)
                        return stage

                    def scaled(r):
                        def stage(i, b):
                            if r == 0:
                                place(b, i * UB + b + UB)
                            if r < R - 1:
                                v.wait_ge(chain.sem, done[0])
                        return stage

                    def weigh_stage(r):
                        def stage(i, b):
                            if r == 0:
                                v.wait_ge(c_e.sem, c_e.of(i, b, UB))
                            weigh(i, b, r)
                        return stage
                    stages = [(0, score)]
                    for r in range(R):
                        stages += [(1, scale(r)), (0, weigh_stage(r)), (1, scaled(r))]
                    staged(v, NBA, UB, stages, chain, 4 + R + R + (R - 1))

                @blk.scalar
                def _(a):
                    def expo(i, b):
                        a.wait_ge(c_w.sem, c_w.base + times(i, b, EXPS))
                        a.activation(w[:, b, :, :], w[:, b, :, :], ACT.Exp).then_inc(c_e.sem, 1)
                    staged(a, NBA, UB, [(0, expo)])

                @blk.tensor
                def _(pe):
                    def add(i, b):
                        if not is_first(i, b):
                            if b == 0:
                                pe.wait_ge(c_batch.sem, c_batch.of(i, b - 1, UB))
                            elif not is_first(i, b, 0, 2):
                                pe.wait_ge(c_batch.sem, c_batch.of(i, b - 2, UB))
                        for r in range(R):
                            pe.wait_ge(c_weighted, times(i, b, R, r + 1))
                            for e in range(SLOT):
                                m = pe.matmul(ps_row(b, r), ident[:, :], kvs[b][:, r * SLOT + e, D:KV], start=(e == 0), stop=(e == SLOT - 1))
                        m.then_inc(c_summed, 1)
                    staged(pe, NBA, UB, [(0, add)])

                @blk.sync
                def _(sp):
                    def store(i, b):
                        sp.wait_ge(c_batch.sem, c_batch.of(i, b, UB))
                        sp.dma_start(ahist_p[:, bass.ds((i * UB + b) * R, R), :], state[b][:, :, :]).then_inc(s_hs[b].sem, 16)
                    staged(sp, NBA, UB, [(0, store)])
                    for b in range(UB):
                        sp.wait_ge(s_hs[b].sem, s_hs[b].base + (NBA // UB) * 16)
            c_eix.close(2 * (NBA + UB))
            c_batch.close(NBA)
            c_w.close(NBA * EXPS)
            c_e.close(NBA)
            for b in range(UB):
                s_eg[b].close(NBA // UB * 16 * GATHERS)
                s_hs[b].close(NBA // UB * 16)

        def carry_attention(state):
            last = state[UB - 1][:, R - 1, :]
            G8 = P // HEADS
            with ExitStack() as st, block() as blk:
                spread = sb(st, "spread", [P, 2, G8, HEADS])
                mc = sb(st, "mc", [P, P + 1])
                ar = sb(st, "ar", [P, 2, P])
                part = sb(st, "part", [P, 3, P])
                sc = sb(st, "sc", [P, 3, P + 1])
                found = sb(st, "found", [P, STATE])
                top_m = sb(st, "top_m", [P, HEADS])
                e2 = sb(st, "e2", [P, 2, HEADS])
                add = sb(st, "add", [P, ACC])
                m0 = s_misc.base

                @blk.tensor
                def _(pe):
                    pe.wait_ge(s_dve.sem, s_dve.base + 1)
                    ins = (last[:, 0:P], last[:, P:2 * P], spread[:, 0, :, :].rearrange("p a b -> p (a b)"),
                           spread[:, 1, :, :].rearrange("p a b -> p (a b)"))
                    for k, a in enumerate(ins):
                        t = pe.transpose(bank[0][:, k * P:(k + 1) * P], a, ident[:, :])
                    t.then_inc(s_pe.sem, 1)
                    pe.wait_ge(s_dve.sem, s_dve.base + 3)
                    for k, a in enumerate((sc[:, 0, 0:P], sc[:, 1, 0:P], sc[:, 2, 0:P], mc[:, 0:P])):
                        t = pe.transpose(bank[1][:, k * P:(k + 1) * P], a, ident[:, :])
                    t.then_inc(s_pe.sem, 1)

                @blk.scalar
                def _(a):
                    a.wait_ge(s_dve.sem, s_dve.base + 2)
                    a.activation(ar[:, :, :], ar[:, :, :], ACT.Exp).then_inc(c_e.sem, 1)
                    a.wait_ge(s_dve.sem, s_dve.base + 4)
                    a.activation(e2[:, :, :], e2[:, :, :], ACT.Exp).then_inc(c_e.sem, 1)

                @blk.vector
                def _(v):
                    chain.inc(v.memset(found[:, :], 0.0))
                    for k in range(2):
                        chain.link(v.tensor_copy(spread[:, k, :, :], last[:, None, D + k * HEADS:ACC + k * HEADS]
                                                 .to_broadcast([P, G8, HEADS])))
                    v.sem_inc(s_dve.sem, 1)
                    chain.inc(v.memset(mc[:, 0:1], NEG))
                    chain.link(v.memset(sc[:, :, 0:1], 0.0))
                    v.wait_ge(s_pe.sem, s_pe.base + 1)
                    chain.link(v.tensor_tensor_scan(mc[:, 1:P + 1], Rrow[:, :], bank[0][:, 3 * P:4 * P], NEG, ALU.add, ALU.max))
                    chain.inc(v.tensor_tensor(ar[:, 0, :], bank[0][:, 3 * P:4 * P], mc[:, 1:P + 1], ALU.subtract))
                    chain.link(v.tensor_tensor(ar[:, 1, :], mc[:, 0:P], Rrow[:, :], ALU.add))
                    chain.link(v.tensor_tensor(ar[:, 1, :], ar[:, 1, :], mc[:, 1:P + 1], ALU.subtract))
                    v.sem_inc(s_dve.sem, 1)
                    v.wait_ge(c_e.sem, c_e.base + 1)
                    for k in range(3):
                        chain.link(v.tensor_tensor(part[:, k, :], bank[0][:, k * P:(k + 1) * P], ar[:, 0, :], ALU.mult))
                    for k in range(3):
                        chain.link(v.tensor_tensor_scan(sc[:, k, 1:P + 1], ar[:, 1, :], part[:, k, :], 0.0, ALU.mult, ALU.add))
                    v.sem_inc(s_dve.sem, 1)
                    v.wait_ge(s_pe.sem, s_pe.base + 2)
                    v.wait_ge(s_misc.sem, m0 + 16)
                    chain.link(v.tensor_tensor(top_m[:, :], bank[1][:, 3 * P:3 * P + HEADS], found[:, ACC:STATE], ALU.max))
                    chain.inc(v.tensor_tensor(e2[:, 0, :], found[:, ACC:STATE], top_m[:, :], ALU.subtract))
                    chain.link(v.tensor_tensor(e2[:, 1, :], bank[1][:, 3 * P:3 * P + HEADS], top_m[:, :], ALU.subtract))
                    v.sem_inc(s_dve.sem, 1)
                    v.wait_ge(c_e.sem, c_e.base + 2)

                    def by_head(ap):
                        return ap.rearrange("p (d h) -> p d h", h=HEADS)

                    def factor(k):
                        return e2[:, k, None, :].to_broadcast([P, ACC // HEADS, HEADS])
                    chain.inc(v.tensor_tensor(by_head(found[:, 0:ACC]), by_head(found[:, 0:ACC]), factor(0), ALU.mult))
                    chain.link(v.tensor_tensor(by_head(add[:, :]), by_head(bank[1][:, 0:ACC]), factor(1), ALU.mult))
                    chain.link(v.tensor_tensor(found[:, 0:ACC], found[:, 0:ACC], add[:, :], ALU.add))
                    v.sem_inc(s_dve.sem, 1)

                @blk.gpsimd
                def _(g):
                    g.wait_ge(s_dve.sem, s_dve.base + 1)
                    g.indirect_dma_start(found[:, :], None, ahist, bass.IndirectOffsetOnAxis(fix_ix[:, 0:1], 0),
                                         bounds_check=NOROW - 1, oob_is_err=False).then_inc(s_misc.sem, 16)
                    g.wait_ge(s_dve.sem, s_dve.base + 5)
                    g.indirect_dma_start(ahist, bass.IndirectOffsetOnAxis(fix_ix[:, 0:1], 0), found[:, :], None,
                                         bounds_check=NOROW - 1, oob_is_err=False).then_inc(s_misc.sem, 16)
                    g.wait_ge(s_misc.sem, m0 + 32)
            s_pe.close(2)
            s_dve.close(5)
            c_e.close(2)
            s_misc.close(32)

        def finish(w, bias):
            with ExitStack() as st, block() as blk:
                rz = sb(st, "rz", [P, UN, HEADS])
                h, hT, o, pool = ring(st, "h"), ring(st, "hT"), ring(st, "o"), ring(st, "pool", STATE)
                node_gathers(blk, pool, ahist, STATE, NOROW)

                @blk.vector
                def _(v):
                    def divide(i, u):
                        v.wait_ge(s_gat[u].sem, s_gat[u].base + (i * 16 + 16))
                        chain.link(v.reciprocal(rz[:, u, :], pool[:, u, D:ACC]))
                        chain.link(v.tensor_tensor(h[:, u, :].rearrange("p (d h) -> p d h", h=HEADS),
                                                   pool[:, u, 0:D].rearrange("p (d h) -> p d h", h=HEADS),
                                                   rz[:, u, None, :].to_broadcast([P, HD, HEADS]), ALU.mult))
                        v.sem_inc(c_h.sem, 1)

                    def join(i, u):
                        v.wait_ge(c_mm.sem, c_mm.of(i, u))
                        v.wait_ge(s_st[u].sem, s_st[u].base + i * 16)
                        chain.link(v.tensor_tensor(o[:, u, :], ps_small(u), bias[:, :], ALU.add))
                        chain.link(v.tensor_tensor(o[:, u, :], o[:, u, :], X[:, bass.ds(i * UN + u, 1), :].rearrange("p a f -> p (a f)"), ALU.add))
                        v.sem_inc(c_out.sem, 1)
                    staged(v, NT, UN, [(0, place_ix(v, node_ix2)), (3, divide), (6, join)], chain, 5)

                @blk.scalar
                def _(a):
                    def evac(i, u):
                        a.wait_ge(c_T.sem, c_T.of(i, u))
                        a.wait_ge(c_mm.sem, c_mm.of(i - 1, u))
                        a.activation(hT[:, u, :], ps_T(u), ACT.Copy).then_inc(c_hT.sem, 1)
                    staged(a, NT, UN, [(0, evac)])

                @blk.tensor
                def _(pe):
                    def turn(i, u):
                        pe.wait_ge(c_h.sem, c_h.of(i, u))
                        pe.wait_ge(c_hT.sem, c_hT.of(i, prior(u, TURNED)))
                        for k in range(KC):
                            t = pe.transpose(ps_T(u)[:, k * P:(k + 1) * P], h[:, u, k * P:(k + 1) * P], ident[:, :])
                        t.then_inc(c_T.sem, 1)

                    def multiply(i, u):
                        pe.wait_ge(c_hT.sem, c_hT.of(i, u))
                        pe.wait_ge(c_out.sem, c_out.of(i, prior(u, PRODUCT)))
                        for k in range(KC):
                            m = pe.matmul(ps_small(u), hT[:, u, k * P:(k + 1) * P], w[:, k, :], start=(k == 0), stop=(k == KC - 1))
                        m.then_inc(c_mm.sem, 1)
                    staged(pe, NT, UN, [(0, turn), (1, multiply)])

                @blk.sync
                def _(sp):
                    def store(i, u):
                        sp.wait_ge(c_out.sem, c_out.of(i, u))
                        if isinstance(i, int) and i * UN + u == NT - 1:
                            sp.dma_start(out[(NT - 1) * P:N, :], o[0:TAIL, u, :]).then_inc(s_st[u].sem, 16)
                        else:
                            sp.dma_start(out[bass.ds((i * UN + u) * P, P), :], o[:, u, :]).then_inc(s_st[u].sem, 16)
                    staged(sp, NT, UN, [(UN, store)])
                    for u in range(UN):
                        sp.wait_ge(s_st[u].sem, s_st[u].base + NT // UN * 16)

        load_base = [loads * 16]

        def load(pairs):
            with block() as blk:
                @blk.sync
                def _(sp):
                    for dest, source in pairs:
                        sp.dma_start(dest, source).then_inc(s_load, 16)
                        load_base[0] += 16
                    sp.wait_ge(s_load, load_base[0])

        def chunks(w):
            return w.rearrange("(k p) n -> p k n", p=P)

        with scope() as l0:
            def mat(name):
                return sb(l0, name, [P, KC, D])

            def vec(name):
                return sb(l0, name, [P, D])
            U = sb(l0, "U", [P, NT, D])
            w_p1, w_m1a, w_m1b, w_m2a, w_m2b, w_m3a, w_m3b = (mat(n) for n in ("w_p1", "w_m1a", "w_m1b", "w_m2a", "w_m2b",
                                                                            "w_m3a", "w_m3b"))
            v_p1, v_m1, v_g2, v_b2, v_g3, v_b3 = (vec(n) for n in ("v_p1", "v_m1", "v_g2", "v_b2", "v_g3", "v_b3"))
            r_m2, r_m3 = sb(l0, "r_m2", [1, D]), sb(l0, "r_m3", [1, D])
            load([(w_p1[:, :, :], chunks(wp1)), (w_m1a[:, :, :], chunks(wm1[0:D, :])), (w_m1b[:, :, :], chunks(wm1[D:2 * D, :])),
                  (w_m2a[:, :, :], chunks(wm2[0:D, :])), (w_m2b[:, :, :], chunks(wm2[D:2 * D, :])),
                  (w_m3a[:, :, :], chunks(wm3[0:D, :])), (w_m3b[:, :, :], chunks(wm3[D:2 * D, :])),
                  (v_p1[:, :], rows(bp1)), (v_m1[:, :], rows(bm1)), (v_g2[:, :], rows(g2)), (v_b2[:, :], rows(b2)),
                  (v_g3[:, :], rows(g3)), (v_b3[:, :], rows(b3)), (r_m2[:, :], rows(bm2, 1)), (r_m3[:, :], rows(bm3, 1))])

            with scope() as t:
                o = ring(t, "o")

                def emit1(v, i, u):
                    chain.inc(v.tensor_tensor(U[:, i * UN + u, :], ps_small(u), v_m1[:, :], ALU.add))
                    chain.link(v.tensor_tensor(o[:, u, :], ps_wide(u)[:, 0:D], v_p1[:, :], ALU.add))
                    chain.link(v.tensor_scalar(o[:, u, :], o[:, u, :], 0.0, None, ALU.max))

                def store1(sp, i, u):
                    sp.dma_start(tab_t[bass.ds(i * UN + u, 1), :, :].rearrange("a p f -> p (a f)"), o[:, u, :]).then_inc(s_st[u].sem, 16)
                project([(lambda k: w_m1a[:, k, :], ps_small), (lambda k: w_p1[:, k, :], lambda u: ps_wide(u)[:, 0:D])],
                        emit1, 1, store1, 3)

            with scope() as g:
                G = [sb(g, f"G{b}", [P, J, D]) for b in range(UB)]
                edge_marks(dst_ix, CH)
                with scope() as c:
                    degrees = Degrees(c)
                    max_pass(G, degrees)
                    find_rows(degrees)
                carry_max(G)
                combine(U, w_m1b, None, None, (w_m2a, r_m2))
                place = sb(g, "place", [P, CH])
                with scope() as c:
                    max_pass(G, Ranks(c, place))
                carry_max(G)
                combine(U, w_m2b, v_g2, v_b2, (w_m3a, r_m3))
                with scope() as c:
                    max_pass(G, Permute(c, place))
                carry_max(G)
                combine(U, w_m3b, v_g3, v_b3, None)
        empty = sb(top, "empty", [P, SL])
        nodes_of_rows(empty)
        edge_marks(src_ix, RP)

        with scope() as l1:
            w_q, w_o = sb(l1, "w_q", [P, KC, D]), sb(l1, "w_o", [P, KC, D])
            w_kv = sb(l1, "w_kv", [P, KC, 2 * D])
            v_q, v_o, v_kv = sb(l1, "v_q", [P, D]), sb(l1, "v_o", [P, D]), sb(l1, "v_kv", [P, 2 * D])
            load([(w_q[:, :, :], chunks(wq)), (w_o[:, :, :], chunks(wo)), (w_kv[:, :, 0:D], chunks(wk)), (w_kv[:, :, D:2 * D], chunks(wv)),
                  (v_q[:, :], rows(bq)), (v_o[:, :], rows(bo)), (v_kv[:, 0:D], rows(bk)), (v_kv[:, D:2 * D], rows(bv))])
            with scope() as t:
                okv, o = ring(t, "okv", KV), ring(t, "o")
                SC = float(HD) ** -0.5
                with block() as blk:
                    @blk.vector
                    def _(v):
                        chain.inc(v.memset(okv[:, :, 2 * D:KV], 1.0))
                        chain.link(v.tensor_scalar(v_q[:, :], v_q[:, :], SC, None, ALU.mult))

                def emit2(v, i, u):
                    chain.inc(v.tensor_tensor(okv[:, u, 0:2 * D], ps_wide(u), v_kv[:, :], ALU.add))
                    chain.link(v.scalar_tensor_tensor(out=o[:, u, :], in0=ps_small(u), scalar=SC, in1=v_q[:, :], op0=ALU.mult, op1=ALU.add))

                def store2(sp, i, u):
                    sp.dma_start(qtab_t[bass.ds(i * UN + u, 1), :, :].rearrange("a p f -> p (a f)"), o[:, u, :]).then_inc(s_st[u].sem, 16)
                    sp.dma_start(kvtab_t[bass.ds(i * UN + u, 1), :, :].rearrange("a p f -> p (a f)"), okv[:, u, :]).then_inc(s_st[u].sem, 16)
                project([(lambda k: w_q[:, k, :], ps_small), (lambda k: w_kv[:, k, :], ps_wide)], emit2, 2, store2, 2)
            with scope() as a:
                state = [sb(a, f"state{b}", [P, R, STATE]) for b in range(UB)]
                with scope() as q:
                    attention_pass(q, state, empty)
                carry_attention(state)
            finish(w_o, v_o)


_INS = [("x", "x"), ("src", "src"), ("dst", "dst"), ("wp1", "L0_gnn_Wp1"), ("bp1", "L0_gnn_bp1"), ("wm1", "L0_gnn_Wm1"),
        ("bm1", "L0_gnn_bm1"), ("wm2", "L0_gnn_Wm2"), ("bm2", "L0_gnn_bm2"), ("wm3", "L0_gnn_Wm3"), ("bm3", "L0_gnn_bm3"),
        ("g2", "L0_gnn_ln2_g"), ("b2", "L0_gnn_ln2_b"), ("g3", "L0_gnn_ln3_g"), ("b3", "L0_gnn_ln3_b"),
        ("wq", "L1_gnn_Wq"), ("bq", "L1_gnn_bq"), ("wk", "L1_gnn_Wk"), ("bk", "L1_gnn_bk"), ("wv", "L1_gnn_Wv"),
        ("bv", "L1_gnn_bv"), ("wo", "L1_gnn_Wo"), ("bo", "L1_gnn_bo")]
_TRANSPOSED = ("wp1", "wm1", "wm2", "wm3")


def kernel(**inputs):
    import numpy as np
    import concourse.bacc as bacc
    from concourse.bass_utils import run_bass_kernel_spmd

    nc = bacc.Bacc("TRN2", target_bir_lowering=False, num_devices=1)
    arrays, args = {}, {}
    for short, name in _INS:
        a = np.asarray(inputs[name])
        a = np.ascontiguousarray(a.T if short in _TRANSPOSED else a)
        arrays[f"in_{short}"] = a
        args[short] = nc.dram_tensor(f"in_{short}", a.shape, mybir.dt.from_np(a.dtype), kind="ExternalInput").ap()
    n, d = inputs["x"].shape
    out = nc.dram_tensor("out_0", (n, d), F32, kind="ExternalOutput").ap()
    gnn_kernel(nc, out=out, **args)
    r = run_bass_kernel_spmd(nc, [arrays], core_ids=[0])
    return r.results[0]["out_0"]
```

```python
from contextlib import ExitStack, contextmanager, nullcontext

import concourse.bass as bass
from concourse import mybir

F32, BF16, I32, I16 = mybir.dt.float32, mybir.dt.bfloat16, mybir.dt.int32, mybir.dt.int16
ALU, ACT, AX = mybir.AluOpType, mybir.ActivationFunctionType, mybir.AxisListType

P = 128
D = 256
KC = D // P
HEADS = 8
HD = D // HEADS
EPS = 1e-5
NEG = -1e30
FAR = 1_000_000.0
ACC = D + HEADS
KV = D + ACC
STATE = ACC + HEADS
SLOT = 4
R = 3
UN = 7
J = 9
UB = 3


class Count:

    def __init__(self, sem, start=0):
        self.sem, self.base = sem, start

    def of(self, i, u, per=UN):
        return self.base + (i * per + (u + 1))

    def close(self, n):
        self.base += n


class Chain:

    def __init__(self, eng, sem):
        self.eng, self.sem, self.base, self.term = eng, sem, 0, 0

    def inc(self, ins):
        ins.then_inc(self.sem, 1)
        self.base += 1
        return self.base + self.term

    def link(self, ins):
        self.eng.wait_ge(self.sem, self.inc(ins))

    @contextmanager
    def body(self, i, per, times):
        start, self.term = self.base, i * per
        yield
        assert self.base - start == per, (self.base - start, per)
        self.base, self.term = start + per * times, 0


def staged(eng, steps, un, stages, chain=None, links=0):
    stages = [(delay, stage, rest[0] if rest else steps) for delay, stage, *rest in stages]
    turns = -(-max(delay + count for delay, _, count in stages) // un)

    def turn(i, active):
        for u in range(un):
            started = []
            for delay, stage, count in stages:
                d, uu = divmod(u - delay, un)
                if not active(delay, count, u):
                    continue
                parts = stage(i + d, uu)
                if parts is not None:
                    started.append(parts)
            while started:
                started = [parts for parts in started if next(parts, False) is not False]

    def filled(t):
        have = [sum(0 <= t * un + u - delay < count for u in range(un)) for delay, _, count in stages]
        return have if all(n in (0, un) for n in have) else None

    first = 1 + -(-max(delay for delay, _, _ in stages) // un)
    t = 0
    while t < turns:
        end = t + 1
        while t >= first and filled(t) and end < turns and filled(end) == filled(t):
            end += 1
        if end == t + 1:
            turn(t, lambda delay, count, u: 0 <= t * un + u - delay < count)
        else:
            with eng.Fori(t, end) as i:
                with chain.body(i - t, links * un, end - t) if chain else nullcontext():
                    turn(i, lambda delay, count, u: 0 <= t * un + u - delay < count)
        t = end


def gnn_kernel(nc, x, src, dst, wp1, bp1, wm1, bm1, wm2, bm2, wm3, bm3, g2, b2, g3, b3,
               wq, bq, wk, bk, wv, bv, wo, bo, out):
    N, E = x.shape[0], src.shape[0]
    NT = -(-N // P)
    NT = -(-NT // UN) * UN
    TAIL = N - (NT - 1) * P
    NB = -(-(-(-E // P)) // J)
    NB = -(-NB // UB) * UB
    CH = NB * J
    LASTE = E - (P - 1) * CH
    EMPTY = P * CH
    PAD = NT * P - 1
    RP = -(-(-(-(E + (SLOT - 1) * N) // SLOT)) // P)
    NBA = -(-(-(-RP // R)) // UB) * UB
    RP = NBA * R
    SL = RP * SLOT
    NOROW = P * RP
    assert 0 < TAIL < P and 0 < LASTE < CH and PAD >= N

    tab = nc.dram_tensor("tab", [NT * P, D], F32, kind="Internal").ap()
    hist = nc.dram_tensor("hist", [EMPTY + 1, D], F32, kind="Internal").ap()
    kvtab = nc.dram_tensor("kvtab", [NT * P, KV], F32, kind="Internal").ap()
    qtab = nc.dram_tensor("qtab", [NT * P, D], F32, kind="Internal").ap()
    ahist = nc.dram_tensor("ahist", [NOROW + 1, STATE], F32, kind="Internal").ap()
    tab_t = tab.rearrange("(t p) f -> t p f", p=P)
    kvtab_t = kvtab.rearrange("(t p) f -> t p f", p=P)
    qtab_t = qtab.rearrange("(t p) f -> t p f", p=P)
    hist_p = hist[0:EMPTY, :].rearrange("(p j) f -> p j f", p=P)
    ahist_p = ahist[0:NOROW, :].rearrange("(p j) f -> p j f", p=P)

    def rows(v, n=P):
        return bass.AP(tensor=v.tensor, offset=v.offset, ap=[[0, n], [1, v.shape[0]]])

    with ExitStack() as top:
        def scope():
            return ExitStack()

        names = {}

        def sb(stack, name, shape, dt=F32):
            names[name] = names.get(name, 0) + 1
            return stack.enter_context(nc.sbuf_tensor(f"{name}_{names[name]}", shape, dt))

        def sem(name):
            return top.enter_context(nc.semaphore(name))

        X = sb(top, "X", [P, NT, D])
        src_ix = sb(top, "src_ix", [P, CH + 2 * J], I32)
        dst_ix = sb(top, "dst_ix", [P, max(CH + 2 * J, SL + UB * R * SLOT)], I32)
        reset = sb(top, "reset", [P, CH])
        row_reset = sb(top, "row_reset", [P, RP])
        row_node = sb(top, "row_node", [P, RP + UB * R], I32)
        ident = sb(top, "ident", [P, P])
        node_ix = sb(top, "node_ix", [P, NT], I32)
        node_ix2 = sb(top, "node_ix2", [P, NT], I32)
        fix_ix = sb(top, "fix_ix", [P, 1], I32)
        row_fix_ix = sb(top, "row_fix_ix", [P, 1], I32)
        Rrow = sb(top, "Rrow", [P, P])
        row_Rrow = sb(top, "row_Rrow", [P, P])
        eps = sb(top, "eps", [P, 1])
        ix = sb(top, "ix", [P, UB, R * SLOT + R], I32)
        nix = sb(top, "nix", [P, UN], I32)
        stat = sb(top, "stat", [P, UN, 6])
        mv = sb(top, "mv", [P, UN, 2])
        sd = sb(top, "sd", [P, UN])
        rstd = sb(top, "rstd", [P, NT])
        nmr = sb(top, "nmr", [P, NT])
        rows_upto = sb(top, "rows_upto", [P, NT])
        rows_own = sb(top, "rows_own", [P, NT])
        bank = [top.enter_context(nc.psum_tensor(f"bank{n}", [P, 512], F32)) for n in range(8)]

        s_const = sem("s_const")
        const_base = [11]
        s_load = sem("s_load")
        s_misc = Count(sem("s_misc"))
        s_misc2 = Count(sem("s_misc2"))
        c_stat, c_sd, c_norm, c_h, c_T, c_hT, c_mm, c_y, c_z, c_out, c_ix = (
            Count(sem(n), UN) for n in ("c_stat", "c_sd", "c_norm", "c_h", "c_T", "c_hT", "c_mm", "c_y", "c_z",
                                    "c_out", "c_ix"))
        c_keep = Count(sem("c_keep"), UN)
        counts = (c_stat, c_sd, c_norm, c_h, c_T, c_hT, c_mm, c_y, c_z, c_out, c_ix, c_keep)
        s_gat = [Count(sem(f"s_gat{u}")) for u in range(UN)]
        s_cur = [Count(sem(f"s_cur{u}")) for u in range(UN)]
        s_st = [Count(sem(f"s_st{u}")) for u in range(UN)]
        s_tile = [Count(sem(f"s_tile{b}")) for b in range(UB)]
        s_eg = [Count(sem(f"s_eg{b}")) for b in range(UB)]
        s_hs = [Count(sem(f"s_hs{b}")) for b in range(UB)]
        c_eix, c_batch, c_w, c_e = (Count(sem(n)) for n in ("c_eix", "c_batch", "c_w", "c_e"))
        s_held = {"vector": sem("s_held_v"), "pool": sem("s_held_p")}
        s_pe = Count(sem("s_pe"))
        s_dve = Count(sem("s_dve"))
        chain = Chain(nc.vector, sem("chain"))

        def block():
            return nc.Block()

        def ring(stack, name, width=D):
            return sb(stack, name, [P, UN, width])

        def hold(eng, who, sem, value):
            eng.wait_ge(sem, value)
            eng.sem_inc(s_held[who], 1)

        TURNED = (0, 1, 0, 1, 0, 1, 0)
        PRODUCT = (0, 1, 2, 0, 1, 2, 1)

        def prior(u, ring):
            return next(v for v in range(u - 1, u - UN - 1, -1) if ring[v % UN] == ring[u])

        def ps_T(u):
            return bank[TURNED[u]][:, 0:D]

        def ps_small(u):
            return bank[2 + 2 * PRODUCT[u]][:, 0:D]

        def ps_wide(u):
            return bank[3 + 2 * PRODUCT[u]][:, :]

        ones = sb(top, "ones", [P, P])
        keys_of = {w: nc.dram_tensor(f"keys{w}", [P * w + 2], I32, kind="Internal").ap() for w in (CH, RP)}

        with scope() as st0:
            zrow = sb(st0, "zrow", [1, D + STATE])
            pad2 = sb(st0, "pad2", [1, 2], I32)
            with block() as blk:
                @blk.gpsimd
                def _(g):
                    g.memset(ident[:, :], 0.0).then_inc(s_const, 1)
                    g.memset(ones[:, :], 1.0).then_inc(s_const, 1)
                    g.memset(src_ix[:, :], PAD).then_inc(s_const, 1)
                    g.memset(row_node[:, :], PAD).then_inc(s_const, 1)
                    g.memset(dst_ix[:, :], PAD).then_inc(s_const, 1)
                    g.memset(pad2[:, :], PAD).then_inc(s_const, 1)
                    g.memset(X[:, NT - 1, :], 0.0).then_inc(s_const, 1)
                    g.memset(eps[:, :], EPS).then_inc(s_const, 1)
                    g.memset(zrow[:, :], 0.0).then_inc(s_const, 1)
                    g.wait_ge(s_const, 9)
                    g.memset(zrow[:, D + D:D + ACC], 1.0).then_inc(s_const, 1)
                    g.affine_select(out=ident[:, :], in_=ident[:, :], compare_op=ALU.not_equal, fill=1.0,
                                    base=0, pattern=[[-1, P]], channel_multiplier=1).then_inc(s_const, 1)

                @blk.sync
                def _(sp):
                    for c in counts:
                        sp.sem_inc(c.sem, UN)
                    sp.dma_start(X[:, 0:NT - 1, :], x[0:(NT - 1) * P, :].rearrange("(t p) f -> p t f", p=P)).then_inc(s_load, 16)
                    sp.wait_ge(s_const, 11)
                    full = (P - 1) * CH
                    for dest, v in ((src_ix, src), (dst_ix, dst)):
                        sp.dma_start(dest[0:P - 1, 0:CH], v[0:full].rearrange("(p j) -> p j", j=CH)).then_inc(s_load, 16)
                        sp.dma_start(dest[P - 1:P, 0:LASTE], v[full:E].rearrange("(p j) -> p j", p=1)).then_inc(s_load, 16)
                    sp.dma_start(X[0:TAIL, NT - 1, :], x[(NT - 1) * P:N, :]).then_inc(s_load, 16)
                    sp.dma_start(hist[EMPTY:EMPTY + 1, :], zrow[:, 0:D]).then_inc(s_load, 16)
                    sp.dma_start(ahist[NOROW:NOROW + 1, :], zrow[:, D:D + STATE]).then_inc(s_load, 16)
                    for w, keys in keys_of.items():
                        sp.dma_start(keys[0:1].rearrange("(a b) -> a b", a=1), pad2[:, 0:1]).then_inc(s_load, 16)
                        sp.dma_start(keys[P * w + 1:P * w + 2].rearrange("(a b) -> a b", a=1), pad2[:, 1:2]).then_inc(s_load, 16)
                    sp.wait_ge(s_load, 16 * 12)
            loads = 12

        class Marks:

            def __init__(self, st, order, CH, reset, fix, passing):
                self.order, self.CH, self.reset, self.fix, self.passing = order, CH, reset, fix, passing
                self.near = sb(st, "near", [P, CH + 2], I32)
                self.nearf = sb(st, "nearf", [P, CH + 2])
                self.jp = sb(st, "jp", [P, CH])
                self.jpi = sb(st, "jpi", [P, CH], I32)
                self.neq = sb(st, "neq", [P, CH + 1])
                self.first_i = sb(st, "first_i", [P, 1], I32)
                self.firstf = sb(st, "firstf", [P, 1])
                self.end = sb(st, "end", [P, 1])
                self.flag = sb(st, "flag", [P, 1])
                self.flagw = sb(st, "flagw", [P, P])
                self.const0 = const_base[0]
                const_base[0] += 2

            def pool(self, g):
                g.iota(self.jpi[:, :], [[1, self.CH]], base=0, channel_multiplier=0).then_inc(s_const, 1)
                g.iota(self.first_i[:, :], [[0, 1]], base=0, channel_multiplier=self.CH).then_inc(s_const, 1)

            def sync(self, sp):
                CH, keys = self.CH, keys_of[self.CH]
                sp.dma_start(keys[1:P * CH + 1].rearrange("(p j) -> p j", j=CH), self.order[:, 0:CH]).then_inc(s_misc2.sem, 16)
                sp.wait_ge(s_misc2.sem, s_misc2.base + 16)
                sp.dma_start(self.near[:, :], bass.AP(tensor=keys.tensor, offset=keys.offset, ap=[[CH, P], [1, CH + 2]])).then_inc(s_misc2.sem, 16)

            def vector(self, v):
                CH, jp, nearf, neq, end, flag = self.CH, self.jp, self.nearf, self.neq, self.end, self.flag
                v.wait_ge(s_const, self.const0 + 2)
                chain.inc(v.tensor_copy(jp[:, :], self.jpi[:, :]))
                chain.inc(v.tensor_copy(self.firstf[:, :], self.first_i[:, :]))
                v.wait_ge(s_misc2.sem, s_misc2.base + 32)
                chain.link(v.tensor_copy(nearf[:, :], self.near[:, :]))
                chain.link(v.tensor_tensor(neq[:, :], nearf[:, 0:CH + 1], nearf[:, 1:CH + 2], ALU.not_equal))
                chain.inc(v.tensor_scalar(self.reset[:, :], neq[:, 0:CH], NEG, None, ALU.mult))
                chain.link(v.tensor_scalar(jp[:, :], jp[:, :], FAR, None, ALU.add))
                chain.inc(v.memset(self.reset[:, 0:1], NEG))
                chain.link(v.scalar_tensor_tensor(out=jp[:, :], in0=neq[:, 1:CH + 1], scalar=-FAR, in1=jp[:, :],
                                                  op0=ALU.mult, op1=ALU.add))
                chain.inc(v.tensor_tensor(flag[:, :], nearf[:, 1:2], nearf[:, CH:CH + 1], ALU.not_equal))
                chain.link(v.tensor_reduce(end[:, :], jp[:, :], AX.X, ALU.min))
                chain.inc(v.tensor_tensor(flag[:, :], flag[:, :], neq[:, 0:1], ALU.max))
                chain.link(v.scalar_tensor_tensor(out=end[:, :], in0=neq[:, 0:1], scalar=FAR,
                                                  in1=end[:, :], op0=ALU.mult, op1=ALU.add))
                chain.inc(v.tensor_scalar(self.flagw[:, :], ones[:, :], flag[:, 0:1], None, ALU.mult))
                chain.link(v.tensor_tensor(end[:, :], end[:, :], self.firstf[:, :], ALU.add))
                chain.link(v.tensor_copy(self.fix[:, :], end[:, :]))
                v.sem_inc(s_dve.sem, 1)
                v.wait_ge(s_pe.sem, s_pe.base + 1)
                chain.link(v.tensor_scalar(self.passing[:, :], bank[5][:, 0:P], NEG, None, ALU.mult))

            def tensor(self, pe):
                pe.wait_ge(s_dve.sem, s_dve.base + 1)
                pe.matmul(bank[5][:, 0:P], self.flagw[:, :], ident[:, :], start=True, stop=True).then_inc(s_pe.sem, 1)

            def close(self):
                s_dve.close(1)
                s_pe.close(1)
                s_misc2.close(32)

        def norm_stages(v, a, of_y):
            def stats(i, u):
                at = chain.inc(v.bn_stats(stat[:, u, :], of_y(i, u)))
                yield
                hold(v, "vector", chain.sem, at)
                v.bn_aggr(mv[:, u, :], stat[:, u, :]).then_inc(c_stat.sem, 1)

            def recip(i, u):
                v.wait_ge(c_sd.sem, c_sd.of(i, u))
                tile = bass.ds(i * UN + u, 1)
                at = chain.inc(v.reciprocal(rstd[:, tile], sd[:, u:u + 1]))
                yield
                v.wait_ge(chain.sem, at)
                v.scalar_tensor_tensor(out=nmr[:, tile], in0=mv[:, u, 0:1], scalar=-1.0,
                                       in1=rstd[:, tile], op0=ALU.mult, op1=ALU.mult).then_inc(c_norm.sem, 1)

            def sqrt(i, u):
                a.wait_ge(c_stat.sem, c_stat.of(i, u))
                a.activation(sd[:, u:u + 1], mv[:, u, 1:2], ACT.Sqrt, bias=eps[:, 0:1]).then_inc(c_sd.sem, 1)
            return stats, recip, sqrt

        def project(weights, emit, stores, store_sp, per_out, now, later, begin=None):
            loaded = s_misc2.base + 16 * len(now)
            with scope() as st, block() as blk:
                h, hT = ring(st, "h"), ring(st, "hT")
                @blk.vector
                def _(v):
                    stats, recip, _ = norm_stages(v, None, lambda i, u: X[:, i * UN + u, :])

                    def finish(i, u):
                        if isinstance(i, int) and i * UN + u == 0:
                            v.wait_ge(s_misc2.sem, loaded)
                            if begin:
                                begin(v)
                        v.wait_ge(c_mm.sem, c_mm.of(i, u))
                        if stores:
                            v.wait_ge(s_st[u].sem, s_st[u].base + i * 16 * stores)
                        yield from emit(v, i, u)
                    staged(v, NT, UN, [(0, stats), (2, recip), (7, finish)], chain, 2 + per_out)

                @blk.scalar
                def _(a):
                    _, _, sqrt = norm_stages(None, a, None)

                    def relu(i, u):
                        a.wait_ge(c_norm.sem, c_norm.of(i, u))
                        a.wait_ge(c_T.sem, c_T.of(i - 1, u))
                        a.activation(h[:, u, :], X[:, i * UN + u, :], ACT.Relu, bias=nmr[:, bass.ds(i * UN + u, 1)],
                                     scale=rstd[:, bass.ds(i * UN + u, 1)]).then_inc(c_h.sem, 1)

                    def evac(i, u):
                        a.wait_ge(c_T.sem, c_T.of(i, u))
                        a.wait_ge(c_mm.sem, c_mm.of(i - 1, u))
                        a.activation(hT[:, u, :], ps_T(u), ACT.Copy).then_inc(c_hT.sem, 1)
                    staged(a, NT, UN, [(1, sqrt), (3, relu), (5, evac)])

                @blk.tensor
                def _(pe):
                    def turn(i, u):
                        pe.wait_ge(c_h.sem, c_h.of(i, u))
                        pe.wait_ge(c_hT.sem, c_hT.of(i, prior(u, TURNED)))
                        for k in range(KC):
                            t = pe.transpose(ps_T(u)[:, k * P:(k + 1) * P], h[:, u, k * P:(k + 1) * P], ident[:, :])
                        t.then_inc(c_T.sem, 1)

                    def multiply(i, u):
                        pe.wait_ge(c_hT.sem, c_hT.of(i, u))
                        pe.wait_ge(c_out.sem, c_out.of(i, prior(u, PRODUCT)))
                        for w, place in weights:
                            for k in range(KC):
                                m = pe.matmul(place(u), hT[:, u, k * P:(k + 1) * P], w(k), start=(k == 0), stop=(k == KC - 1))
                        m.then_inc(c_mm.sem, 1)
                    pe.wait_ge(s_misc2.sem, loaded)
                    staged(pe, NT, UN, [(4, turn), (6, multiply)])

                if stores:
                    @blk.sync
                    def _(sp):
                        for dest, source in now:
                            sp.dma_start(dest, source).then_inc(s_misc2.sem, 16)
                        for dest, source in later:
                            sp.dma_start(dest, source).then_inc(s_load, 16)
                            load_base[0] += 16

                        def store(i, u):
                            sp.wait_ge(c_out.sem, c_out.of(i, u))
                            store_sp(sp, i, u)
                        staged(sp, NT, UN, [(7, store)])
                        for u in range(UN):
                            sp.wait_ge(s_st[u].sem, s_st[u].base + (NT // UN) * 16 * stores)
            s_misc2.close(16 * len(now))
            for c in (c_stat, c_sd, c_norm, c_h, c_T, c_hT, c_mm, c_out):
                c.close(NT)
            for c in s_st:
                c.close((NT // UN) * 16 * stores)

        def max_pass(G, side, tiles, marks=None):
            with block() as blk:
                @blk.gpsimd
                def _(g):
                    if marks:
                        marks.pool(g)
                    side.start_pool(g)

                    def gather(i, b):
                        hold(g, "pool", c_eix.sem, c_eix.of(i, b, UB))
                        hold(g, "pool", s_hs[b].sem, s_hs[b].base + i * 16)
                        for k in range(J):
                            g.indirect_dma_start(G[b][:, k, :], None, tab, bass.IndirectOffsetOnAxis(ix[:, b, k:k + 1], 0),
                                                 bounds_check=NT * P - 1, oob_is_err=False).then_inc(s_eg[b].sem, 16)
                    staged(g, NB, UB, [(0, gather)])

                @blk.vector
                def _(v):
                    chain.link(v.memset(G[UB - 1][:, J - 1, :], 0.0))
                    for m in range(2):
                        v.tensor_copy(ix[:, m, 0:J], src_ix[:, m * J:(m + 1) * J]).then_inc(c_eix.sem, 1)
                    if marks:
                        marks.vector(v)
                    side.start(v)
                    done = [0]

                    def fold(k):
                        def stage(i, b):
                            n = i * UB + b
                            if k == 0:
                                v.wait_ge(s_eg[b].sem, s_eg[b].base + (i * (16 * J) + 16 * J))
                                if not is_first(i, b):
                                    v.wait_ge(c_batch.sem, c_batch.of(i, b - 1, UB))
                            before = G[b][:, k - 1, :] if k else G[(b - 1) % UB][:, J - 1, :]
                            ins = v.scalar_tensor_tensor(out=G[b][:, k, :], in0=before, scalar=reset[:, bass.ds(n * J + k, 1)],
                                                         in1=G[b][:, k, :], op0=ALU.add, op1=ALU.max)
                            if k == J - 1:
                                ins.then_inc(c_batch.sem, 1)
                            else:
                                done[0] = chain.inc(ins)
                        return stage

                    def folded(k):
                        def stage(i, b):
                            if k < J - 1:
                                v.wait_ge(chain.sem, done[0])
                            if k == 0:
                                v.tensor_copy(ix[:, (b + 2) % UB, 0:J], src_ix[:, bass.ds((i * UB + b) * J + 2 * J, J)]).then_inc(c_eix.sem, 1)
                        return stage
                    fillers, own = side.vector(v), {side.KEEP_AT: tiles.vector(v)}
                    stages = []
                    for k in range(J):
                        stages += [(0, fold(k))] + fillers.get(k, []) + own.get(k, []) + [(0, folded(k))]
                    staged(v, NB, UB, stages, chain, J - 1 + side.links)

                @blk.sync
                def _(sp):
                    if marks:
                        marks.sync(sp)

                    def store(i, b):
                        sp.wait_ge(c_batch.sem, c_batch.of(i, b, UB))
                        sp.dma_start(hist_p[:, bass.ds((i * UB + b) * J, J), :], G[b][:, :, :]).then_inc(s_hs[b].sem, 16)
                    staged(sp, NB, UB, tiles.sync(sp) + [(0, store)])
                    for b in range(UB):
                        sp.wait_ge(s_hs[b].sem, s_hs[b].base + (NB // UB) * 16)

                @blk.tensor
                def _(pe):
                    if marks:
                        marks.tensor(pe)
                    staged(pe, NB, UB, side.tensor(pe, *tiles.tensor(pe)))

                @blk.scalar
                def _(a):
                    fill, evac = tiles.scalar(a)
                    staged(a, NB, UB, fill + side.scalar(a, evac))
            c_eix.close(NB + 2)
            c_batch.close(NB)
            for b in range(UB):
                s_eg[b].close(NB // UB * 16 * J)
                s_hs[b].close(NB // UB * 16)
            if marks:
                marks.close()
            side.close()
            tiles.close()

        class LayerInput:

            def __init__(self, st, w, bias, from_x, to_x=None):
                self.w, self.bias, self.from_x, self.to_x = w, bias, from_x, to_x
                self.h, self.hT = sb(st, "h", [P, UB, D]), sb(st, "hT", [P, D])
                self.turned, self.product = bank[7][:, 0:D], bank[7][:, D:2 * D]

            def vector(self, v):
                def keep(i, b):
                    v.wait_ge(c_mm.sem, c_mm.of(i, b, UB))
                    v.tensor_tensor(U[:, i * UB + b, :], self.product, self.bias[:, :], ALU.add).then_inc(c_keep.sem, 1)

                def add_bias(i, b):
                    v.tensor_tensor(X[:, i * UB + b, :], X[:, i * UB + b, :], self.to_x[:, :], ALU.add)
                return [(1, keep, NT)] + ([(0, add_bias, NT)] if self.to_x is not None else [])

            def scalar(self, a):
                def relu(i, b):
                    a.wait_ge(c_T.sem, c_T.of(i - 1, b, UB))
                    a.activation(self.h[:, b, :], X[:, i * UB + b, :], ACT.Relu, bias=nmr[:, bass.ds(i * UB + b, 1)],
                                 scale=rstd[:, bass.ds(i * UB + b, 1)]).then_inc(c_h.sem, 1)

                def evac(i, b):
                    a.wait_ge(c_T.sem, c_T.of(i, b, UB))
                    a.activation(self.hT[:, :], self.turned, ACT.Copy).then_inc(c_hT.sem, 1)
                return [(0, relu, NT)] if self.from_x else [], (0, evac, NT)

            def sync(self, sp):
                def load(i, b):
                    sp.wait_ge(c_T.sem, c_T.of(i - 1, b, UB))
                    sp.dma_start(self.h[:, b, :], tab_t[bass.ds(i * UB + b, 1), :, :].rearrange("a p f -> p (a f)")).then_inc(s_tile[b].sem, 16)
                return [] if self.from_x else [(0, load, NT)]

            def tensor(self, pe):
                def turn(i, b):
                    if self.from_x:
                        pe.wait_ge(c_h.sem, c_h.of(i, b, UB))
                    else:
                        pe.wait_ge(s_tile[b].sem, s_tile[b].base + (i * 16 + 16))
                    pe.wait_ge(c_keep.sem, c_keep.of(i, b - 1, UB))
                    for k in range(KC):
                        t = pe.transpose(self.turned[:, k * P:(k + 1) * P], self.h[:, b, k * P:(k + 1) * P], ident[:, :])
                    t.then_inc(c_T.sem, 1)

                def multiply(i, b):
                    pe.wait_ge(c_hT.sem, c_hT.of(i, b, UB))
                    for k in range(KC):
                        m = pe.matmul(self.product, self.hT[:, k * P:(k + 1) * P], self.w[:, k, :], start=(k == 0), stop=(k == KC - 1))
                    m.then_inc(c_mm.sem, 1)
                return (0, turn, NT), (0, multiply, NT)

            def close(self):
                for c in (c_T, c_hT, c_mm, c_keep):
                    c.close(NT)
                if self.from_x:
                    c_h.close(NT)
                else:
                    for b in range(UB):
                        s_tile[b].close(len(range(b, NT, UB)) * 16)

        def is_first(i, b, k=0, first=1):
            return isinstance(i, int) and i * UB + b < first and k == 0

        def times(i, b, per, k=None):
            return i * (UB * per) + (b * per + (per if k is None else k))

        def spread_key(v, key, n, width):
            return key[:, bass.ds(n * J, J)][:, :, None].to_broadcast([P, J, width])

        def split_keys(v, key_ix, ti, lo, hi):
            chain.link(v.tensor_scalar(ti[:, :], key_ix[:, 0:CH], P - 1, None, ALU.bitwise_and))
            chain.link(v.tensor_copy(lo[:, :], ti[:, :]))
            chain.link(v.tensor_scalar(ti[:, :], key_ix[:, 0:CH], P.bit_length() - 1, None, ALU.logical_shift_right))
            chain.link(v.tensor_copy(hi[:, :], ti[:, :]))

        class Degrees:
            links = 0
            KEEP_AT = 4

            def __init__(self, st):
                self.cnt = [sb(st, "cnt", [P, NT]) for _ in range(2)]
                self.low = [sb(st, "low", [P, J, P], BF16) for _ in range(2)]
                self.high = [sb(st, "high", [P, J, NT], BF16) for _ in range(2)]
                self.iota = sb(st, "iota", [P, P], BF16)
                self.lo = [sb(st, "lo", [P, CH], BF16) for _ in range(2)]
                self.hi = [sb(st, "hi", [P, CH], BF16) for _ in range(2)]
                self.oh, self.mm, self.added = sem("deg_oh"), sem("deg_mm"), sem("deg_added")
                self.ti = sb(st, "ti", [P, CH], I32)
                self.const0 = const_base[0]
                const_base[0] += 1

            def start_pool(self, g):
                g.iota(self.ti[:, 0:P], [[1, P]], base=0, channel_multiplier=0).then_inc(s_const, 1)

            def start(self, v):
                v.wait_ge(s_const, self.const0 + 1)
                chain.link(v.tensor_copy(self.iota[:, :], self.ti[:, 0:P]))
                for k, key in enumerate((dst_ix, src_ix)):
                    chain.inc(v.memset(self.cnt[k][:, :], 0.0))
                    split_keys(v, key, self.ti, self.lo[k], self.hi[k])

            def vector(self, v):
                def add(i, b):
                    v.wait_ge(self.mm, times(i, b, 1))
                    for k in range(2):
                        v.tensor_tensor(self.cnt[k][:, :], bank[k][:, 0:NT], self.cnt[k][:, :], ALU.add).then_inc(self.added, 1)

                def make(to, key, width):
                    def stage(i, b):
                        v.tensor_tensor(to[:, :, :], self.iota[:, None, 0:width].to_broadcast([P, J, width]),
                                        spread_key(v, key, i * UB + b, width), ALU.is_equal).then_inc(self.oh, 1)
                    return stage
                return {2: [(1, add)], 3: [(0, make(self.low[0], self.lo[0], P))], 4: [(0, make(self.high[0], self.hi[0], NT))],
                        5: [(0, make(self.low[1], self.lo[1], P))], 6: [(0, make(self.high[1], self.hi[1], NT))]}

            def tensor(self, pe, turn_tile, multiply_tile):
                def count(i, b):
                    pe.wait_ge(self.oh, times(i, b, 4))
                    if not is_first(i, b):
                        pe.wait_ge(self.added, times(i, b - 1, 2))
                    for n in range(2):
                        for k in range(J):
                            m = pe.matmul(bank[n][:, 0:NT], self.low[n][:, k, :], self.high[n][:, k, :], start=(k == 0), stop=(k == J - 1))
                    m.then_inc(self.mm, 1)
                return [turn_tile, (0, count), multiply_tile]

            def scalar(self, a, evac):
                return [evac]

            def close(self):
                pass

        class Ranks:
            links = 0
            KEEP_AT = 4

            def __init__(self, st, place):
                self.place = place
                self.low = [sb(st, "low", [P, J, P], BF16) for _ in range(UB)]
                self.high = [sb(st, "high", [P, J, NT], BF16) for _ in range(UB)]
                self.lowT = [sb(st, "lowT", [P, J, P]) for _ in range(UB)]
                self.lowTb = sb(st, "lowTb", [P, J, P], BF16)
                self.same = sb(st, "same", [P, J, P], BF16)
                self.next = [sb(st, "next", [P, J + 1, NT]) for _ in range(UB)]
                self.first = sb(st, "first", [P, NT])
                self.iota = sb(st, "iota", [P, P], BF16)
                self.identb = sb(st, "identb", [P, P], BF16)
                self.upper = sb(st, "upper", [P, P])
                self.pick = sb(st, "pick", [P, J, NT])
                self.lo, self.hi = sb(st, "lo", [P, CH], BF16), sb(st, "hi", [P, CH], BF16)
                self.c = {n: sem("rank_" + n) for n in ("oh", "turn", "lowT", "pair", "same", "count", "next", "sum", "pick", "place")}
                self.const0 = const_base[0]
                const_base[0] += 2
                self.ti = self.lowT[0][:, :, :].rearrange("p k e -> p (k e)")[:, 0:CH].bitcast(I32)

            def start_pool(self, g):
                g.iota(self.ti[:, 0:P], [[1, P]], base=0, channel_multiplier=0).then_inc(s_const, 1)
                g.affine_select(out=self.upper[:, :], in_=ones[:, :], compare_op=ALU.is_gt, fill=0.0, base=0,
                                pattern=[[1, P]], channel_multiplier=-1).then_inc(s_const, 1)

            def start(self, v):
                v.wait_ge(s_const, self.const0 + 2)
                chain.inc(v.tensor_copy(self.identb[:, :], ident[:, :]))
                chain.link(v.tensor_copy(self.iota[:, :], self.ti[:, 0:P]))
                chain.link(v.tensor_tensor(self.first[:, :], rows_upto[:, :], rows_own[:, :], ALU.subtract))
                chain.link(v.tensor_scalar(self.first[:, :], self.first[:, :], float(SLOT), None, ALU.mult))
                split_keys(v, src_ix, self.ti, self.lo, self.hi)

            def vector(self, v):
                c = self.c

                def make_low(i, b):
                    v.tensor_tensor(self.low[b][:, :, :], self.iota[:, None, :].to_broadcast([P, J, P]),
                                    spread_key(v, self.lo, i * UB + b, P), ALU.is_equal).then_inc(c["oh"], 1)

                def make_high(i, b):
                    v.tensor_tensor(self.high[b][:, :, :], self.iota[:, None, 0:NT].to_broadcast([P, J, NT]),
                                    spread_key(v, self.hi, i * UB + b, NT), ALU.is_equal).then_inc(c["oh"], 1)

                def mask(q):
                    def stage(i, b):
                        k, n = 4 * q, min(4, J - 4 * q)
                        if q == 0:
                            v.wait_ge(c["pair"], times(i, b, 1))
                        v.tensor_tensor(self.same[:, k:k + n, :], bank[2 + q][:, 0:n * P].rearrange("p (k e) -> p k e", e=P),
                                        self.upper[:, None, :].to_broadcast([P, n, P]), ALU.mult).then_inc(c["same"], 1)
                    return stage

                def choose(i, b):
                    v.wait_ge(c["sum"], times(i, b, 1))
                    if not is_first(i, b):
                        v.wait_ge(c["place"], times(i, b - 1, 1))
                    v.tensor_tensor(self.pick[:, :, :], bank[5][:, 0:J * NT].rearrange("p (k t) -> p k t", t=NT),
                                    self.high[b][:, :, :], ALU.mult).then_inc(c["pick"], 1)

                def chosen(i, b):
                    v.wait_ge(c["pick"], times(i, b, 1))
                    v.tensor_reduce(self.place[:, bass.ds((i * UB + b) * J, J)], self.pick[:, :, :], AX.X, ALU.add).then_inc(c["place"], 1)
                return {0: [(3, choose)], 1: [(2, mask(0))], 2: [(2, mask(1))], 3: [(2, mask(2))],
                        4: [(3, chosen)], 5: [(0, make_low)], 6: [(0, make_high)]}

            def scalar(self, a, evac):
                c = self.c

                def copy_low(i, b):
                    a.wait_ge(c["turn"], times(i, b, 1))
                    if not is_first(i, b):
                        a.wait_ge(c["pair"], times(i, b - 1, 1))
                    for to in (self.lowTb, self.lowT[b]):
                        for k in range(0, J, 8):
                            n = min(8, J - k)
                            m = a.activation(to[:, k:k + n, :], self.bf(k // 8)[:, 0:n * P].rearrange("p (k e) -> p k e", e=P), ACT.Copy)
                            m.then_inc(c["lowT"], 1)

                def copy_next(i, b):
                    a.wait_ge(c["count"], times(i, b, 1))
                    a.activation(self.next[b][:, :, :], bank[6][:, 0:(J + 1) * NT].rearrange("p (k t) -> p k t", t=NT), ACT.Copy).then_inc(c["next"], 1)
                return [evac, (0, copy_next), (0, copy_low)]

            def bf(self, n):
                return bank[n][:, :].bitcast(BF16)

            def tensor(self, pe, turn_tile, multiply_tile):
                c = self.c

                def count(i, b):
                    pe.wait_ge(c["oh"], times(i, b, 2))
                    before = self.first[:, :]
                    if not is_first(i, b):
                        pe.wait_ge(c["next"], times(i, b - 1, 1))
                        before = self.next[(b - 1) % UB][:, J, :]
                    pe.matmul(bank[6][:, 0:(J + 1) * NT], ident[:, :], before[:, None, :].to_broadcast([P, J + 1, NT]), start=True, stop=False,
                              skip_group_check=True)
                    for k in range(J):
                        m = pe.matmul(bank[6][:, (k + 1) * NT:(J + 1) * NT], self.low[b][:, k, :],
                                      self.high[b][:, k:k + 1, :].to_broadcast([P, J - k, NT]), start=False, stop=(k == J - 1),
                                      skip_group_check=True)
                    m.then_inc(c["count"], 1)

                def turn(i, b):
                    if not is_first(i, b):
                        pe.wait_ge(c["lowT"], times(i, b - 1, 4))
                    for k in range(J):
                        t = pe.transpose(self.bf(k // 8)[:, (k % 8) * P:(k % 8 + 1) * P], self.low[b][:, k, :], self.identb[:, :])
                    t.then_inc(c["turn"], 1)

                def pair(i, b):
                    pe.wait_ge(c["lowT"], times(i, b, 4))
                    if not is_first(i, b):
                        pe.wait_ge(c["same"], times(i, b - 1, 3))
                    for k in range(J):
                        t = pe.matmul(bank[2 + k // 4][:, (k % 4) * P:(k % 4 + 1) * P], self.lowTb[:, k, :], self.lowTb[:, k, :],
                                      start=True, stop=True)
                    t.then_inc(c["pair"], 1)

                def add_up(i, b):
                    pe.wait_ge(c["next"], times(i, b, 1))
                    if not is_first(i, b):
                        pe.wait_ge(c["pick"], times(i, b - 1, 1))
                    for k in range(J):
                        if k % 4 == 0:
                            pe.wait_ge(c["same"], times(i, b, 3, k // 4 + 1))
                        to = bank[5][:, k * NT:(k + 1) * NT]
                        pe.matmul(to, self.same[:, k, :], self.high[b][:, k, :], start=True, stop=False)
                        m = pe.matmul(to, self.lowT[b][:, k, :], self.next[b][:, k, :], start=False, stop=True)
                    m.then_inc(c["sum"], 1)
                return [(2, add_up), (1, pair), turn_tile, (0, count), (0, turn), multiply_tile]

            def close(self):
                pass

        class Permute:
            links = 1
            KEEP_AT = 7
            RG = 3

            def __init__(self, st, place):
                self.row, self.lo, self.hi = (sb(st, n, [P, CH], BF16) for n in ("row", "lo", "hi"))
                self.off = sb(st, "off", [P, CH])
                self.iota = sb(st, "iota", [P, SL + 1])
                self.iotab = sb(st, "iotab", [P, P], BF16)
                self.rows_made, self.signs_made, self.mm = sem("perm_rows"), sem("perm_signs"), sem("perm_mm")
                self.ready = sem("perm_ready")
                self.cuts = ((0, 512), (512, SL + 1))
                self.signs = sb(st, "signs", [P, self.RG, SL + 1], BF16)
                self.hot = sb(st, "hot", [P, J, P], BF16)
                work = sb(st, "work", [P, 4 * (SL + 1)])
                self.vals = work[:, 0:UB * J * P].bitcast(BF16).rearrange("p (b m k e) -> p b m k e", b=UB, m=2, k=J)
                self.ti, self.tf, self.quot, self.rest = (work[:, n * (SL + 1):(n + 1) * (SL + 1)] for n in range(4))
                self.ti = self.ti.bitcast(I32)
                self.rank_place = place
                self.const0 = const_base[0]
                const_base[0] += 1

            def start_pool(self, g):
                g.iota(self.ti[:, :], [[1, SL + 1]], base=-1, channel_multiplier=0).then_inc(s_const, 1)

            def start(self, v):
                ti, tf, quot, rest = (t[:, 0:CH] for t in (self.ti, self.tf, self.quot, self.rest))
                v.wait_ge(s_const, self.const0 + 1)
                chain.inc(v.tensor_copy(self.iotab[:, :], self.ti[:, 1:P + 1]))
                chain.link(v.tensor_copy(self.iota[:, :], self.ti[:, :]))
                split_keys(v, dst_ix, ti, self.lo, self.hi)
                chain.link(v.tensor_scalar(self.lo[:, :], self.lo[:, :], 1.0, None, ALU.add))
                divide(v, self.rank_place[:, :], SL, quot, rest, ti, tf)
                chain.link(v.tensor_copy(self.row[:, :], quot))
                chain.link(v.tensor_scalar(self.off[:, :], rest, -1.0, 0.5, ALU.mult, ALU.add))
                v.sem_inc(self.ready, 1)

            def vector(self, v):
                def make(i, b):
                    chain.inc(v.tensor_tensor(self.hot[:, :, :], self.iotab[:, None, :].to_broadcast([P, J, P]),
                                              spread_key(v, self.row, i * UB + b, P), ALU.is_equal))

                def value(m, key):
                    def stage(i, b):
                        if m == 0 and not is_first(i, b, 0, UB):
                            v.wait_ge(self.mm, times(i - 1, b, J))
                        v.tensor_tensor(self.vals[:, b, m, :, :], self.hot[:, :, :], spread_key(v, key, i * UB + b, P),
                                        ALU.mult).then_inc(self.rows_made, 1)
                    return stage
                return {0: [(0, make)], 2: [(0, value(0, self.lo))], 4: [(0, value(1, self.hi))]}

            def scalar(self, a, evac):
                def sign(ks):
                    def stage(i, b):
                        for k in ks:
                            r = k % self.RG
                            if is_first(i, b, k):
                                a.wait_ge(self.ready, 1)
                            if not (is_first(i, b) and k < self.RG):
                                a.wait_ge(self.mm, times(i, b, J, k - self.RG + 1))
                            a.activation(self.signs[:, r, :], self.iota[:, :], ACT.Sign,
                                         bias=self.off[:, bass.ds((i * UB + b) * J + k, 1)]).then_inc(self.signs_made, 1)
                    return stage
                return [(0, sign(range(0, 7))), evac, (0, sign(range(7, J)))]

            def tensor(self, pe, turn_tile, multiply_tile):
                def put(ks):
                    def stage(i, b):
                        pe.wait_ge(self.rows_made, times(i, b, 2))
                        for k in ks:
                            r = k % self.RG
                            pe.wait_ge(self.signs_made, times(i, b, J, k + 1))
                            for m in range(2):
                                for half, (c0, c1) in enumerate(self.cuts):
                                    t = pe.matmul(bank[2 * m + half][:, 0:c1 - c0], self.vals[:, b, m, k, :], self.signs[:, r, c0:c1],
                                                  start=is_first(i, b, k), stop=True, skip_group_check=True)
                            t.then_inc(self.mm, 1)
                    return stage
                return [(0, put(range(0, 5))), turn_tile, (0, put(range(5, J))), multiply_tile]

            def close(self):
                total = self.iota
                with block() as blk:
                    @blk.vector
                    def _(v):
                        for half, (c0, c1) in enumerate(self.cuts):
                            chain.link(v.tensor_copy(total[:, c0:c1], bank[half][:, 0:c1 - c0]))
                            chain.link(v.scalar_tensor_tensor(out=total[:, c0:c1], in0=bank[2 + half][:, 0:c1 - c0], scalar=float(P),
                                                              in1=total[:, c0:c1], op0=ALU.mult, op1=ALU.add))
                        chain.link(v.tensor_scalar(total[:, :], total[:, :], 0.5, None, ALU.mult))
                        chain.link(v.tensor_tensor(dst_ix[:, 0:SL], total[:, 1:SL + 1], total[:, 0:SL], ALU.subtract))

        def divide(v, a, by, quot, rest, ti, tf):
            chain.link(v.tensor_scalar(tf, a, 1.0 / by, None, ALU.mult))
            chain.link(v.tensor_copy(ti, tf))
            chain.link(v.tensor_copy(quot, ti))
            chain.link(v.scalar_tensor_tensor(out=rest, in0=quot, scalar=-float(by), in1=a, op0=ALU.mult, op1=ALU.add))
            for op, bound, step in ((ALU.is_lt, 0.0, -1.0), (ALU.is_ge, float(by), 1.0)):
                chain.link(v.tensor_scalar(tf, rest, bound, step, op, ALU.mult))
                chain.link(v.tensor_tensor(quot, quot, tf, ALU.add))
                chain.link(v.scalar_tensor_tensor(out=rest, in0=tf, scalar=-float(by), in1=rest, op0=ALU.mult, op1=ALU.add))

        class RowNodes:
            def __init__(self, st):
                self.iota = sb(st, "iota", [P, RP], BF16)
                self.all1 = sb(st, "all1", [P, RP], BF16)
                self.eq, self.gt = (sb(st, n, [P, UN, P], BF16) for n in ("eq", "gt"))
                self.ge = sb(st, "ge", [P, UN, RP], BF16)
                self.made, self.mm = Count(sem("node_made"), 0), Count(sem("node_mm"), 0)
                self.total = bank[7][:, 0:RP]
                self.ti = sb(st, "ti", [P, RP], I32)
                self.const0 = const_base[0]
                const_base[0] += 1

            def pool(self, g):
                g.iota(self.ti[:, :], [[1, RP]], base=0, channel_multiplier=0).then_inc(s_const, 1)

            def start(self, v):
                v.wait_ge(s_const, self.const0 + 1)
                chain.inc(v.memset(self.all1[:, :], 1.0))
                chain.link(v.tensor_copy(self.iota[:, :], self.ti[:, :]))

            def vector(self, v):
                def make(i, u):
                    if not (isinstance(i, int) and i == 0):
                        v.wait_ge(self.mm.sem, self.mm.of(i - 1, u))
                    tile = bass.ds(i * UN + u, 1)
                    for to, key, op, width in ((self.gt, end_row, ALU.is_gt, P), (self.eq, end_row, ALU.is_equal, P),
                                               (self.ge, end_col, ALU.is_ge, RP)):
                        v.tensor_scalar(to[:, u, :], self.iota[:, 0:width], key[:, tile], None, op).then_inc(self.made.sem, 1)
                return [(0, make)]

            def tensor(self, pe):
                def count(i, u):
                    pe.wait_ge(self.made.sem, self.made.base + (i * (UN * 3) + (u + 1) * 3))
                    first = isinstance(i, int) and i * UN + u == 0
                    pe.matmul(self.total, self.gt[:, u, :], self.all1[:, :], start=first, stop=True, skip_group_check=True)
                    pe.matmul(self.total, self.eq[:, u, :], self.ge[:, u, :], start=False, stop=True,
                              skip_group_check=True).then_inc(self.mm.sem, 1)
                return [(1, count)]

            def finish(self, v):
                v.wait_ge(self.mm.sem, self.mm.base + NT)
                chain.link(v.tensor_scalar(row_node[:, 0:RP], self.total, float(PAD), None, ALU.min))

        def empty_slots(empty):
            with scope() as st, block() as blk:
                slot = sb(st, "slot", [P, SL])

                @blk.vector
                def _(v):
                    chain.link(v.tensor_copy(slot[:, :], dst_ix[:, 0:SL]))
                    chain.link(v.tensor_scalar(empty[:, :], slot[:, :], 0.0, NEG, ALU.is_equal, ALU.mult))
                    chain.link(v.tensor_scalar(slot[:, :], slot[:, :], -1.0, 0.0, ALU.add, ALU.max))
                    chain.link(v.tensor_copy(dst_ix[:, 0:SL], slot[:, :]))

        def find_rows(degrees):
            by_dst, by_src = degrees.cnt
            with ExitStack() as st, block() as blk:
                upto = sb(st, "upto", [P, P])
                tot, cum, has = sb(st, "tot", [P, 2, NT]), sb(st, "cum", [P, 2, NT]), sb(st, "has", [P, NT])
                ti = sb(st, "ti", [P, NT], I32)
                const0 = const_base[0]
                const_base[0] += 1

                @blk.gpsimd
                def _(g):
                    g.affine_select(out=upto[:, :], in_=ones[:, :], compare_op=ALU.is_ge, fill=0.0, base=0,
                                    pattern=[[1, P]], channel_multiplier=-1).then_inc(s_const, 1)

                @blk.tensor
                def _(pe):
                    pe.wait_ge(s_const, const0 + 1)
                    pe.wait_ge(s_dve.sem, s_dve.base + 1)
                    for k, own in enumerate((by_dst, rows_own)):
                        pe.matmul(bank[2 * k][:, 0:NT], upto[:, :], own[:, :], start=True, stop=True)
                        m = pe.matmul(bank[2 * k + 1][:, 0:NT], ones[:, :], own[:, :], start=True, stop=True)
                    m.then_inc(s_pe.sem, 1)

                @blk.vector
                def _(v):
                    chain.link(v.tensor_scalar(ti[:, :], by_src[:, :], SLOT - 1.0, None, ALU.add))
                    chain.link(v.tensor_scalar(ti[:, :], ti[:, :], SLOT.bit_length() - 1, None, ALU.logical_shift_right))
                    chain.link(v.tensor_copy(rows_own[:, :], ti[:, :]))
                    v.sem_inc(s_dve.sem, 1)
                    v.wait_ge(s_pe.sem, s_pe.base + 1)
                    for k, (own, none, dest) in enumerate(((by_dst, EMPTY, node_ix), (rows_own, NOROW, node_ix2))):
                        c, t = cum[:, k, :], tot[:, k, :]
                        chain.link(v.tensor_copy(t, bank[2 * k + 1][:, 0:NT]))
                        chain.link(v.tensor_tensor_scan(c, ones[:, 0:NT], t, 0.0, ALU.mult, ALU.add))
                        chain.link(v.tensor_tensor(c, c, t, ALU.subtract))
                        chain.link(v.tensor_tensor(c, bank[2 * k][:, 0:NT], c, ALU.add))
                        if k:
                            chain.inc(v.tensor_copy(rows_upto[:, :], c))
                        chain.link(v.tensor_scalar(has[:, :], own[:, :], 0.0, None, ALU.is_gt))
                        chain.link(v.tensor_scalar(c, c, -1.0 - none, None, ALU.add))
                        chain.link(v.tensor_tensor(c, c, has[:, :], ALU.mult))
                        chain.link(v.tensor_scalar(c, c, float(none), float(none), ALU.add, ALU.min))
                        chain.link(v.tensor_copy(dest[:, :], c))
                    divide(v, rows_upto[:, :], RP, end_row[:, :], end_col[:, :], ti[:, :], has[:, :])
            s_dve.close(1)
            s_pe.close(1)

        def carry_max(G):
            last = G[UB - 1][:, J - 1, :]
            with ExitStack() as st, block() as blk:
                scanned = sb(st, "scanned", [P, KC, P])
                found = sb(st, "found", [P, D])
                m0 = s_misc.base

                @blk.tensor
                def _(pe):
                    for k in range(KC):
                        t = pe.transpose(bank[0][:, k * P:(k + 1) * P], last[:, k * P:(k + 1) * P], ident[:, :])
                    t.then_inc(s_pe.sem, 1)
                    pe.wait_ge(s_dve.sem, s_dve.base + 2)
                    for k in range(KC):
                        t = pe.transpose(bank[1][:, k * P:(k + 1) * P], scanned[:, k, :], ident[:, :])
                    t.then_inc(s_pe.sem, 1)

                @blk.vector
                def _(v):
                    chain.link(v.memset(found[:, :], 0.0))
                    v.sem_inc(s_dve.sem, 1)
                    chain.link(v.memset(scanned[:, :, 0:1], NEG))
                    v.wait_ge(s_pe.sem, s_pe.base + 1)
                    for k in range(KC):
                        chain.link(v.tensor_tensor_scan(scanned[:, k, 1:P], Rrow[:, 0:P - 1], bank[0][:, k * P:(k + 1) * P - 1],
                                                        NEG, ALU.add, ALU.max))
                    v.sem_inc(s_dve.sem, 1)
                    v.wait_ge(s_pe.sem, s_pe.base + 2)
                    v.wait_ge(s_misc.sem, m0 + 16)
                    chain.link(v.tensor_tensor(found[:, :], bank[1][:, 0:D], found[:, :], ALU.max))
                    v.sem_inc(s_dve.sem, 1)

                @blk.gpsimd
                def _(g):
                    g.wait_ge(s_dve.sem, s_dve.base + 1)
                    g.indirect_dma_start(found[:, :], None, hist, bass.IndirectOffsetOnAxis(fix_ix[:, 0:1], 0),
                                         bounds_check=EMPTY - 1, oob_is_err=False).then_inc(s_misc.sem, 16)
                    g.wait_ge(s_dve.sem, s_dve.base + 3)
                    g.indirect_dma_start(hist, bass.IndirectOffsetOnAxis(fix_ix[:, 0:1], 0), found[:, :], None,
                                         bounds_check=EMPTY - 1, oob_is_err=False).then_inc(s_misc.sem, 16)
                    g.wait_ge(s_misc.sem, m0 + 32)
            s_pe.close(2)
            s_dve.close(3)
            s_misc.close(32)

        def node_gathers(blk, pool, table, width, last, nodes=None):
            @blk.gpsimd
            def _(g):
                if nodes:
                    nodes.pool(g)

                def gather(i, u):
                    hold(g, "pool", c_ix.sem, c_ix.of(i, u))
                    hold(g, "pool", c_T.sem, c_T.of(i - 1, u))
                    g.indirect_dma_start(pool[:, u, 0:width], None, table, bass.IndirectOffsetOnAxis(nix[:, u:u + 1], 0),
                                         bounds_check=last, oob_is_err=False).then_inc(s_gat[u].sem, 16)
                staged(g, NT, UN, [(0, gather)])

        def place_ix(v, rows_of):
            def stage(i, u):
                v.wait_ge(s_gat[u].sem, s_gat[u].base + i * 16)
                v.tensor_copy(nix[:, u:u + 1], rows_of[:, bass.ds(i * UN + u, 1)]).then_inc(c_ix.sem, 1)
            return stage

        def combine(U, w, gain, bias, to_table, beside=None):
            residual = gain is not None
            with scope() as st, block() as blk:
                hT, o, y, pool = (ring(st, n) for n in ("hT", "o", "y", "pool"))
                if residual:
                    cur = ring(st, "cur")
                nodes = beside(st) if beside else None
                node_gathers(blk, pool, hist, D, EMPTY, nodes)
                final = c_out if residual else c_z
                store_at = 11 if residual else 7

                def small(u):
                    return bank[2 + TURNED[u]][:, 0:D]

                @blk.vector
                def _(v):
                    stats, recip, _ = norm_stages(v, None, lambda i, u: y[:, u, :])

                    def join(i, u):
                        v.wait_ge(c_mm.sem, c_mm.of(i, u))
                        v.wait_ge(c_z.sem, c_z.of(i - 1, u))
                        if residual:
                            v.wait_ge(s_cur[u].sem, s_cur[u].base + (i * 16 + 16))
                            v.scalar_tensor_tensor(out=y[:, u, :], in0=small(u), scalar=0.0, in1=cur[:, u, :],
                                                   op0=ALU.max, op1=ALU.add).then_inc(c_y.sem, 1)
                        else:
                            v.tensor_tensor(y[:, u, :], small(u), U[:, i * UN + u, :], ALU.add).then_inc(c_y.sem, 1)

                    def stats_y(i, u):
                        v.wait_ge(c_y.sem, c_y.of(i, u))
                        yield from stats(i, u)

                    def scale(i, u):
                        v.wait_ge(c_z.sem, c_z.of(i, u))
                        at = chain.inc(v.tensor_tensor(o[:, u, :], o[:, u, :], gain[:, :], ALU.mult))
                        yield
                        v.wait_ge(chain.sem, at)
                        if to_table:
                            v.tensor_tensor(o[:, u, :], o[:, u, :], bias[:, :], ALU.add).then_inc(c_out.sem, 1)
                        else:
                            v.tensor_tensor(X[:, i * UN + u, :], o[:, u, :], X[:, i * UN + u, :], ALU.add).then_inc(c_out.sem, 1)

                    stages = [(0, place_ix(v, node_ix)), (5, join)]
                    if residual:
                        stages += [(6, stats_y), (8, recip), (10, scale)]
                    if nodes:
                        nodes.start(v)
                        stages += nodes.vector(v)
                    staged(v, NT, UN, stages, chain, residual * 3)
                    if nodes:
                        nodes.finish(v)

                @blk.scalar
                def _(a):
                    _, _, sqrt = norm_stages(None, a, None)

                    def evac(i, u):
                        a.wait_ge(c_T.sem, c_T.of(i, u))
                        a.wait_ge(c_mm.sem, c_mm.of(i - 1, u))
                        a.activation(hT[:, u, :], ps_T(u), ACT.Copy).then_inc(c_hT.sem, 1)

                    def free_o(i, u):
                        if to_table:
                            a.wait_ge(s_st[u].sem, s_st[u].base + i * 16)
                        else:
                            a.wait_ge(c_out.sem, c_out.of(i - 1, u))

                    def relu(i, u):
                        a.wait_ge(c_y.sem, c_y.of(i, u))
                        free_o(i, u)
                        a.activation(o[:, u, :], y[:, u, :], ACT.Relu).then_inc(c_z.sem, 1)

                    def normal(i, u):
                        a.wait_ge(c_norm.sem, c_norm.of(i, u))
                        free_o(i, u)
                        a.activation(o[:, u, :], y[:, u, :], ACT.Identity, bias=nmr[:, bass.ds(i * UN + u, 1)],
                                     scale=rstd[:, bass.ds(i * UN + u, 1)]).then_inc(c_z.sem, 1)

                    staged(a, NT, UN, [(3, evac)] + ([(7, sqrt), (9, normal)] if residual else [(6, relu)]))

                @blk.tensor
                def _(pe):
                    def turn(i, u):
                        pe.wait_ge(s_gat[u].sem, s_gat[u].base + (i * 16 + 16))
                        pe.wait_ge(c_hT.sem, c_hT.of(i, prior(u, TURNED)))
                        for k in range(KC):
                            t = pe.transpose(ps_T(u)[:, k * P:(k + 1) * P], pool[:, u, k * P:(k + 1) * P], ident[:, :])
                        t.then_inc(c_T.sem, 1)

                    def multiply(i, u):
                        pe.wait_ge(c_hT.sem, c_hT.of(i, u))
                        pe.wait_ge(c_y.sem, c_y.of(i, prior(u, TURNED)))
                        if residual:
                            pe.matmul(small(u), ident[:, :], U[:, i * UN + u, :], start=True, stop=False)
                        for k in range(KC):
                            m = pe.matmul(small(u), hT[:, u, k * P:(k + 1) * P], w[:, k, :], start=(k == 0 and not residual), stop=(k == KC - 1))
                        m.then_inc(c_mm.sem, 1)

                    staged(pe, NT, UN, [(2, turn), (4, multiply)] + (nodes.tensor(pe) if nodes else []))

                if residual or to_table:
                    @blk.sync
                    def _(sp):
                        def load(i, u):
                            sp.wait_ge(c_y.sem, c_y.of(i - 1, u))
                            sp.dma_start(cur[:, u, :], tab_t[bass.ds(i * UN + u, 1), :, :].rearrange("a p f -> p (a f)")).then_inc(s_cur[u].sem, 16)

                        def store(i, u):
                            sp.wait_ge(final.sem, final.of(i, u))
                            sp.dma_start(tab_t[bass.ds(i * UN + u, 1), :, :].rearrange("a p f -> p (a f)"), o[:, u, :]).then_inc(s_st[u].sem, 16)
                        staged(sp, NT, UN, ([(0, load)] if residual else []) + ([(store_at, store)] if to_table else []))
                        if to_table:
                            for u in range(UN):
                                sp.wait_ge(s_st[u].sem, s_st[u].base + NT // UN * 16)
            for c in (c_ix, c_T, c_hT, c_mm, c_y, c_z):
                c.close(NT)
            if residual:
                for c in (c_stat, c_sd, c_norm, c_out):
                    c.close(NT)
            for u in range(UN):
                s_gat[u].close(NT // UN * 16)
                s_cur[u].close(NT // UN * 16 * residual)
                s_st[u].close(NT // UN * 16 * to_table)

        def attention_pass(st, state, empty):
            kvs = [sb(st, f"kv{b}", [P, R * SLOT, KV]) for b in range(UB)]
            qs = [sb(st, f"q{b}", [P, R, D]) for b in range(UB)]
            s = sb(st, "s", [P, R, SLOT, HEADS])
            row_max = sb(st, "row_max", [P, R, HEADS])
            w = sb(st, "w", [P, UB, R * SLOT + R, HEADS])
            tmp = sb(st, "tmp", [P, ACC])
            c_weighted, c_summed = sem("att_weighted"), sem("att_summed")
            GATHERS = R * SLOT + R
            EXPS = R + 1

            def ps_row(b, r):
                return bank[(b * R + r) % 8][:, 0:ACC]

            def heads(ap):
                return ap.rearrange("p (d h) -> p d h", h=HEADS)

            with block() as blk:
                @blk.gpsimd
                def _(g):
                    def gather(i, b):
                        hold(g, "pool", c_eix.sem, c_eix.base + times(i, b, 2))
                        for r in range(R):
                            g.indirect_dma_start(qs[b][:, r, :], None, qtab, bass.IndirectOffsetOnAxis(ix[:, b, R * SLOT + r:R * SLOT + r + 1], 0),
                                                 bounds_check=NT * P - 1, oob_is_err=False).then_inc(s_eg[b].sem, 16)
                        for k in range(R * SLOT):
                            g.indirect_dma_start(kvs[b][:, k, :], None, kvtab, bass.IndirectOffsetOnAxis(ix[:, b, k:k + 1], 0),
                                                 bounds_check=NT * P - 1, oob_is_err=False).then_inc(s_eg[b].sem, 16)
                    staged(g, NBA, UB, [(0, gather)])

                @blk.vector
                def _(v):
                    def place(b, n):
                        v.tensor_copy(ix[:, b, 0:R * SLOT], dst_ix[:, bass.ds(n * (R * SLOT), R * SLOT)]).then_inc(c_eix.sem, 1)
                        v.tensor_copy(ix[:, b, R * SLOT:R * SLOT + R], row_node[:, bass.ds(n * R, R)]).then_inc(c_eix.sem, 1)
                    chain.link(v.memset(state[UB - 1][:, R - 1, :], 0.0))
                    for m in range(UB):
                        place(m, m)

                    def score(i, b):
                        n = i * UB + b
                        kv, q, top_m = kvs[b], qs[b], state[b][:, :, ACC:STATE]
                        v.wait_ge(s_eg[b].sem, s_eg[b].base + (i * (16 * GATHERS) + 16 * GATHERS))
                        v.wait_ge(s_hs[b].sem, s_hs[b].base + i * 16)
                        keys = kv[:, :, 0:D].rearrange("p (r e) f -> p r e f", e=SLOT)
                        chain.link(v.tensor_tensor(keys, keys, q[:, :, None, :].to_broadcast([P, R, SLOT, D]), ALU.mult))
                        chain.link(v.tensor_reduce(s[:, :, :, :].rearrange("p r e h -> p (r e) h"),
                                                   kv[:, :, 0:D].rearrange("p k (d h) -> p k h d", h=HEADS), AX.X, ALU.add))
                        flat = s[:, :, :, :].rearrange("p r e h -> p (r e) h")
                        chain.link(v.tensor_tensor(flat, flat, empty[:, bass.ds(n * (R * SLOT), R * SLOT)][:, :, None]
                                                   .to_broadcast([P, R * SLOT, HEADS]), ALU.add))
                        chain.link(v.tensor_reduce(row_max[:, :, :], s[:, :, :, :].rearrange("p r e h -> p r h e"), AX.X, ALU.max))

                        def before(r):
                            return top_m[:, r - 1, :] if r else state[(b - 1) % UB][:, R - 1, ACC:STATE]
                        for r in range(R):
                            chain.link(v.scalar_tensor_tensor(out=top_m[:, r, :], in0=before(r), scalar=row_reset[:, bass.ds(n * R + r, 1)],
                                                              in1=row_max[:, r, :], op0=ALU.add, op1=ALU.max))
                        for r in range(R):
                            v.scalar_tensor_tensor(out=w[:, b, R * SLOT + r, :], in0=before(r), scalar=row_reset[:, bass.ds(n * R + r, 1)],
                                                   in1=top_m[:, r, :], op0=ALU.add, op1=ALU.subtract).then_inc(c_w.sem, 1)
                        v.tensor_tensor(w[:, b, 0:R * SLOT, :].rearrange("p (r e) h -> p r e h", e=SLOT), s[:, :, :, :],
                                        top_m[:, :, None, :].to_broadcast([P, R, SLOT, HEADS]), ALU.subtract).then_inc(c_w.sem, 1)

                    def weigh(i, b, r):
                        vals = kvs[b][:, r * SLOT:(r + 1) * SLOT, D:KV].rearrange("p e (d h) -> p e d h", h=HEADS)
                        v.tensor_tensor(vals, vals, w[:, b, r * SLOT:(r + 1) * SLOT, None, :].to_broadcast([P, SLOT, ACC // HEADS, HEADS]),
                                        ALU.mult).then_inc(c_weighted, 1)

                    done = [0]

                    def scale(r):
                        def stage(i, b):
                            if r == 0:
                                v.wait_ge(c_summed, times(i, b, 1))
                                if not is_first(i, b):
                                    v.wait_ge(c_batch.sem, c_batch.of(i, b - 1, UB))
                            before = state[b][:, r - 1, 0:ACC] if r else state[(b - 1) % UB][:, R - 1, 0:ACC]
                            chain.link(v.tensor_tensor(heads(tmp[:, :]), heads(before),
                                                       w[:, b, R * SLOT + r, None, :].to_broadcast([P, ACC // HEADS, HEADS]), ALU.mult))
                            ins = v.tensor_tensor(state[b][:, r, 0:ACC], ps_row(b, r), tmp[:, :], ALU.add)
                            if r == R - 1:
                                ins.then_inc(c_batch.sem, 1)
                            else:
                                done[0] = chain.inc(ins)
                        return stage

                    def scaled(r):
                        def stage(i, b):
                            if r == 0:
                                place(b, i * UB + b + UB)
                            if r < R - 1:
                                v.wait_ge(chain.sem, done[0])
                        return stage

                    def weigh_stage(r):
                        def stage(i, b):
                            if r == 0:
                                v.wait_ge(c_e.sem, c_e.of(i, b, UB))
                            weigh(i, b, r)
                        return stage
                    stages = [(0, score)]
                    for r in range(R):
                        stages += [(1, scale(r)), (0, weigh_stage(r)), (1, scaled(r))]
                    staged(v, NBA, UB, stages, chain, 4 + R + R + (R - 1))

                @blk.scalar
                def _(a):
                    def expo(i, b):
                        a.wait_ge(c_w.sem, c_w.base + times(i, b, EXPS))
                        a.activation(w[:, b, :, :], w[:, b, :, :], ACT.Exp).then_inc(c_e.sem, 1)
                    staged(a, NBA, UB, [(0, expo)])

                @blk.tensor
                def _(pe):
                    def add(i, b):
                        if not is_first(i, b):
                            if b == 0:
                                pe.wait_ge(c_batch.sem, c_batch.of(i, b - 1, UB))
                            elif not is_first(i, b, 0, 2):
                                pe.wait_ge(c_batch.sem, c_batch.of(i, b - 2, UB))
                        for r in range(R):
                            pe.wait_ge(c_weighted, times(i, b, R, r + 1))
                            for e in range(SLOT):
                                m = pe.matmul(ps_row(b, r), ident[:, :], kvs[b][:, r * SLOT + e, D:KV], start=(e == 0), stop=(e == SLOT - 1))
                        m.then_inc(c_summed, 1)
                    staged(pe, NBA, UB, [(0, add)])

                @blk.sync
                def _(sp):
                    def store(i, b):
                        sp.wait_ge(c_batch.sem, c_batch.of(i, b, UB))
                        sp.dma_start(ahist_p[:, bass.ds((i * UB + b) * R, R), :], state[b][:, :, :]).then_inc(s_hs[b].sem, 16)
                    staged(sp, NBA, UB, [(0, store)])
                    for b in range(UB):
                        sp.wait_ge(s_hs[b].sem, s_hs[b].base + (NBA // UB) * 16)
            c_eix.close(2 * (NBA + UB))
            c_batch.close(NBA)
            c_w.close(NBA * EXPS)
            c_e.close(NBA)
            for b in range(UB):
                s_eg[b].close(NBA // UB * 16 * GATHERS)
                s_hs[b].close(NBA // UB * 16)

        def carry_attention(state):
            last = state[UB - 1][:, R - 1, :]
            G8 = P // HEADS
            with ExitStack() as st, block() as blk:
                spread = sb(st, "spread", [P, 2, G8, HEADS])
                mc = sb(st, "mc", [P, P + 1])
                ar = sb(st, "ar", [P, 2, P])
                part = sb(st, "part", [P, 3, P])
                sc = sb(st, "sc", [P, 3, P + 1])
                found = sb(st, "found", [P, STATE])
                top_m = sb(st, "top_m", [P, HEADS])
                e2 = sb(st, "e2", [P, 2, HEADS])
                add = sb(st, "add", [P, ACC])
                m0 = s_misc.base

                @blk.tensor
                def _(pe):
                    pe.wait_ge(s_dve.sem, s_dve.base + 1)
                    ins = (last[:, 0:P], last[:, P:2 * P], spread[:, 0, :, :].rearrange("p a b -> p (a b)"),
                           spread[:, 1, :, :].rearrange("p a b -> p (a b)"))
                    for k, a in enumerate(ins):
                        t = pe.transpose(bank[0][:, k * P:(k + 1) * P], a, ident[:, :])
                    t.then_inc(s_pe.sem, 1)
                    pe.wait_ge(s_dve.sem, s_dve.base + 3)
                    for k, a in enumerate((sc[:, 0, 0:P], sc[:, 1, 0:P], sc[:, 2, 0:P], mc[:, 0:P])):
                        t = pe.transpose(bank[1][:, k * P:(k + 1) * P], a, ident[:, :])
                    t.then_inc(s_pe.sem, 1)

                @blk.scalar
                def _(a):
                    a.wait_ge(s_dve.sem, s_dve.base + 2)
                    a.activation(ar[:, :, :], ar[:, :, :], ACT.Exp).then_inc(c_e.sem, 1)
                    a.wait_ge(s_dve.sem, s_dve.base + 4)
                    a.activation(e2[:, :, :], e2[:, :, :], ACT.Exp).then_inc(c_e.sem, 1)

                @blk.vector
                def _(v):
                    chain.inc(v.memset(found[:, :], 0.0))
                    for k in range(2):
                        chain.link(v.tensor_copy(spread[:, k, :, :], last[:, None, D + k * HEADS:ACC + k * HEADS]
                                                 .to_broadcast([P, G8, HEADS])))
                    v.sem_inc(s_dve.sem, 1)
                    chain.inc(v.memset(mc[:, 0:1], NEG))
                    chain.link(v.memset(sc[:, :, 0:1], 0.0))
                    v.wait_ge(s_pe.sem, s_pe.base + 1)
                    chain.link(v.tensor_tensor_scan(mc[:, 1:P + 1], row_Rrow[:, :], bank[0][:, 3 * P:4 * P], NEG, ALU.add, ALU.max))
                    chain.inc(v.tensor_tensor(ar[:, 0, :], bank[0][:, 3 * P:4 * P], mc[:, 1:P + 1], ALU.subtract))
                    chain.link(v.tensor_tensor(ar[:, 1, :], mc[:, 0:P], row_Rrow[:, :], ALU.add))
                    chain.link(v.tensor_tensor(ar[:, 1, :], ar[:, 1, :], mc[:, 1:P + 1], ALU.subtract))
                    v.sem_inc(s_dve.sem, 1)
                    v.wait_ge(c_e.sem, c_e.base + 1)
                    for k in range(3):
                        chain.link(v.tensor_tensor(part[:, k, :], bank[0][:, k * P:(k + 1) * P], ar[:, 0, :], ALU.mult))
                    for k in range(3):
                        chain.link(v.tensor_tensor_scan(sc[:, k, 1:P + 1], ar[:, 1, :], part[:, k, :], 0.0, ALU.mult, ALU.add))
                    v.sem_inc(s_dve.sem, 1)
                    v.wait_ge(s_pe.sem, s_pe.base + 2)
                    v.wait_ge(s_misc.sem, m0 + 16)
                    chain.link(v.tensor_tensor(top_m[:, :], bank[1][:, 3 * P:3 * P + HEADS], found[:, ACC:STATE], ALU.max))
                    chain.inc(v.tensor_tensor(e2[:, 0, :], found[:, ACC:STATE], top_m[:, :], ALU.subtract))
                    chain.link(v.tensor_tensor(e2[:, 1, :], bank[1][:, 3 * P:3 * P + HEADS], top_m[:, :], ALU.subtract))
                    v.sem_inc(s_dve.sem, 1)
                    v.wait_ge(c_e.sem, c_e.base + 2)

                    def by_head(ap):
                        return ap.rearrange("p (d h) -> p d h", h=HEADS)

                    def factor(k):
                        return e2[:, k, None, :].to_broadcast([P, ACC // HEADS, HEADS])
                    chain.inc(v.tensor_tensor(by_head(found[:, 0:ACC]), by_head(found[:, 0:ACC]), factor(0), ALU.mult))
                    chain.link(v.tensor_tensor(by_head(add[:, :]), by_head(bank[1][:, 0:ACC]), factor(1), ALU.mult))
                    chain.link(v.tensor_tensor(found[:, 0:ACC], found[:, 0:ACC], add[:, :], ALU.add))
                    v.sem_inc(s_dve.sem, 1)

                @blk.gpsimd
                def _(g):
                    g.wait_ge(s_dve.sem, s_dve.base + 1)
                    g.indirect_dma_start(found[:, :], None, ahist, bass.IndirectOffsetOnAxis(row_fix_ix[:, 0:1], 0),
                                         bounds_check=NOROW - 1, oob_is_err=False).then_inc(s_misc.sem, 16)
                    g.wait_ge(s_dve.sem, s_dve.base + 5)
                    g.indirect_dma_start(ahist, bass.IndirectOffsetOnAxis(row_fix_ix[:, 0:1], 0), found[:, :], None,
                                         bounds_check=NOROW - 1, oob_is_err=False).then_inc(s_misc.sem, 16)
                    g.wait_ge(s_misc.sem, m0 + 32)
            s_pe.close(2)
            s_dve.close(5)
            c_e.close(2)
            s_misc.close(32)

        def finish(w, bias):
            with ExitStack() as st, block() as blk:
                rz = sb(st, "rz", [P, UN, HEADS])
                h, hT, o, pool = ring(st, "h"), ring(st, "hT"), ring(st, "o"), ring(st, "pool", STATE)
                node_gathers(blk, pool, ahist, STATE, NOROW)

                @blk.vector
                def _(v):
                    def divide(i, u):
                        v.wait_ge(s_gat[u].sem, s_gat[u].base + (i * 16 + 16))
                        at = chain.inc(v.reciprocal(rz[:, u, :], pool[:, u, D:ACC]))
                        yield
                        v.wait_ge(chain.sem, at)
                        v.tensor_tensor(h[:, u, :].rearrange("p (d h) -> p d h", h=HEADS),
                                        pool[:, u, 0:D].rearrange("p (d h) -> p d h", h=HEADS),
                                        rz[:, u, None, :].to_broadcast([P, HD, HEADS]), ALU.mult).then_inc(c_h.sem, 1)

                    def join(i, u):
                        v.wait_ge(c_mm.sem, c_mm.of(i, u))
                        v.wait_ge(s_st[u].sem, s_st[u].base + i * 16)
                        at = chain.inc(v.tensor_tensor(o[:, u, :], ps_small(u), bias[:, :], ALU.add))
                        yield
                        v.wait_ge(chain.sem, at)
                        v.tensor_tensor(o[:, u, :], o[:, u, :], X[:, i * UN + u, :], ALU.add).then_inc(c_out.sem, 1)
                    staged(v, NT, UN, [(0, place_ix(v, node_ix2)), (3, divide), (7, join)], chain, 2)

                @blk.scalar
                def _(a):
                    def evac(i, u):
                        a.wait_ge(c_T.sem, c_T.of(i, u))
                        a.wait_ge(c_mm.sem, c_mm.of(i - 1, u))
                        a.activation(hT[:, u, :], ps_T(u), ACT.Copy).then_inc(c_hT.sem, 1)
                    staged(a, NT, UN, [(5, evac)])

                @blk.tensor
                def _(pe):
                    def turn(i, u):
                        pe.wait_ge(c_h.sem, c_h.of(i, u))
                        pe.wait_ge(c_hT.sem, c_hT.of(i, prior(u, TURNED)))
                        for k in range(KC):
                            t = pe.transpose(ps_T(u)[:, k * P:(k + 1) * P], h[:, u, k * P:(k + 1) * P], ident[:, :])
                        t.then_inc(c_T.sem, 1)

                    def multiply(i, u):
                        pe.wait_ge(c_hT.sem, c_hT.of(i, u))
                        pe.wait_ge(c_out.sem, c_out.of(i, prior(u, PRODUCT)))
                        for k in range(KC):
                            m = pe.matmul(ps_small(u), hT[:, u, k * P:(k + 1) * P], w[:, k, :], start=(k == 0), stop=(k == KC - 1))
                        m.then_inc(c_mm.sem, 1)
                    staged(pe, NT, UN, [(4, turn), (6, multiply)])

                @blk.sync
                def _(sp):
                    def store(i, u):
                        sp.wait_ge(c_out.sem, c_out.of(i, u))
                        sp.dma_start(out[bass.ds((i * UN + u) * P, P), :], o[:, u, :]).then_inc(s_st[u].sem, 16)
                    staged(sp, NT, UN, [(UN, store, NT - 1)])
                    sp.wait_ge(c_out.sem, c_out.of(NT // UN - 1, UN - 1))
                    sp.dma_start(out[(NT - 1) * P:N, :], o[0:TAIL, UN - 1, :]).then_inc(s_st[UN - 1].sem, 16)
                    for u in range(UN):
                        sp.wait_ge(s_st[u].sem, s_st[u].base + NT // UN * 16)

        load_base = [loads * 16]

        def all_loaded():
            with block() as blk:
                @blk.sync
                def _(sp):
                    sp.wait_ge(s_load, load_base[0])

        def chunks(w):
            return w.rearrange("(k p) n -> p k n", p=P)

        with scope() as l0:
            def mat(name):
                return sb(l0, name, [P, KC, D])

            def vec(name):
                return sb(l0, name, [P, D])
            U = sb(l0, "U", [P, NT, D])
            w_m1a, w_m1b, w_m2a, w_m2b, w_m3a, w_m3b = (mat(n) for n in ("w_m1a", "w_m1b", "w_m2a", "w_m2b", "w_m3a", "w_m3b"))
            v_m1, v_g2, v_b2, v_g3, v_b3, v_m2, v_m3 = (vec(n) for n in ("v_m1", "v_g2", "v_b2", "v_g3", "v_b3", "v_m2", "v_m3"))
            with scope() as t:
                w_p1, v_p1 = sb(t, "w_p1", [P, KC, D]), sb(t, "v_p1", [P, D])
                now = [(w_p1[:, :, :], chunks(wp1)), (v_p1[:, :], rows(bp1))]
                later = [(w_m1a[:, :, :], chunks(wm1[0:D, :])), (w_m1b[:, :, :], chunks(wm1[D:2 * D, :])),
                         (w_m2a[:, :, :], chunks(wm2[0:D, :])), (w_m2b[:, :, :], chunks(wm2[D:2 * D, :])),
                         (w_m3a[:, :, :], chunks(wm3[0:D, :])), (w_m3b[:, :, :], chunks(wm3[D:2 * D, :])),
                         (v_m1[:, :], rows(bm1)), (v_m2[:, :], rows(bm2)), (v_m3[:, :], rows(bm3)),
                         (v_g2[:, :], rows(g2)), (v_b2[:, :], rows(b2)), (v_g3[:, :], rows(g3)), (v_b3[:, :], rows(b3))]
                o = ring(t, "o")

                def emit1(v, i, u):
                    at = chain.inc(v.tensor_tensor(o[:, u, :], ps_small(u), v_p1[:, :], ALU.add))
                    yield
                    v.wait_ge(chain.sem, at)
                    v.tensor_scalar(o[:, u, :], o[:, u, :], 0.0, None, ALU.max).then_inc(c_out.sem, 1)

                def store1(sp, i, u):
                    sp.dma_start(tab_t[bass.ds(i * UN + u, 1), :, :].rearrange("a p f -> p (a f)"), o[:, u, :]).then_inc(s_st[u].sem, 16)
                project([(lambda k: w_p1[:, k, :], ps_small)], emit1, 1, store1, 1, now, later)
            all_loaded()

            with scope() as g:
                G = [sb(g, f"G{b}", [P, J, D]) for b in range(UB)]
                end_row, end_col = sb(g, "end_row", [P, NT]), sb(g, "end_col", [P, NT])
                with scope() as c:
                    marks = Marks(c, dst_ix, CH, reset, fix_ix, Rrow)
                    degrees = Degrees(c)
                    max_pass(G, degrees, LayerInput(c, w_m1a, v_m1, True), marks)
                    find_rows(degrees)
                carry_max(G)
                combine(U, w_m1b, None, None, True, RowNodes)
                place = sb(g, "place", [P, CH])
                with scope() as c:
                    max_pass(G, Ranks(c, place), LayerInput(c, w_m2a, v_m2, False))
                carry_max(G)
                combine(U, w_m2b, v_g2, v_b2, True)
                with scope() as c:
                    row_marks = Marks(c, row_node, RP, row_reset, row_fix_ix, row_Rrow)
                    max_pass(G, Permute(c, place), LayerInput(c, w_m3a, v_m3, False, v_b3), row_marks)
                carry_max(G)
                combine(U, w_m3b, v_g3, None, False)
        empty = sb(top, "empty", [P, SL])
        empty_slots(empty)

        with scope() as l1:
            w_q, w_o = sb(l1, "w_q", [P, KC, D]), sb(l1, "w_o", [P, KC, D])
            w_kv = sb(l1, "w_kv", [P, KC, 2 * D])
            v_q, v_o, v_kv = sb(l1, "v_q", [P, D]), sb(l1, "v_o", [P, D]), sb(l1, "v_kv", [P, 2 * D])
            now = [(w_q[:, :, :], chunks(wq)), (w_kv[:, :, 0:D], chunks(wk)), (w_kv[:, :, D:2 * D], chunks(wv)),
                   (v_q[:, :], rows(bq)), (v_kv[:, 0:D], rows(bk)), (v_kv[:, D:2 * D], rows(bv))]
            later = [(w_o[:, :, :], chunks(wo)), (v_o[:, :], rows(bo))]
            with scope() as t:
                okv, o = ring(t, "okv", KV), ring(t, "o")
                SC = float(HD) ** -0.5

                def begin2(v):
                    chain.inc(v.memset(okv[:, :, 2 * D:KV], 1.0))
                    chain.link(v.tensor_scalar(v_q[:, :], v_q[:, :], SC, None, ALU.mult))

                def emit2(v, i, u):
                    at = chain.inc(v.tensor_tensor(okv[:, u, 0:2 * D], ps_wide(u), v_kv[:, :], ALU.add))
                    yield
                    v.wait_ge(chain.sem, at)
                    v.scalar_tensor_tensor(out=o[:, u, :], in0=ps_small(u), scalar=SC, in1=v_q[:, :], op0=ALU.mult, op1=ALU.add).then_inc(c_out.sem, 1)

                def store2(sp, i, u):
                    sp.dma_start(qtab_t[bass.ds(i * UN + u, 1), :, :].rearrange("a p f -> p (a f)"), o[:, u, :]).then_inc(s_st[u].sem, 16)
                    sp.dma_start(kvtab_t[bass.ds(i * UN + u, 1), :, :].rearrange("a p f -> p (a f)"), okv[:, u, :]).then_inc(s_st[u].sem, 16)
                project([(lambda k: w_q[:, k, :], ps_small), (lambda k: w_kv[:, k, :], ps_wide)], emit2, 2, store2, 1, now, later, begin2)
            all_loaded()
            with scope() as a:
                state = [sb(a, f"state{b}", [P, R, STATE]) for b in range(UB)]
                with scope() as q:
                    attention_pass(q, state, empty)
                carry_attention(state)
            finish(w_o, v_o)


_INS = [("x", "x"), ("src", "src"), ("dst", "dst"), ("wp1", "L0_gnn_Wp1"), ("bp1", "L0_gnn_bp1"), ("wm1", "L0_gnn_Wm1"),
        ("bm1", "L0_gnn_bm1"), ("wm2", "L0_gnn_Wm2"), ("bm2", "L0_gnn_bm2"), ("wm3", "L0_gnn_Wm3"), ("bm3", "L0_gnn_bm3"),
        ("g2", "L0_gnn_ln2_g"), ("b2", "L0_gnn_ln2_b"), ("g3", "L0_gnn_ln3_g"), ("b3", "L0_gnn_ln3_b"),
        ("wq", "L1_gnn_Wq"), ("bq", "L1_gnn_bq"), ("wk", "L1_gnn_Wk"), ("bk", "L1_gnn_bk"), ("wv", "L1_gnn_Wv"),
        ("bv", "L1_gnn_bv"), ("wo", "L1_gnn_Wo"), ("bo", "L1_gnn_bo")]
_TRANSPOSED = ("wp1", "wm1", "wm2", "wm3")


def kernel(**inputs):
    import numpy as np
    import concourse.bacc as bacc
    from concourse.bass_utils import run_bass_kernel_spmd

    nc = bacc.Bacc("TRN2", target_bir_lowering=False, num_devices=1)
    arrays, args = {}, {}
    for short, name in _INS:
        a = np.asarray(inputs[name])
        a = np.ascontiguousarray(a.T if short in _TRANSPOSED else a)
        arrays[f"in_{short}"] = a
        args[short] = nc.dram_tensor(f"in_{short}", a.shape, mybir.dt.from_np(a.dtype), kind="ExternalInput").ap()
    n, d = inputs["x"].shape
    out = nc.dram_tensor("out_0", (n, d), F32, kind="ExternalOutput").ap()
    gnn_kernel(nc, out=out, **args)
    r = run_bass_kernel_spmd(nc, [arrays], core_ids=[0])
    return r.results[0]["out_0"]
```
